# Optimizing a Trainium2 kernel written in Bass

```python
import numpy as np
import jax
import jax.numpy as jnp

def _softmax(x, axis=-1):
    return jax.nn.softmax(x, axis=axis)

def _gelu(x):
    return jax.nn.gelu(x, approximate=True)

def _silu(x):
    return jax.nn.silu(x)

def _sigmoid(x):
    return jax.nn.sigmoid(x)

def _layernorm(x, axis=-1, eps=1e-05):
    m = jnp.mean(x, axis=axis, keepdims=True)
    v = jnp.var(x, axis=axis, keepdims=True)
    return (x - m) / jnp.sqrt(v + eps)

def _scatter_add(tgt, idx, src, axis=0):
    return tgt.at[idx].add(src)

def _segment_sum(src, seg, n):
    return jax.ops.segment_sum(src, seg, n)
kernel_name = 'mk_flamingo_gated_d2_seqx_r8_1630c6'

def setup_inputs(seed: int=0):
    np.random.seed(seed)
    _w = jnp.asarray

    def _rec_inputs():
        import jax
        import jax.numpy as jnp
        _rk = jax.random.key(seed)
        x = -0.0003929 + 0.9999 * jax.random.normal(jax.random.fold_in(_rk, 1), (32, 64, 512), jnp.float32)
        _lenS = 64 - jax.random.randint(jax.random.fold_in(_rk, 7), (32,), 0, max(1, 64 // 4) + 1, jnp.int32)
        _lenS2 = 64 - jax.random.randint(jax.random.fold_in(_rk, 8), (32,), 0, max(1, 64 // 4) + 1, jnp.int32)
        _ctx_4096P = jax.random.normal(jax.random.fold_in(_rk, 11), (32, 16, 512), jnp.float32)
        _ctx_4096c = jax.random.dirichlet(jax.random.fold_in(_rk, 511), 0.3 * jnp.ones((16,), jnp.float32), (32, 64))
        _ctx_4096t = jnp.einsum('bsk,bkd->bsd', _ctx_4096c, _ctx_4096P)
        _ctx_4096t = _ctx_4096t * jax.lax.rsqrt(jnp.mean(jnp.square(_ctx_4096t)) + 1e-12) * 0.953939
        ctx_4096 = 2.81802e-05 + 1.00001 * (_ctx_4096t + 0.3 * jax.random.normal(jax.random.fold_in(_rk, 611), (32, 64, 512), jnp.float32))
        _g = jax.random.normal(jax.random.fold_in(_rk, 9001), (2, 2), jnp.float32)
        _g = jnp.sign(_g) * jnp.maximum(jnp.abs(_g), 1.0) + (_g == 0) * 1.0
        g_xattn = _g[0]
        g_ffn = _g[1]
        return (x, ctx_4096, g_xattn, g_ffn)
    x, ctx_4096, g_xattn, g_ffn = _rec_inputs()

    def _L0_xattn_setup():
        import jax, jax.numpy as jnp
        import numpy as np
        EMBED = 512
        NUM_Q = 32
        NUM_KV = 8
        GROUPS = NUM_Q // NUM_KV
        HEAD_DIM = EMBED // NUM_Q
        KV_DIM = HEAD_DIM * NUM_KV
        key = jax.random.key(seed)
        ks = jax.random.split(key, 12)
        B, S = (2, 256)
        s = 0.02
        return {'query': jax.random.normal(ks[0], (B, S, EMBED), jnp.float32), 'key': jax.random.normal(ks[1], (B, S, EMBED), jnp.float32), 'value': jax.random.normal(ks[2], (B, S, EMBED), jnp.float32), 'Wq': jax.random.normal(ks[3], (EMBED, EMBED), jnp.float32) * s, 'bq': jnp.zeros((EMBED,), jnp.float32), 'Wk': jax.random.normal(ks[4], (EMBED, KV_DIM), jnp.float32) * s, 'bk': jnp.zeros((KV_DIM,), jnp.float32), 'Wv': jax.random.normal(ks[5], (EMBED, KV_DIM), jnp.float32) * s, 'bv': jnp.zeros((KV_DIM,), jnp.float32), 'Wo': jax.random.normal(ks[6], (EMBED, EMBED), jnp.float32) * s, 'bo': jnp.zeros((EMBED,), jnp.float32)}
    _L0_xattn_all = _L0_xattn_setup()
    _L0_xattn_in = {k: v for k, v in _L0_xattn_all.items() if k in ('Wq', 'bq', 'Wk', 'bk', 'Wv', 'bv', 'Wo', 'bo')}
    del _L0_xattn_all

    def _L0_ffn_setup():
        import jax, jax.numpy as jnp
        import numpy as np
        H = 512
        I = 256
        E = 16
        TOPK = 4
        SI = 256
        key = jax.random.key(seed)
        ks = jax.random.split(key, 9)
        s = 0.02
        return {'hidden_states': jax.random.normal(ks[0], (2, 256, H), dtype=jnp.float32), 'gate_w': jax.random.normal(ks[1], (E, H), dtype=jnp.float32) * s, 'bias': jnp.zeros((E,), dtype=jnp.float32), 'Wg': jax.random.normal(ks[2], (E, I, H), dtype=jnp.float32) * s, 'Wu': jax.random.normal(ks[3], (E, I, H), dtype=jnp.float32) * s, 'Wd': jax.random.normal(ks[4], (E, H, I), dtype=jnp.float32) * s, 'Sg': jax.random.normal(ks[5], (SI, H), dtype=jnp.float32) * s, 'Su': jax.random.normal(ks[6], (SI, H), dtype=jnp.float32) * s, 'Sd': jax.random.normal(ks[7], (H, SI), dtype=jnp.float32) * s}
    _L0_ffn_all = _L0_ffn_setup()
    _L0_ffn_in = {k: v for k, v in _L0_ffn_all.items() if k in ('gate_w', 'bias', 'Wg', 'Wu', 'Wd', 'Sg', 'Su', 'Sd')}
    del _L0_ffn_all

    def _L1_xattn_setup():
        import jax, jax.numpy as jnp
        import numpy as np
        import math
        EPS = 1e-05
        LAMBDA = 0.6

        def _crucial_k(C):
            f = math.floor(LAMBDA * C)
            return f + f % 2

        def _conv1d(y, w):
            return jax.lax.conv_general_dilated(y, w, window_strides=(1,), padding=((3, 3),), dimension_numbers=('NCH', 'OIH', 'NCH'))

        def _norm_active(z, gamma, beta):
            mu = jnp.mean(z, axis=(0, 2), keepdims=True)
            var = jnp.mean((z - mu) ** 2, axis=(0, 2), keepdims=True)
            zn = (z - mu) * jax.lax.rsqrt(var + EPS)
            zn = zn * gamma.reshape(1, -1, 1) + beta.reshape(1, -1, 1)
            return jax.nn.sigmoid(jax.nn.relu(zn))
        key = jax.random.key(seed)
        k1, k2, k3 = jax.random.split(key, 3)
        B, C, L = (32, 32, 512)
        x = jax.random.normal(k1, (B, C, L), dtype=jnp.float32)
        channel_map = jax.random.normal(k2, (B, C, L), dtype=jnp.float32)
        fan_in = 2 * 7
        bound = 1.0 / math.sqrt(fan_in)
        conv_w = jax.random.uniform(k3, (1, 2, 7), jnp.float32, -bound, bound)
        bn_gamma = jnp.ones((1,), jnp.float32)
        bn_beta = jnp.zeros((1,), jnp.float32)
        return {'x': x, 'channel_map': channel_map, 'conv_w': conv_w, 'bn_gamma': bn_gamma, 'bn_beta': bn_beta}
    _L1_xattn_all = _L1_xattn_setup()
    _L1_xattn_in = {k: v for k, v in _L1_xattn_all.items() if k in ('conv_w', 'bn_gamma', 'bn_beta')}
    del _L1_xattn_all

    def _L1_ffn_setup():
        import jax, jax.numpy as jnp
        import numpy as np
        E = 8
        R = 16
        TOP_K = 2
        SCALING = 32.0 / 16.0
        D_IN = 512
        D_OUT = 512
        key = jax.random.key(seed)
        ks = jax.random.split(key, 6)
        x = jax.random.normal(ks[0], (4, 256, D_IN), jnp.float32)
        Wb = jax.random.normal(ks[1], (D_OUT, D_IN), jnp.float32) * 0.02
        bias = jax.random.normal(ks[2], (D_OUT,), jnp.float32) * 0.02
        Wr = jax.random.normal(ks[3], (E, D_IN), jnp.float32) * 0.01
        A = jax.random.normal(ks[4], (E, R, D_IN), jnp.float32) * (1.0 / np.sqrt(D_IN))
        Bm = jax.random.normal(ks[5], (E, D_OUT, R), jnp.float32) * 0.01
        return {'x': x, 'Wb': Wb, 'bias': bias, 'Wr': Wr, 'A': A, 'Bm': Bm}
    _L1_ffn_all = _L1_ffn_setup()
    _L1_ffn_in = {k: v for k, v in _L1_ffn_all.items() if k in ('Wb', 'bias', 'Wr', 'A', 'Bm')}
    del _L1_ffn_all
    return {'x': x, 'ctx_4096': ctx_4096, 'g_xattn': g_xattn, 'g_ffn': g_ffn, 'L0_xattn_Wq': _L0_xattn_in['Wq'], 'L0_xattn_bq': _L0_xattn_in['bq'], 'L0_xattn_Wk': _L0_xattn_in['Wk'], 'L0_xattn_bk': _L0_xattn_in['bk'], 'L0_xattn_Wv': _L0_xattn_in['Wv'], 'L0_xattn_bv': _L0_xattn_in['bv'], 'L0_xattn_Wo': _L0_xattn_in['Wo'], 'L0_xattn_bo': _L0_xattn_in['bo'], 'L0_ffn_gate_w': _L0_ffn_in['gate_w'], 'L0_ffn_bias': _L0_ffn_in['bias'], 'L0_ffn_Wg': _L0_ffn_in['Wg'], 'L0_ffn_Wu': _L0_ffn_in['Wu'], 'L0_ffn_Wd': _L0_ffn_in['Wd'], 'L0_ffn_Sg': _L0_ffn_in['Sg'], 'L0_ffn_Su': _L0_ffn_in['Su'], 'L0_ffn_Sd': _L0_ffn_in['Sd'], 'L1_xattn_conv_w': _L1_xattn_in['conv_w'], 'L1_xattn_bn_gamma': _L1_xattn_in['bn_gamma'], 'L1_xattn_bn_beta': _L1_xattn_in['bn_beta'], 'L1_ffn_Wb': _L1_ffn_in['Wb'], 'L1_ffn_bias': _L1_ffn_in['bias'], 'L1_ffn_Wr': _L1_ffn_in['Wr'], 'L1_ffn_A': _L1_ffn_in['A'], 'L1_ffn_Bm': _L1_ffn_in['Bm']}

def reference(x, ctx_4096, g_xattn, g_ffn, L0_xattn_Wq, L0_xattn_bq, L0_xattn_Wk, L0_xattn_bk, L0_xattn_Wv, L0_xattn_bv, L0_xattn_Wo, L0_xattn_bo, L0_ffn_gate_w, L0_ffn_bias, L0_ffn_Wg, L0_ffn_Wu, L0_ffn_Wd, L0_ffn_Sg, L0_ffn_Su, L0_ffn_Sd, L1_xattn_conv_w, L1_xattn_bn_gamma, L1_xattn_bn_beta, L1_ffn_Wb, L1_ffn_bias, L1_ffn_Wr, L1_ffn_A, L1_ffn_Bm):
    import jax
    import jax.numpy as jnp

    def _L0_xattn_ref(query, key, value, Wq, bq, Wk, bk, Wv, bv, Wo, bo):
        import jax, jax.numpy as jnp
        import numpy as np
        EMBED = 512
        NUM_Q = 32
        NUM_KV = 8
        GROUPS = NUM_Q // NUM_KV
        HEAD_DIM = EMBED // NUM_Q
        KV_DIM = HEAD_DIM * NUM_KV
        B, S, _ = query.shape
        Q = query @ Wq + bq
        K = key @ Wk + bk
        V = value @ Wv + bv
        Q = Q.reshape(B, S, NUM_KV, GROUPS, HEAD_DIM).transpose(0, 2, 3, 1, 4)
        K = K.reshape(B, S, NUM_KV, HEAD_DIM).transpose(0, 2, 1, 3)
        V = V.reshape(B, S, NUM_KV, HEAD_DIM).transpose(0, 2, 1, 3)
        scale = 1.0 / jnp.sqrt(jnp.asarray(HEAD_DIM, query.dtype))
        scores = jnp.einsum('bhgqd,bhkd->bhgqk', Q, K) * scale
        w = jax.nn.softmax(scores, axis=-1)
        y = jnp.einsum('bhgqk,bhkd->bhgqd', w, V)
        y = y.transpose(0, 3, 1, 2, 4).reshape(B, S, EMBED)
        return y @ Wo + bo

    def _L0_ffn_ref(hidden_states, gate_w, bias, Wg, Wu, Wd, Sg, Su, Sd):
        import jax, jax.numpy as jnp
        import numpy as np
        H = 512
        I = 256
        E = 16
        TOPK = 4
        SI = 256
        orig_shape = hidden_states.shape
        x = hidden_states.reshape(-1, orig_shape[-1])
        scores = jax.nn.sigmoid(x @ gate_w.T) + bias
        topk_w, topk_idx = jax.lax.top_k(scores, TOPK)
        topk_w = topk_w / (jnp.sum(topk_w, axis=-1, keepdims=True) + 1e-20)
        cw = jnp.sum(jax.nn.one_hot(topk_idx, E, dtype=x.dtype) * topk_w[..., None], axis=1)
        g = jnp.einsum('th,eih->eti', x, Wg)
        u = jnp.einsum('th,eih->eti', x, Wu)
        z = jax.nn.silu(g) * u
        zw = z * cw.T[:, :, None]
        out = jnp.einsum('eti,ehi->th', zw, Wd)
        out = out + jax.nn.silu(x @ Sg.T) * (x @ Su.T) @ Sd.T
        return out.reshape(orig_shape)

    def _L1_xattn_ref(x, channel_map, conv_w, bn_gamma, bn_beta):
        import jax, jax.numpy as jnp
        import numpy as np
        import math
        EPS = 1e-05
        LAMBDA = 0.6

        def _crucial_k(C):
            f = math.floor(LAMBDA * C)
            return f + f % 2

        def _conv1d(y, w):
            return jax.lax.conv_general_dilated(y, w, window_strides=(1,), padding=((3, 3),), dimension_numbers=('NCH', 'OIH', 'NCH'))

        def _norm_active(z, gamma, beta):
            mu = jnp.mean(z, axis=(0, 2), keepdims=True)
            var = jnp.mean((z - mu) ** 2, axis=(0, 2), keepdims=True)
            zn = (z - mu) * jax.lax.rsqrt(var + EPS)
            zn = zn * gamma.reshape(1, -1, 1) + beta.reshape(1, -1, 1)
            return jax.nn.sigmoid(jax.nn.relu(zn))
        B, C, L = x.shape
        k = _crucial_k(C)
        cm = jnp.moveaxis(channel_map, 1, 2)
        _, topk_idx = jax.lax.top_k(cm, k)
        b_idx = jnp.arange(B)[:, None, None]
        l_idx = jnp.arange(L)[None, :, None]
        mask = jnp.zeros((B, L, C), x.dtype).at[b_idx, l_idx, topk_idx].set(1.0)
        crucial_channels = jnp.moveaxis(mask, 2, 1)
        subcrucial_channels = 1.0 - crucial_channels
        crucial_features = crucial_channels * x
        subcrucial_features = subcrucial_channels * x
        c_max = jnp.max(crucial_features, axis=1, keepdims=True)
        c_avg = jnp.mean(crucial_features, axis=1, keepdims=True) * (C / k)
        s_max = jnp.max(subcrucial_features, axis=1, keepdims=True)
        s_avg = jnp.mean(subcrucial_features, axis=1, keepdims=True) * (C / (C - k))
        crucial_x = jnp.concatenate([c_max, c_avg], axis=1)
        subcrucial_x = jnp.concatenate([s_max, s_avg], axis=1)
        A_S1 = _norm_active(_conv1d(crucial_x, conv_w), bn_gamma, bn_beta)
        A_S2 = _norm_active(_conv1d(subcrucial_x, conv_w), bn_gamma, bn_beta)
        return crucial_features * A_S1 + subcrucial_features * A_S2

    def _L1_ffn_ref(x, Wb, bias, Wr, A, Bm):
        import jax, jax.numpy as jnp
        import numpy as np
        E = 8
        R = 16
        TOP_K = 2
        SCALING = 32.0 / 16.0
        D_IN = 512
        D_OUT = 512
        xf = x.reshape(-1, x.shape[-1])
        T = xf.shape[0]
        logits = xf @ Wr.T
        probs = jax.nn.softmax(logits, axis=-1)
        topk_p, topk_i = jax.lax.top_k(probs, TOP_K)
        topk_p = topk_p / jnp.sum(topk_p, axis=-1, keepdims=True)
        w = jnp.zeros((T, E), xf.dtype).at[jnp.arange(T)[:, None], topk_i].add(topk_p)
        h = jnp.einsum('ti,eri->ter', xf, A)
        lora = jnp.einsum('ter,te,eor->to', h, w, Bm) * SCALING
        base = xf @ Wb.T + bias
        out = (base + lora).reshape(*x.shape[:-1], D_OUT)
        return out
    x = x + jnp.tanh(g_xattn[0]) * _L0_xattn_ref(_layernorm(x, axis=-1), ctx_4096, ctx_4096, L0_xattn_Wq, L0_xattn_bq, L0_xattn_Wk, L0_xattn_bk, L0_xattn_Wv, L0_xattn_bv, L0_xattn_Wo, L0_xattn_bo)
    x = x + jnp.tanh(g_ffn[0]) * _L0_ffn_ref(_layernorm(x, axis=-1), L0_ffn_gate_w, L0_ffn_bias, L0_ffn_Wg, L0_ffn_Wu, L0_ffn_Wd, L0_ffn_Sg, L0_ffn_Su, L0_ffn_Sd)
    x = x + jnp.tanh(g_xattn[1]) * _L1_xattn_ref(_layernorm(x, axis=-1), ctx_4096, L1_xattn_conv_w, L1_xattn_bn_gamma, L1_xattn_bn_beta)
    x = x + jnp.tanh(g_ffn[1]) * _L1_ffn_ref(_layernorm(x, axis=-1), L1_ffn_Wb, L1_ffn_bias, L1_ffn_Wr, L1_ffn_A, L1_ffn_Bm)
    return x

_drawn_inputs = setup_inputs


def setup_inputs(seed=0):
    import zlib

    import numpy as np

    out = dict(_drawn_inputs(seed))
    spreads = {'g_ffn': (-1.0, 0.2),
     'L0_xattn_bq': (0.0, 0.8),
     'L0_xattn_bk': (0.0, 2.0),
     'L0_xattn_bv': (0.0, 0.1),
     'L0_xattn_bo': (0.0, 0.1),
     'L0_ffn_bias': (0.0, 0.509)}
    factors = {'L0_xattn_Wq': 6.669,
     'L0_xattn_Wk': 6.388,
     'L0_ffn_gate_w': 4.542,
     'L0_ffn_Wg': 3.6,
     'L0_ffn_Wu': 3.433,
     'L0_ffn_Wd': 3.506,
     'L1_ffn_bias': 2.778}
    for name, (base, spread) in spreads.items():
        noise = np.random.default_rng([zlib.crc32(name.encode()), seed]).standard_normal(out[name].shape)
        drawn = base * np.exp(spread * noise) if base else spread * noise
        out[name] = jnp.asarray(drawn.astype(out[name].dtype))
    for name, factor in factors.items():
        out[name] = (out[name] * factor).astype(out[name].dtype)
    return out
```

```python
from contextlib import ExitStack

import concourse.bass as bass
from concourse import mybir

F32 = mybir.dt.float32
F32R = mybir.dt.float32r
I32 = mybir.dt.int32
ALU = mybir.AluOpType
ACT = mybir.ActivationFunctionType
AX = mybir.AxisListType.X

P = 128
B, S, D = 32, 64, 512
T = B * S
NT = T // P
KD = D // P
NKV, NG, HD = 8, 4, 16
E, I, TOPK = 16, 256, 4
WGU = KD * 2 * I
WALL = WGU + (I // P) * D
NU = T * TOPK // P + E
NSEL = 38
NSUB = S - NSEL
NF = 11
KONST1, KONST2 = 12, 21
LE, LR = 8, 16
EPS = 1e-5
BIG = 3.0e38

C_GATE, C_RB, C_CONV, C_BN, C_BQ, C_BK, C_BV = 0, 4, 20, 34, 36, 40, 41
C_ALL = 42


def holds(n, least):
    return n >= least if isinstance(n, int) else True


def below(n, limit):
    return n < limit if isinstance(n, int) else True


def block_program(nc, io):
    (x_in, ctxT_in, cst_in, wq_in, wkv_in, wo_in, bo_in, gate_in, wall_in,
     wb_in, aw_in, bm_in, b1_in, out) = io
    with ExitStack() as ctx:
        def sb(name, shape, dt=F32, stack=ctx):
            return stack.enter_context(nc.sbuf_tensor(name, shape, dt))

        def sem(name):
            return ctx.enter_context(nc.semaphore(name))

        bank = [ctx.enter_context(nc.psum_tensor(f"bank{i}", [P, 512], F32)) for i in range(8)]

        X = sb("X", [P, NT, D])
        ctxT = sb("ctxT", [P, KD, T])
        cst = sb("cst", [P, C_ALL])
        tg = sb("tg", [P, 4])
        eps = sb("eps", [P, 1])
        ident = sb("ident", [P, P])
        stats = sb("stats", [P, NT, 6])
        mu = sb("mu", [P, NT])
        va = sb("va", [P, NT])
        dm = sb("dm", [P, NT])
        sd = sb("sd", [P, NT])
        rs = sb("rs", [P, NT])
        xn = [sb(f"xn{j}", [P, D]) for j in range(2)]

        wk = sb("wk", [P, NT, TOPK])
        sidx = sb("sidx", [P, NT, TOPK], I32)
        gidx = [sb(f"gidx{j}", [P, TOPK], I32) for j in range(2)]

        with ExitStack() as s1:
            QT = sb("QT", [P, NG, T], F32, s1)
            KT = sb("KT", [P, T], F32, s1)
            VT = sb("VT", [P, T], F32, s1)
            xnT = sb("xnT", [P, KD, 512], F32, s1)
            wq = sb("wq", [P, KD, NG, P], F32, s1)
            wkv = sb("wkv", [P, KD, 2, P], F32, s1)
            wo = sb("wo", [P, NG, D], F32, s1)
            bo = sb("bo", [P, D], F32, s1)
            hmask = sb("hmask", [P, NKV], F32, s1)
            qTb = [sb(f"qTb{j}", [P, NG, S], F32, s1) for j in range(2)]
            kblk = [sb(f"kblk{j}", [P, NKV, S], F32, s1) for j in range(2)]
            vTb = [sb(f"vTb{j}", [P, 2, S], F32, s1) for j in range(2)]
            vblk = [sb(f"vblk{j}", [P, 4, 34], F32, s1) for j in range(2)]
            mx = [sb(f"mx{j}", [P, NKV], F32, s1) for j in range(2)]
            dif = [sb(f"dif{j}", [P, NKV, S], F32, s1) for j in range(2)]
            prob = [sb(f"prob{j}", [P, NKV * S], F32, s1) for j in range(2)]
            probT = [sb(f"probT{j}", [P, 4, P], F32, s1) for j in range(2)]
            rec = [sb(f"rec{j}", [P, 4, 2], F32, s1) for j in range(2)]
            yn = [sb(f"yn{j}", [P, 4, 2, HD], F32, s1) for j in range(2)]
            yT = sb("yT", [P, NG, P], F32, s1)

        with ExitStack() as s2:
            wh = sb("wh", [P, 3, WALL], F32R, s2)
            wl = sb("wl", [P, 3, WALL], F32R, s2)
            wraw = sb("wraw", [P, WALL], F32, s2)
            gw = sb("gw", [P, KD, E], F32, s2)
            gwh = sb("gwh", [P, KD, E], F32R, s2)
            gwl = sb("gwl", [P, KD, E], F32R, s2)
            xh = [sb(f"xh{j}", [P, KD, P], F32R, s2) for j in range(2)]
            xl = [sb(f"xl{j}", [P, KD, P], F32R, s2) for j in range(2)]
            sg = [sb(f"sg{j}", [P, I], F32, s2) for j in range(2)]
            zz = [sb(f"zz{j}", [P, I], F32, s2) for j in range(2)]
            zh = [sb(f"zh{j}", [P, 2, P], F32R, s2) for j in range(2)]
            zl = [sb(f"zl{j}", [P, 2, P], F32R, s2) for j in range(2)]
            yo = [sb(f"yo{j}", [P, D], F32, s2) for j in range(2)]
            neg = [sb("neg", [P, 8, S], F32, s2)]
            best = sb("best", [P, 8, 8], F32, s2)
            lg = sb("lg", [P, NT, E], F32, s2)
            sc = sb("sc", [P, NT, 24], F32, s2)
            scr = sb("scr", [P, NT, 24], F32, s2)
            v8 = sb("v8", [P, NT, 8], F32, s2)
            wsum = sb("wsum", [P, NT], F32, s2)
            wrec = sb("wrec", [P, NT], F32, s2)
            sel = sb("sel", [P, NT, E], F32, s2)
            pre = sb("pre", [P, NT + 1, E], F32, s2)
            slot = sb("slot", [P, NT, E], F32, s2)
            eq = sb("eq", [P, NT, E], F32, s2)
            k8 = sb("k8", [P, NT, 8], F32, s2)
            tix = sb("tix", [P, NT, TOPK], I32, s2)
            tiy = sb("tiy", [P, NT, TOPK], I32, s2)
            tok = sb("tok", [P, NT], I32, s2)
            ids = sb("ids", [P, NU], I32, s2)
            ucnt = sb("ucnt", [P, E], I32, s2)
            ushf = sb("ushf", [P, E], I32, s2)
            unum = sb("unum", [P, E], F32, s2)
            uend = sb("uend", [P, E], F32, s2)
            ubase = sb("ubase", [P, E], F32, s2)
            ones16 = sb("ones16", [P, E], F32, s2)
            uiota = sb("uiota", [1, NU], F32, s2)
            ule = sb("ule", [1, NU, E], F32, s2)
            ueid = sb("ueid", [1, NU + 1], F32, s2)
            upar = sb("upar", [1, NU], I32, s2)
            uexp = sb("uexp", [1, NU + 1], I32, s2)
            ufirst = sb("ufirst", [1, NU], I32, s2)
            lower = sb("lower", [P, P], F32, s2)
            onesm = sb("onesm", [P, P], F32, s2)

        with ExitStack() as s3:
            cg = [sb(f"cg{j}", [P, TOPK, D], F32, s3) for j in range(2)]
            x3T = sb("x3T", [P, KD, T], F32, s3)
            cf = [sb(f"cf{j}", [P, KD, P], F32, s3) for j in range(2)]
            sf = [sb(f"sf{j}", [P, KD, P], F32, s3) for j in range(2)]
            maps = sb("maps", [P, 2, KD, 2, B], F32, s3)
            wide = sb("wide", [P, 390], F32, s3)
            band = sb("band", [P, 2, 384], F32, s3)
            ones3 = sb("ones3", [P, P], F32, s3)
            zc = sb("zc", [P, 2, KD, B], F32, s3)
            zq = sb("zq", [P, 2, KD, B], F32, s3)
            part = sb("part", [P, 2], F32, s3)
            mean = sb("mean", [P, 2], F32, s3)
            var = sb("var", [P, 2], F32, s3)
            gain = sb("gain", [P, 2], F32, s3)
            amap = sb("amap", [P, 2, KD, B], F32, s3)
            asel = [sb(f"asel{j}", [P, KD, P], F32, s3) for j in range(2)]
            wb = sb("wb", [P, KD, D], F32, s3)
            aw = sb("aw", [P, KD, 136], F32, s3)
            bm = sb("bm", [P, D], F32, s3)
            b1 = sb("b1", [P, D], F32, s3)
            wbs = [sb(f"wbs{i}", [P, KD, D], F32R, s3) for i in range(2)]
            aws = [sb(f"aws{i}", [P, KD, 136], F32R, s3) for i in range(2)]
            bms = [sb(f"bms{i}", [P, D], F32R, s3) for i in range(2)]
            fh = [sb(f"fh{j}", [P, KD, P], F32R, s3) for j in range(2)]
            fl = [sb(f"fl{j}", [P, KD, P], F32R, s3) for j in range(2)]
            pr = [sb(f"pr{j}", [P, 16], F32, s3) for j in range(2)]
            prr = [sb(f"prr{j}", [P, 16], F32, s3) for j in range(2)]
            m8 = [sb(f"m8{j}", [P, 8], F32, s3) for j in range(2)]
            nm = [sb(f"nm{j}", [P, 8], F32, s3) for j in range(2)]
            lw = [sb(f"lw{j}", [P, LE], F32, s3) for j in range(2)]
            hw = [sb(f"hw{j}", [P, P], F32, s3) for j in range(2)]
            hth = [sb(f"hth{j}", [P, P], F32R, s3) for j in range(2)]
            htl = [sb(f"htl{j}", [P, P], F32R, s3) for j in range(2)]
            fo = [sb(f"fo{j}", [P, D], F32, s3) for j in range(2)]

        xn_d = nc.dram_tensor("xn_d", (T, D), F32, kind="Internal").ap()
        tab_d = nc.dram_tensor("tab_d", (NU * P, 1), I32, kind="Internal").ap()
        y_d = nc.dram_tensor("y_d", (NU * P, D), F32, kind="Internal").ap()

        names = """cst_in x_in ctx_in watt_in gw_in wraw_in w4_in konst gates
            lnstat lnvar lnsd lnrs
            xn_ready tx_done xnT_ready proj_done proj_out
            b_ready s_ready mx_ready dif_ready exp_done pt_done ptc_done pv_done rec_ready yn_ready
            yt_done ytc_done wo_done x1_done v_done vhalf v_ready
            w_split w_hi n2 store_in0 store_in1 a_tx a_hi a_lo a_rt a_rtc a_gu a_sg a_z a_zt a_zh a_zl a_y a_x
            rsig rstep rmm tables scat scat_in tab0 ids_in
            g_in0 g_in1 gid u_tx u_hi u_lo u_gu u_sg u_z u_zt u_zh u_zl u_y u_yo y_out0 y_out1
            neg_done tstep
            c_in0 c_in1 cid c_add cpre
            l3 t_done x3_done d3 c3 m3 conv_done carried sel_ready utab sum_step bn_step bn_mm bn_act as3 y3 y3t x3_sum
            konst3 w4_split l4 f_tx f_hi f_lo f_h f_base f_step f_exp f_hw f_ht f_hth f_htl f_out f_fin out_d0 out_d1 x4b""".split()
        sm = {n: sem(n) for n in names}

        block = ctx.enter_context(nc.Block())

        def carry(eng):
            eng.sem_inc(sm["carried"], 1)

        def split3(eng, dst, a, b, k_list, first, last):
            n, m = 0, 3 * len(k_list)
            for k in k_list:
                for ia, ib in ((0, 0), (0, 1), (1, 0)):
                    ins = eng.matmul(dst, a[ia](k), b[ib](k), start=(first and n == 0), stop=(last and n == m - 1),
                                     skip_group_check=True)
                    n += 1
            return ins

        @block.sync
        def _(sp):
            sp.dma_start(cst[:], cst_in).then_inc(sm["cst_in"], 16)
            x_v = x_in.rearrange("(t p) d -> p t d", p=P)
            c_v = ctxT_in.rearrange("(k p) n -> p k n", p=P)
            sp.dma_start(X[:, 0:4, :], x_v[:, 0:4, :]).then_inc(sm["x_in"], 16)
            sp.dma_start(wq[:].rearrange("p k g m -> p k (g m)"), wq_in.rearrange("(k p) n -> p k n", p=P)).then_inc(sm["watt_in"], 16)
            sp.dma_start(wkv[:].rearrange("p k g m -> p k (g m)"), wkv_in.rearrange("(k p) n -> p k n", p=P)).then_inc(sm["watt_in"], 16)
            sp.dma_start(ctxT[:, :, 0:512], c_v[:, :, 0:512]).then_inc(sm["ctx_in"], 16)
            for q in range(1, 4):
                sp.wait_ge(sm["x_in"], 16 * q)
                sp.dma_start(X[:, 4 * q:4 * q + 4, :], x_v[:, 4 * q:4 * q + 4, :]).then_inc(sm["x_in"], 16)
                sp.wait_ge(sm["ctx_in"], 16 * q)
                sp.dma_start(ctxT[:, :, 512 * q:512 * q + 512], c_v[:, :, 512 * q:512 * q + 512]).then_inc(sm["ctx_in"], 16)
            sp.wait_ge(sm["watt_in"], 32)
            sp.dma_start(wo[:], wo_in.rearrange("g p n -> p g n")).then_inc(sm["watt_in"], 16)
            sp.dma_start(bo[:], bo_in).then_inc(sm["watt_in"], 16)
            sp.wait_ge(sm["x1_done"], NT)
            sp.dma_start(gw[:], gate_in.rearrange("(k p) n -> p k n", p=P)).then_inc(sm["gw_in"], 16)

            def store(n, j):
                sp.wait_ge(sm["n2"], n + 1)
                sp.dma_start(xn_d[bass.ds(n * P, P), :], xn[j][:]).then_inc(sm[f"store_in{j}"], 16)

            with sp.Fori(0, NT // 2) as h:
                for j in range(2):
                    store(2 * h + j, j)

            def store_y(n, j):
                sp.wait_ge(sm["u_yo"], n + 1)
                sp.dma_start(y_d[bass.ds(n * P, P), :], yo[j][:]).then_inc(sm[f"y_out{j}"], 16)

            with sp.Fori(0, NU // 2) as h:
                for j in range(2):
                    store_y(2 * h + j, j)
            sp.wait_ge(sm["c_add"], NT * TOPK)
            sp.dma_start(wb[:], wb_in.rearrange("(k p) n -> p k n", p=P)).then_inc(sm["w4_in"], 16)
            sp.dma_start(aw[:], aw_in.rearrange("(k p) n -> p k n", p=P)).then_inc(sm["w4_in"], 16)
            sp.dma_start(bm[:], bm_in).then_inc(sm["w4_in"], 16)
            sp.dma_start(b1[:], b1_in).then_inc(sm["w4_in"], 16)

            def store_out(n, j):
                sp.wait_ge(sm["f_out"], n + 1)
                sp.dma_start(out[bass.ds(n * P, P), :], fo[j][:]).then_inc(sm[f"out_d{j}"], 16)

            with sp.Fori(0, NT // 2) as h:
                for j in range(2):
                    store_out(2 * h + j, j)
            for j in range(2):
                sp.wait_ge(sm[f"out_d{j}"], 16 * (NT // 2))

        @block.gpsimd
        def _(pool):
            kc = [0]

            def k0(ins):
                kc[0] += 1
                ins.then_inc(sm["konst"], 1)
                pool.wait_ge(sm["konst"], kc[0])

            k0(pool.memset(ident[:], 0.0))
            k0(pool.memset(eps[:], EPS))
            k0(pool.memset(hmask[:], 1.0))
            for j in range(2):
                k0(pool.memset(vblk[j][:], 0.0))
            k0(pool.affine_select(ident[:], ident[:], [[-1, P]], ALU.not_equal, 1.0, base=0, channel_multiplier=1))
            k0(pool.affine_select(hmask[:], hmask[:], [[-HD, NKV]], ALU.is_ge, 0.0, base=0, channel_multiplier=1))
            for j in range(2):
                k0(pool.memset(vblk[j][0:S, :, 32:33], 1.0))
                k0(pool.memset(vblk[j][S:P, :, 33:34], 1.0))
            k0(pool.affine_select(hmask[:], hmask[:], [[HD, NKV]], ALU.is_ge, 0.0, base=HD - 1, channel_multiplier=-1))
            pool.wait_ge(sm["gates"], 1)
            pool.wait_ge(sm["watt_in"], 64)
            k0(pool.tensor_scalar(bo[:], bo[:], tg[:, 0:1], None, ALU.mult))
            pool.wait_ge(sm["proj_out"], 24)

            def prepare(b, j):
                if holds(b, 2):
                    pool.wait_ge(sm["s_ready"], 2 * b - 2)
                    pool.wait_ge(sm["v_done"], b - 1)
                pool.tensor_copy(qTb[j][:], QT[:, :, bass.ds(b * S, S)]).then_inc(sm["b_ready"], 1)
                kv = KT[:, bass.ds(b * S, S)].unsqueeze(1).broadcast_to([P, NKV, S])
                pool.tensor_tensor(kblk[j][:], kv, hmask[:].unsqueeze(2).broadcast_to([P, NKV, S]),
                                   ALU.mult).then_inc(sm["b_ready"], 1)
                pool.tensor_copy(vTb[j][:], VT[:, bass.ds(b * S, S)].unsqueeze(1).broadcast_to([P, 2, S]))\
                    .then_inc(sm["b_ready"], 1)

            def add_bias(t):
                pool.tensor_tensor(X[:, bass.ds(t, 1), :], X[:, bass.ds(t, 1), :], bo[:].unsqueeze(1), ALU.add)\
                    .then_inc(sm["x4b"], 1)

            for b in range(2):
                prepare(b, b)
            add_bias(0)
            with pool.Fori(1, B // 2) as h:
                for j in range(2):
                    prepare(2 * h + j, j)
                add_bias(h)

            pool.wait_ge(sm["x1_done"], NT)

            def split(e, at, count):
                pool.wait_ge(sm["wraw_in"], 16 * count)
                pool.tensor_copy(wh[:, at, :], wraw[:]).then_inc(sm["w_hi"], 1)
                pool.wait_ge(sm["w_hi"], count)
                pool.tensor_tensor(wl[:, at, :], wraw[:], wh[:, at, :].bitcast(F32), ALU.subtract)\
                    .then_inc(sm["w_split"], 1)
                pool.wait_ge(sm["w_split"], count)

            pool.dma_start(wraw[:], wall_in[E]).then_inc(sm["wraw_in"], 16)
            split(E, 2, 1)
            pool.dma_start(wraw[:], wall_in[0]).then_inc(sm["wraw_in"], 16)
            k0(pool.memset(ids[:], 0))
            k0(pool.memset(lower[:], 1.0))
            k0(pool.memset(onesm[:], 1.0))
            k0(pool.memset(ones16[:], 1.0))
            k0(pool.iota(tok[:], [[P, NT]], base=0, channel_multiplier=1))
            k0(pool.iota(uiota[:], [[1, NU]], base=0, channel_multiplier=0, allow_small_or_imprecise_dtypes=True))
            k0(pool.memset(sc[:, :, E:24], -BIG))
            k0(pool.affine_select(lower[:], lower[:], [[1, P]], ALU.is_gt, 0.0, base=0, channel_multiplier=-1))
            pool.dma_start(tab_d.rearrange("(p u) o -> p (u o)", p=P), ids[:]).then_inc(sm["tab0"], 16)
            split(0, 0, 2)
            pool.dma_start(wraw[:], wall_in[1]).then_inc(sm["wraw_in"], 16)
            split(1, 1, 3)
            pool.dma_start(wraw[:], wall_in[2]).then_inc(sm["wraw_in"], 16)

            pool.wait_ge(sm["tab0"], 16)
            pool.wait_ge(sm["tables"], 1)
            for t in range(NT):
                for k in range(TOPK):
                    pool.indirect_dma_start(tab_d, bass.IndirectOffsetOnAxis(ap=tix[:, t, k:k + 1], axis=0),
                                            tok[:, t:t + 1], None).then_inc(sm["scat"], 16)
            pool.wait_ge(sm["scat"], 16 * NT * TOPK)
            pool.dma_start(ids[:], tab_d.rearrange("(p u) o -> p (u o)", p=P)).then_inc(sm["ids_in"], 16)
            pool.wait_ge(sm["ids_in"], 16)
            for j in range(2):
                pool.wait_ge(sm[f"store_in{j}"], 16 * (NT // 2))

            def gather(n, j):
                if holds(n, 2):
                    pool.wait_ge(sm[f"g_in{j}"], 16 * (n // 2))
                    pool.wait_ge(sm["u_tx"], n - 1)
                pool.tensor_copy(gidx[j][:, 0:1], ids[:, bass.ds(n, 1)]).then_inc(sm["gid"], 1)
                pool.wait_ge(sm["gid"], n + 1)
                carry(pool)
                pool.indirect_dma_start(xn[j][:], None, xn_d, bass.IndirectOffsetOnAxis(ap=gidx[j][:, 0:1], axis=0))\
                    .then_inc(sm[f"g_in{j}"], 16)

            def next_expert(n):
                first = pool.value_load(ufirst[0:1, bass.ds(n, 1)], min_val=0, max_val=1)
                with pool.If(first > 0):
                    e = pool.value_load(uexp[0:1, bass.ds(n, 1)], min_val=1, max_val=E - 2)
                    at = pool.value_load(upar[0:1, bass.ds(n, 1)], min_val=0, max_val=2)
                    pool.wait_ge(sm["u_y"], n)
                    pool.wait_ge(sm["wraw_in"], 16 * e + 48)
                    nxt = bass.ds((at + 1) % 3, 1)
                    pool.tensor_copy(wh[:, nxt, :], wraw[:].unsqueeze(1)).then_inc(sm["w_hi"], 1)
                    pool.wait_ge(sm["w_hi"], e + 3)
                    pool.tensor_tensor(wl[:, nxt, :], wraw[:].unsqueeze(1), wh[:, nxt, :].bitcast(F32), ALU.subtract)\
                        .then_inc(sm["w_split"], 1)
                    pool.wait_ge(sm["w_split"], e + 3)
                    pool.dma_start(wraw[:], wall_in[bass.ds(e + 2, 1)].rearrange("a p n -> p (a n)"))\
                        .then_inc(sm["wraw_in"], 16)

            pool.wait_ge(sm["utab"], 1)
            gather(0, 0)
            gather(1, 1)
            with pool.Fori(1, NU // 2) as h:
                for j in range(2):
                    gather(2 * h + j, j)
                    next_expert(2 * h + j - 1)
            next_expert(NU - 1)
            pool.wait_ge(sm["wraw_in"], 16 * (E + 2))

            for j in range(2):
                pool.wait_ge(sm[f"y_out{j}"], 16 * (NU // 2))
                pool.wait_ge(sm[f"g_in{j}"], 16 * (NU // 2))

            def collect(t, j):
                if holds(t, 2):
                    pool.wait_ge(sm[f"c_in{j}"], 64 * (t // 2))
                    pool.wait_ge(sm["c_add"], TOPK * t - TOPK)
                pool.tensor_copy(gidx[j][:], sidx[:, bass.ds(t, 1), :].rearrange("p a k -> p (a k)")).then_inc(sm["cid"], 1)
                pool.wait_ge(sm["cid"], t + 1)
                carry(pool)
                for k in range(TOPK):
                    pool.indirect_dma_start(cg[j][:, k, :], None, y_d,
                                            bass.IndirectOffsetOnAxis(ap=gidx[j][:, k:k + 1], axis=0))\
                        .then_inc(sm[f"c_in{j}"], 16)

            for t in range(2):
                collect(t, t)
            with pool.Fori(1, NT // 2) as h:
                for j in range(2):
                    collect(2 * h + j, j)

            pool.wait_ge(sm["c_add"], TOPK * NT)
            kd = [0]

            def k3(ins, wait=True):
                kd[0] += 1
                ins.then_inc(sm["konst3"], 1)
                if wait:
                    pool.wait_ge(sm["konst3"], kd[0])

            k3(pool.memset(wide[:], 0.0))
            k3(pool.affine_select(wide[:], wide[:], [[-1, 390]], ALU.not_equal, 1.0, base=P + 3, channel_multiplier=1))
            k3(pool.memset(ones3[:], 1.0))
            k3(pool.memset(pr[0][:], -1.0))
            k3(pool.memset(pr[1][:], -1.0))

            def rest(t, j):
                pool.wait_ge(sm["c3"], t + 1)
                if holds(t, 2):
                    pool.wait_ge(sm["m3"], 2 * t - 2)
                pool.tensor_tensor(sf[j][:], x3T[:, :, bass.ds(t * P, P)], cf[j][:], ALU.subtract).then_inc(sm["d3"], 1)

            for t in range(2):
                rest(t, t)
            with pool.Fori(1, NT // 2) as h:
                for j in range(2):
                    rest(2 * h + j, j)

            pool.wait_ge(sm["w4_in"], 64)
            for n, (raw, parts) in enumerate(((wb, wbs), (aw, aws), (bm, bms))):
                pool.tensor_copy(parts[0][:], raw[:]).then_inc(sm["w4_split"], 1)
                pool.wait_ge(sm["w4_split"], 2 * n + 1)
                pool.tensor_tensor(parts[1][:], raw[:], parts[0][:].bitcast(F32), ALU.subtract).then_inc(sm["w4_split"], 1)
                pool.wait_ge(sm["w4_split"], 2 * n + 2)
            k3(pool.tensor_scalar(b1[:], b1[:], tg[:, 3:4], None, ALU.mult))

            def add_bias4(t):
                pool.wait_ge(sm["l4"], t + 1)
                pool.tensor_tensor(X[:, bass.ds(t, 1), :], X[:, bass.ds(t, 1), :], b1[:].unsqueeze(1), ALU.add)\
                    .then_inc(sm["cpre"], 1)

            with pool.Fori(0, NT) as t:
                add_bias4(t)

        @block.scalar
        def _(act):
            act.wait_ge(sm["cst_in"], 16)
            act.activation(tg[:], cst[:, C_GATE:C_GATE + 4], ACT.Tanh).then_inc(sm["gates"], 1)

            def sqrt(lo, n, count):
                act.wait_ge(sm["lnvar"], 7 * count)
                act.activation(sd[:, bass.ds(lo, n)], va[:, bass.ds(lo, n)],
                               ACT.Sqrt, bias=eps[:, 0:1]).then_inc(sm["lnsd"], 1)

            act.wait_ge(sm["konst"], 5)

            def stage1a(s):
                sqrt(4 * s, 4, s + 1)
                for i in range(4):
                    t = 4 * s + i
                    act.wait_ge(sm["tx_done"], t + 1)
                    if i == 0 and holds(s, 1):
                        act.wait_ge(sm["proj_done"], 6 * s - 2)
                    act.copy(xnT[:, :, i * P:(i + 1) * P],
                             bank[2 + i % 2][:].rearrange("p (k n) -> p k n", k=KD)).then_inc(sm["xnT_ready"], 1)
                for q in range(6):
                    act.wait_ge(sm["proj_done"], 6 * s + q + 1)
                    if q < 4:
                        dst, bias, scale = QT[:, q, bass.ds(s * 512, 512)], cst[:, C_BQ + q:C_BQ + q + 1], 0.25
                    elif q == 4:
                        dst, bias, scale = KT[:, bass.ds(s * 512, 512)], cst[:, C_BK:C_BK + 1], 1.0
                    else:
                        dst, bias, scale = VT[:, bass.ds(s * 512, 512)], cst[:, C_BV:C_BV + 1], 1.0
                    act.activation(dst, bank[q % 2][:], ACT.Identity, bias=bias, scale=scale).then_inc(sm["proj_out"], 1)

            stage1a(0)
            with act.Fori(1, 4) as s:
                stage1a(s)

            def exps(u, j):
                act.wait_ge(sm["dif_ready"], u + 1)
                if holds(u, 2):
                    act.wait_ge(sm["pt_done"], u - 1)
                act.activation(prob[j][:], dif[j][:].rearrange("p h k -> p (h k)"), ACT.Exp).then_inc(sm["exp_done"], 1)

            def prob_out(u, j):
                act.wait_ge(sm["pt_done"], u + 1)
                if holds(u, 2):
                    act.wait_ge(sm["pv_done"], u - 1)
                act.copy(probT[j][:].rearrange("p a q -> p (a q)"), bank[2 + j][:]).then_inc(sm["ptc_done"], 1)

            def v_out(b, j):
                act.wait_ge(sm["v_done"], b + 1)
                if holds(b, 2):
                    act.wait_ge(sm["pv_done"], 2 * b - 2)
                v = bank[5][:, 0:P].rearrange("p (a h d) -> p a h d", a=4, h=2)
                act.copy(vblk[j][0:S, :, 0:HD], v[0:S, :, 0, :]).then_inc(sm["v_ready"], 1)
                act.copy(vblk[j][S:P, :, HD:2 * HD], v[S:P, :, 1, :]).then_inc(sm["v_ready"], 1)

            def yT_out(u, i):
                act.wait_ge(sm["yt_done"], u + 1)
                if i == 0 and holds(u, 4):
                    act.wait_ge(sm["wo_done"], u // 4)
                g, b = 2 * (i % 2), i // 2
                act.copy(yT[:, g:g + 2, b * S:(b + 1) * S],
                         bank[7][:, 0:P].rearrange("p (g q) -> p g q", g=2))\
                    .then_inc(sm["ytc_done"], 1)

            def att_act(u, i):
                if below(u, 2 * B):
                    prob_out(u, i % 2)
                if i % 2 == 1 and below(u, 2 * B - 1):
                    v_out((u + 1) // 2, (i + 1) // 2 % 2)
                if holds(u, 2) and below(u, 2 * B + 2):
                    yT_out(u - 2, (i - 2) % 4)
                if below(u, 2 * B - 1):
                    exps(u + 1, (i + 1) % 2)

            v_out(0, 0)
            exps(0, 0)
            for i in range(4):
                att_act(i, i)
            with act.Fori(1, NT - 1) as t:
                for i in range(4):
                    att_act(4 * t + i, i)
            for u in range(2 * B - 4, 2 * B + 2):
                att_act(u, u % 4)

            def hi(p, n, j):
                act.wait_ge(sm[p + "tx"], n + 1)
                if holds(n, 2):
                    act.wait_ge(sm[p + "gu"], n - 1)
                act.copy(xh[j][:].rearrange("p k n -> p (k n)"), bank[j][:]).then_inc(sm[p + "hi"], 1)

            def silu(p, n, j):
                act.wait_ge(sm[p + "gu"], n + 1)
                if holds(n, 2):
                    act.wait_ge(sm[p + "z"], n - 1)
                act.activation(sg[j][:], bank[2 + j][:, 0:I], ACT.Silu).then_inc(sm[p + "sg"], 1)

            def z_hi(p, n, j):
                act.wait_ge(sm[p + "zt"], n + 1)
                if holds(n, 2):
                    act.wait_ge(sm[p + "y"], n - 1)
                act.copy(zh[j][:].rearrange("p k n -> p (k n)"), bank[4][:, 0:I]).then_inc(sm[p + "zh"], 1)

            def logits_out(n):
                act.wait_ge(sm["a_rt"], n + 1)
                act.copy(lg[:, bass.ds(n, 1), :].rearrange("p a e -> p (a e)"), bank[7][:, 0:E]).then_inc(sm["a_rtc"], 1)

            def y_out(n, j):
                act.wait_ge(sm["u_y"], n + 1)
                if holds(n, 2):
                    act.wait_ge(sm[f"y_out{j}"], 16 * (n // 2))
                act.copy(yo[j][:], bank[5 + j][:]).then_inc(sm["u_yo"], 1)

            def shared_act(n, j):
                if below(n, NT - 1):
                    hi("a_", n + 1, 1 - j)
                if holds(n, 1) and below(n, NT + 1):
                    z_hi("a_", n - 1, 1 - j)
                if below(n, NT):
                    silu("a_", n, j)
                    logits_out(n)

            sqrt(0, NT, 5)
            hi("a_", 0, 0)
            for n in range(2):
                shared_act(n, n)
            with act.Fori(1, (NT - 2) // 2) as h:
                for j in range(2):
                    shared_act(2 * h + j, j)
            for n in range(NT - 2, NT + 1):
                shared_act(n, n % 2)
            act.wait_ge(sm["a_rtc"], NT)
            act.activation(sc[:, :, 0:E], lg[:], ACT.Sigmoid).then_inc(sm["rsig"], 1)

            def negate(g):
                if holds(g, 1):
                    act.wait_ge(sm["tstep"], 10 * g)
                src = ctxT[:, bass.ds(g // 4, 1), bass.ds((g % 4) * 512, 512)].rearrange("p a (b c) -> p (a b) c", c=S)
                act.mul(neg[0][:, :, ::-1], src, -1.0).then_inc(sm["neg_done"], 1)

            def unit_act(n, j):
                if below(n, NU - 1):
                    hi("u_", n + 1, 1 - j)
                if holds(n, 2) and below(n, NU + 2):
                    y_out(n - 2, j)
                if holds(n, 1) and below(n, NU + 1):
                    z_hi("u_", n - 1, 1 - j)
                if below(n, NU):
                    silu("u_", n, j)

            negate(0)
            hi("u_", 0, 0)
            for n in range(2):
                unit_act(n, n)
            unit_act(2, 0)
            unit_act(3, 1)
            negate(1)
            with act.Fori(1, 15) as h:
                for j in range(4):
                    unit_act(4 * h + j, j % 2)
                negate(h + 1)
            with act.Fori(30, (NU - 2) // 2) as h:
                for j in range(2):
                    unit_act(2 * h + j, j)
            for n in range(NU - 2, NU + 2):
                unit_act(n, n % 2)

            sqrt(0, NT, 6)

            def x3_out(t, j):
                act.wait_ge(sm["t_done"], t + 1)
                act.copy(x3T[:, :, bass.ds(t * P, P)], bank[j][:].rearrange("p (k n) -> p k n", k=KD))\
                    .then_inc(sm["x3_done"], 1)

            with act.Fori(0, NT // 2) as h:
                for j in range(2):
                    x3_out(2 * h + j, j)
            act.wait_ge(sm["bn_step"], 8)
            act.activation(gain[:], var[:], ACT.Sqrt, bias=eps[:, 0:1]).then_inc(sm["bn_act"], 1)
            act.wait_ge(sm["bn_step"], 13)
            act.activation(amap[:], zc[:], ACT.Sigmoid).then_inc(sm["bn_act"], 1)

            sqrt(0, NT, 7)

            def f_hi(n, j):
                act.wait_ge(sm["f_tx"], n + 1)
                if holds(n, 2):
                    act.wait_ge(sm["f_base"], n - 1)
                act.copy(fh[j][:].rearrange("p k n -> p (k n)"), bank[j][:]).then_inc(sm["f_hi"], 1)

            def f_exp(n, j):
                act.wait_ge(sm["f_step"], NF * n + 2)
                act.activation(pr[j][:, 0:LE], bank[4 + j][:, P:P + LE], ACT.Exp, bias=nm[j][:, 0:1],
                               accum_out=nm[j][:, 1:2]).then_inc(sm["f_exp"], 1)

            def f_hth(n, j):
                act.wait_ge(sm["f_ht"], n + 1)
                if holds(n, 2):
                    act.wait_ge(sm["f_fin"], n - 1)
                act.copy(hth[j][:], bank[6][:, 0:P]).then_inc(sm["f_hth"], 1)

            def lora_act(n, j):
                if below(n, NT - 1):
                    f_hi(n + 1, 1 - j)
                if holds(n, 1) and below(n, NT + 1):
                    f_hth(n - 1, 1 - j)
                if below(n, NT):
                    f_exp(n, j)

            f_hi(0, 0)
            for n in range(2):
                lora_act(n, n)
            with act.Fori(1, (NT - 2) // 2) as h:
                for j in range(2):
                    lora_act(2 * h + j, j)
            for n in range(NT - 2, NT + 1):
                lora_act(n, n % 2)

        @block.vector
        def _(dve):
            def ln_stats(t):
                dve.bn_stats(stats[:, bass.ds(t, 1), :].rearrange("p a s -> p (a s)"),
                             X[:, bass.ds(t, 1), :].rearrange("p a d -> p (a d)")).then_inc(sm["lnstat"], 1)

            def ln_scale(lo, n, tiles, count):
                dve.wait_ge(sm["lnstat"], tiles)
                at = bass.ds(lo, n)
                m_e, v_e, m_o, v_o = (stats[:, at, c:c + 1].rearrange("p t o -> p (t o)") for c in (1, 2, 4, 5))
                for n_, ins in enumerate((
                        lambda: dve.tensor_tensor(mu[:, at], m_e, m_o, ALU.add),
                        lambda: dve.tensor_scalar(mu[:, at], mu[:, at], 0.5, None, ALU.mult),
                        lambda: dve.tensor_tensor(dm[:, at], m_e, m_o, ALU.subtract),
                        lambda: dve.tensor_tensor(dm[:, at], dm[:, at], dm[:, at], ALU.mult),
                        lambda: dve.tensor_tensor(va[:, at], v_e, v_o, ALU.add),
                        lambda: dve.tensor_scalar(va[:, at], va[:, at], 1.0 / D, None, ALU.mult),
                        lambda: dve.scalar_tensor_tensor(va[:, at], dm[:, at], 0.25, va[:, at], ALU.mult, ALU.add))):
                    ins().then_inc(sm["lnvar"], 1)
                    dve.wait_ge(sm["lnvar"], 7 * count - 6 + n_)
                dve.wait_ge(sm["lnsd"], count)
                dve.reciprocal(rs[:, at], sd[:, at]).then_inc(sm["lnrs"], 1)
                dve.wait_ge(sm["lnrs"], count)

            def ln_apply(t, j, done):
                return dve.tensor_scalar(xn[j][:], X[:, bass.ds(t, 1), :].rearrange("p a d -> p (a d)"),
                                         mu[:, bass.ds(t, 1)],
                                         rs[:, bass.ds(t, 1)], ALU.subtract, ALU.mult).then_inc(sm[done], 1)

            dve.wait_ge(sm["cst_in"], 16)
            dve.tensor_scalar(cst[:, C_BQ:C_BQ + NG], cst[:, C_BQ:C_BQ + NG], 0.25, None, ALU.mult).then_inc(sm["sum_step"], 1)

            def stage1a(s):
                dve.wait_ge(sm["x_in"], 16 * s + 16)
                for i in range(4):
                    ln_stats(4 * s + i)
                ln_scale(4 * s, 4, 4 * s + 4, s + 1)
                for i in range(4):
                    t = 4 * s + i
                    if holds(t, 2):
                        dve.wait_ge(sm["tx_done"], t - 1)
                    ln_apply(t, i % 2, "xn_ready")

            stage1a(0)
            with dve.Fori(1, 4) as s:
                stage1a(s)

            def shift(u, j):
                dve.wait_ge(sm["s_ready"], u + 1)
                sc_v = bank[j][:].rearrange("p (h k) -> p h k", h=NKV)
                dve.tensor_reduce(mx[j][:], sc_v, AX, ALU.max).then_inc(sm["mx_ready"], 1)
                dve.wait_ge(sm["mx_ready"], u + 1)
                if holds(u, 2):
                    dve.wait_ge(sm["exp_done"], u - 1)
                dve.tensor_tensor(dif[j][:], sc_v, mx[j][:].unsqueeze(2).broadcast_to([P, NKV, S]), ALU.subtract)\
                    .then_inc(sm["dif_ready"], 1)

            def normalise(u, j):
                dve.wait_ge(sm["pv_done"], u + 1)
                o = bank[6][:, 0:136].rearrange("p (a n) -> p a n", a=4)
                dve.reciprocal(rec[j][:], o[:, :, 32:34]).then_inc(sm["rec_ready"], 1)
                dve.wait_ge(sm["rec_ready"], u + 1)
                if holds(u, 2):
                    dve.wait_ge(sm["yt_done"], u - 1)
                dve.tensor_tensor(yn[j][:], o[:, :, 0:32].rearrange("p a (h d) -> p a h d", h=2),
                                  rec[j][:].unsqueeze(3).broadcast_to([P, 4, 2, HD]), ALU.mult)\
                    .then_inc(sm["yn_ready"], 1)

            def residual1(t):
                dve.wait_ge(sm["wo_done"], t + 1)
                dve.wait_ge(sm["x4b"], t + 1)
                dve.scalar_tensor_tensor(X[:, bass.ds(t, 1), :].rearrange("p a d -> p (a d)"), bank[4][:], tg[:, 0:1],
                                         X[:, bass.ds(t, 1), :].rearrange("p a d -> p (a d)"), ALU.mult, ALU.add)\
                    .then_inc(sm["x1_done"], 1)
                dve.wait_ge(sm["x1_done"], t + 1)
                ln_stats(t)

            def att_dve(u, i):
                if below(u, 2 * B - 1):
                    shift(u + 1, (i + 1) % 2)
                if holds(u, 1) and below(u, 2 * B + 1):
                    normalise(u - 1, (i - 1) % 2)
                if i == 2 and holds(u, 4):
                    residual1((u - 2) // 4 - 1)

            dve.wait_ge(sm["gates"], 1)
            shift(0, 0)
            for i in range(4):
                att_dve(i, i)
            with dve.Fori(1, NT - 1) as t:
                for i in range(4):
                    if below(t, NT):
                        shift(4 * t + i + 1, (i + 1) % 2)
                        normalise(4 * t + i - 1, (i - 1) % 2)
                        if i == 2:
                            residual1(t - 1)
            for u in range(2 * B - 4, 2 * B + 1):
                att_dve(u, u % 4)
            residual1(NT - 1)

            ln_scale(0, NT, 2 * NT, 5)
            for n, (o, i) in enumerate(((gwh, gw), (gwl, gw))):
                dve.wait_ge(sm["gw_in"], 16)
                if n == 0:
                    dve.tensor_copy(gwh[:], gw[:]).then_inc(sm["sum_step"], 1)
                    dve.wait_ge(sm["sum_step"], 2)
                else:
                    dve.tensor_tensor(gwl[:], gw[:], gwh[:].bitcast(F32), ALU.subtract).then_inc(sm["sum_step"], 1)

            def x2n(n, j):
                if holds(n, 2):
                    dve.wait_ge(sm["a_tx"], n - 1)
                    dve.wait_ge(sm[f"store_in{j}"], 16 * (n // 2))
                ln_apply(n, j, "n2")

            def lo(p, n, j):
                dve.wait_ge(sm[p + "hi"], n + 1)
                dve.tensor_tensor(xl[j][:].rearrange("p k n -> p (k n)"), bank[j][:],
                                  xh[j][:].rearrange("p k n -> p (k n)").bitcast(F32), ALU.subtract)\
                    .then_inc(sm[p + "lo"], 1)

            def z_lo(p, n, j):
                dve.wait_ge(sm[p + "zh"], n + 1)
                dve.tensor_tensor(zl[j][:].rearrange("p k n -> p (k n)"), bank[4][:, 0:I],
                                  zh[j][:].rearrange("p k n -> p (k n)").bitcast(F32), ALU.subtract)\
                    .then_inc(sm[p + "zl"], 1)

            def inner(p, n, j):
                dve.wait_ge(sm[p + "sg"], n + 1)
                if holds(n, 2):
                    dve.wait_ge(sm[p + "zt"], n - 1)
                dve.tensor_tensor(zz[j][:], bank[2 + j][:, I:2 * I], sg[j][:], ALU.mult).then_inc(sm[p + "z"], 1)

            def shared_out(n, j):
                dve.wait_ge(sm["a_y"], n + 1)
                xt = X[:, bass.ds(n, 1), :].rearrange("p a d -> p (a d)")
                dve.scalar_tensor_tensor(xt, bank[5 + j][:], tg[:, 2:3], xt, ALU.mult, ALU.add).then_inc(sm["a_x"], 1)

            def shared_dve(n, j):
                if below(n, NT - 2):
                    x2n(n + 2, j)
                if below(n, NT - 1):
                    lo("a_", n + 1, 1 - j)
                if holds(n, 2) and below(n, NT + 2):
                    shared_out(n - 2, j)
                if holds(n, 1) and below(n, NT + 1):
                    z_lo("a_", n - 1, 1 - j)
                if below(n, NT):
                    inner("a_", n, j)

            x2n(0, 0)
            x2n(1, 1)
            lo("a_", 0, 0)
            for n in range(2):
                shared_dve(n, n)
            with dve.Fori(1, (NT - 2) // 2) as h:
                for j in range(2):
                    shared_dve(2 * h + j, j)
            for n in range(NT - 2, NT + 2):
                shared_dve(n, n % 2)

            rc = [0]

            def r(ins, wait=True):
                rc[0] += 1
                ins.then_inc(sm["rstep"], 1)
                if wait:
                    dve.wait_ge(sm["rstep"], rc[0])

            dve.wait_ge(sm["rsig"], 1)
            dve.wait_ge(sm["konst"], KONST2)
            rb = cst[:, C_RB:C_RB + E].unsqueeze(1).broadcast_to([P, NT, E])
            r(dve.tensor_tensor(sc[:, :, 0:E], sc[:, :, 0:E], rb, ALU.add))
            for t in range(NT):
                r(dve.max(v8[:, t, :], sc[:, t, 0:E]), t == NT - 1)
            r(dve.tensor_reduce(wsum[:], v8[:, :, 0:TOPK], AX, ALU.add))
            r(dve.tensor_scalar(wsum[:], wsum[:], 1e-20, None, ALU.add))
            r(dve.reciprocal(wrec[:], wsum[:]))
            r(dve.tensor_scalar(wrec[:], wrec[:], tg[:, 2:3], None, ALU.mult))
            r(dve.memset(v8[:, :, TOPK:8], -BIG))
            for t in range(NT):
                r(dve.match_replace(scr[:, t, :], v8[:, t, :], sc[:, t, :], BIG), t == NT - 1)
            r(dve.tensor_scalar(sel[:], scr[:, :, 0:E], 1e38, None, ALU.is_gt), False)
            dve.wait_ge(sm["rstep"], rc[0])
            dve.sem_inc(sm["sel_ready"], 1)
            r(dve.memset(pre[:, 0, :], 0.0))
            dve.wait_ge(sm["rmm"], 1)
            for t in range(NT):
                r(dve.tensor_tensor(pre[:, t + 1, :], pre[:, t, :], bank[1][:, t * E:(t + 1) * E], ALU.add))
            r(dve.tensor_scalar(ucnt[:], pre[:, NT, :], float(P - 1), None, ALU.add))
            r(dve.tensor_scalar(ushf[:], ucnt[:], 7, None, ALU.arith_shift_right))
            r(dve.tensor_scalar(unum[:], ushf[:], 1.0, None, ALU.max))
            r(dve.tensor_tensor_scan(uend[:], ones16[:], unum[:], 0.0, ALU.mult, ALU.add))
            r(dve.tensor_tensor(ubase[:], uend[:], unum[:], ALU.subtract))
            r(dve.tensor_scalar(ubase[:], ubase[:], float(P), 1.0, ALU.mult, ALU.add))
            r(dve.tensor_tensor(slot[:], bank[0][:, 0:NT * E].rearrange("p (t e) -> p t e", e=E), pre[:, 0:NT, :], ALU.add))
            r(dve.tensor_tensor(slot[:], slot[:], ubase[:].unsqueeze(1).broadcast_to([P, NT, E]), ALU.add))
            r(dve.tensor_tensor(slot[:], slot[:], sel[:], ALU.mult))
            for t in range(NT):
                r(dve.max(k8[:, t, :], slot[:, t, :]), t == NT - 1)
            r(dve.tensor_scalar(sidx[:], k8[:, :, 0:TOPK], -1.0, None, ALU.add))
            r(dve.tensor_scalar(tix[:], sidx[:], P - 1, None, ALU.bitwise_and))
            r(dve.tensor_scalar(tiy[:], sidx[:], 7, None, ALU.arith_shift_right))
            r(dve.scalar_tensor_tensor(tix[:], tix[:], float(NU), tiy[:], ALU.mult, ALU.add))
            dve.sem_inc(sm["tables"], 1)
            for k in range(TOPK):
                r(dve.tensor_tensor(eq[:], slot[:], k8[:, :, k:k + 1].broadcast_to([P, NT, E]), ALU.is_equal))
                r(dve.tensor_tensor(eq[:], eq[:], sc[:, :, 0:E], ALU.mult))
                r(dve.tensor_reduce(wk[:, :, k], eq[:], AX, ALU.add))
            r(dve.tensor_tensor(wk[:], wk[:], wrec[:].unsqueeze(2).broadcast_to([P, NT, TOPK]), ALU.mult))
            r(dve.tensor_tensor(ule[:], uend[0:1, :].unsqueeze(1).broadcast_to([1, NU, E]),
                                uiota[:].unsqueeze(2).broadcast_to([1, NU, E]), ALU.is_le))
            r(dve.memset(ueid[:, 0:1], 0.0))
            r(dve.tensor_reduce(ueid[:, 1:NU + 1], ule[:], AX, ALU.add))
            r(dve.tensor_scalar(ueid[:, 1:NU + 1], ueid[:, 1:NU + 1], float(E - 1), None, ALU.min))
            r(dve.tensor_copy(uexp[:, 0:NU], ueid[:, 1:NU + 1]))
            gt = ule[:, 0:NU, 0]
            r(dve.tensor_tensor(gt, ueid[:, 1:NU + 1], ueid[:, 0:NU], ALU.is_gt))
            r(dve.scalar_tensor_tensor(ufirst[:], ueid[:, 1:NU + 1], E - 1.5, gt, ALU.is_lt, ALU.mult))
            r(dve.tensor_scalar(gt, ueid[:, 1:NU + 1], 3.0, None, ALU.is_ge))
            for m in range(6, E, 3):
                r(dve.scalar_tensor_tensor(gt, ueid[:, 1:NU + 1], float(m), gt, ALU.is_ge, ALU.add))
            r(dve.scalar_tensor_tensor(upar[:], gt, -3.0, ueid[:, 1:NU + 1], ALU.mult, ALU.add))
            dve.sem_inc(sm["utab"], 1)

            def choose(g, rnd):
                c0 = 10 * g + 2 * rnd
                if rnd == 0:
                    dve.wait_ge(sm["neg_done"], g + 1)
                    carry(dve)
                for b in range(8):
                    mxi = dve.max(best[:, b, :], neg[0][:, b, :])
                mxi.then_inc(sm["tstep"], 1)
                dve.wait_ge(sm["tstep"], c0 + 1)
                if rnd < 3:
                    carry(dve)
                if rnd == 3:
                    dve.memset(best[:, :, NSUB - 24:8], -BIG).then_inc(sm["tstep"], 1)
                    c0 += 1
                    dve.wait_ge(sm["tstep"], c0 + 1)
                    carry(dve)
                for b in range(8):
                    mr = dve.match_replace(neg[0][:, b, :], best[:, b, :], neg[0][:, b, :], -BIG)
                mr.then_inc(sm["tstep"], 1)
                dve.wait_ge(sm["tstep"], c0 + 2)
                if rnd == 3:
                    dst = ctxT[:, bass.ds(g // 4, 1), bass.ds((g % 4) * 512, 512)]\
                        .rearrange("p a (b c) -> p (a b) c", c=S)
                    dve.tensor_scalar(dst, neg[0][:, :, ::-1], -1e38, None, ALU.is_lt).then_inc(sm["tstep"], 1)

            def unit_dve(n, j, g=None, rnd=0):
                if below(n, NU - 1):
                    lo("u_", n + 1, 1 - j)
                if holds(n, 1) and below(n, NU + 1):
                    z_lo("u_", n - 1, 1 - j)
                if g is not None:
                    choose(g, rnd)
                if below(n, NU):
                    inner("u_", n, j)

            lo("u_", 0, 0)
            for n in range(4):
                unit_dve(n, n % 2, 0, n)
            with dve.Fori(1, 16) as g:
                for i in range(4):
                    unit_dve(4 * g + i, i % 2, g, i)
            with dve.Fori(32, (NU - 2) // 2) as h:
                for j in range(2):
                    unit_dve(2 * h + j, j)
            for n in range(NU - 2, NU + 1):
                unit_dve(n, n % 2)

            def combine(t, j):
                xt = X[:, bass.ds(t, 1), :].rearrange("p a d -> p (a d)")
                dve.wait_ge(sm[f"c_in{j}"], 64 * (t // 2) + 64)
                for k in range(TOPK):
                    dve.scalar_tensor_tensor(xt, cg[j][:, k, :], wk[:, bass.ds(t, 1), k:k + 1].rearrange("p a k -> p (a k)"),
                                             xt, ALU.mult, ALU.add).then_inc(sm["c_add"], 1)
                    dve.wait_ge(sm["c_add"], TOPK * t + k + 1)
                ln_stats(t)

            dve.wait_ge(sm["a_x"], NT)
            with dve.Fori(0, NT // 2) as h:
                for j in range(2):
                    combine(2 * h + j, j)

            ln_scale(0, NT, 3 * NT, 6)

            def x3n(t, j):
                if holds(t, 2):
                    dve.wait_ge(sm["t_done"], t - 1)
                ln_apply(t, j, "l3")

            def features(t, j):
                dve.wait_ge(sm["x3_done"], t + 1)
                if holds(t, 2):
                    dve.wait_ge(sm["d3"], t - 1)
                m = ctxT[:, :, bass.ds(t * P, P)]
                dve.scalar_tensor_tensor(cf[j][:], m, 0.5, x3T[:, :, bass.ds(t * P, P)], ALU.is_lt, ALU.mult)\
                    .then_inc(sm["c3"], 1)
                dve.wait_ge(sm["c3"], t + 1)
                cv = cf[j][:].rearrange("p k (b c) -> p k b c", c=S)
                dve.tensor_reduce(maps[:, 0, :, 0, bass.ds(2 * t, 2)], cv, AX, ALU.max)
                dve.tensor_reduce(maps[:, 1, :, 0, bass.ds(2 * t, 2)], cv, AX, ALU.add)

            def features_rest(t, j):
                dve.wait_ge(sm["d3"], t + 1)
                sv = sf[j][:].rearrange("p k (b c) -> p k b c", c=S)
                dve.tensor_reduce(maps[:, 0, :, 1, bass.ds(2 * t, 2)], sv, AX, ALU.max).then_inc(sm["m3"], 1)
                dve.tensor_reduce(maps[:, 1, :, 1, bass.ds(2 * t, 2)], sv, AX, ALU.add).then_inc(sm["m3"], 1)

            def gate_dve(t, j):
                if below(t, NT - 2):
                    x3n(t + 2, j)
                if below(t, NT):
                    features(t, j)
                if holds(t, 1):
                    features_rest(t - 1, 1 - j)

            x3n(0, 0)
            x3n(1, 1)
            for t in range(2):
                gate_dve(t, t)
            with dve.Fori(1, (NT - 2) // 2) as h:
                for j in range(2):
                    gate_dve(2 * h + j, j)
            for t in range(NT - 2, NT + 1):
                gate_dve(t, t % 2)
            dve.wait_ge(sm["m3"], 2 * NT)

            cc = [0]

            def c(ins):
                cc[0] += 1
                ins.then_inc(sm["conv_done"], 1)
                dve.wait_ge(sm["conv_done"], cc[0])

            c(dve.tensor_scalar(maps[:, 1, :, 0, :], maps[:, 1, :, 0, :], 1.0 / NSEL, None, ALU.mult))
            c(dve.tensor_scalar(maps[:, 1, :, 1, :], maps[:, 1, :, 1, :], 1.0 / NSUB, None, ALU.mult))
            dve.wait_ge(sm["konst3"], 5)
            for ch in range(2):
                for w in range(7):
                    tap = cst[:, C_CONV + 7 * ch + w:C_CONV + 7 * ch + w + 1]
                    if w == 0:
                        c(dve.tensor_scalar(band[:, ch, :], wide[:, 0:384], tap, None, ALU.mult))
                    else:
                        c(dve.scalar_tensor_tensor(band[:, ch, :], wide[:, w:w + 384], tap, band[:, ch, :],
                                                   ALU.mult, ALU.add))
            dve.sem_inc(sm["as3"], 1)

            bc = [0]

            def b_(ins):
                bc[0] += 1
                ins.then_inc(sm["bn_step"], 1)
                dve.wait_ge(sm["bn_step"], bc[0])

            dve.wait_ge(sm["bn_mm"], 1)
            b_(dve.tensor_copy(zc[:], bank[4][:, 0:2 * KD * B].rearrange("p (k r b) -> p r k b", k=KD, r=2)))
            b_(dve.tensor_reduce(part[:], zc[:].rearrange("p r k b -> p r (k b)"), AX, ALU.add))
            dve.wait_ge(sm["bn_mm"], 2)
            b_(dve.tensor_scalar(mean[:], bank[5][:, 0:2], 1.0 / (B * D), None, ALU.mult))
            for rr in range(2):
                b_(dve.tensor_scalar(zc[:, rr], zc[:, rr], mean[:, rr:rr + 1], None, ALU.subtract))
            b_(dve.tensor_tensor(zq[:], zc[:], zc[:], ALU.mult))
            b_(dve.tensor_reduce(part[:], zq[:].rearrange("p r k b -> p r (k b)"), AX, ALU.add))
            dve.wait_ge(sm["bn_mm"], 3)
            b_(dve.tensor_scalar(var[:], bank[5][:, 0:2], 1.0 / (B * D), None, ALU.mult))
            dve.wait_ge(sm["bn_act"], 1)
            b_(dve.reciprocal(gain[:], gain[:]))
            b_(dve.tensor_scalar(gain[:], gain[:], cst[:, C_BN:C_BN + 1], None, ALU.mult))
            for rr in range(2):
                b_(dve.tensor_scalar(zc[:, rr], zc[:, rr], gain[:, rr:rr + 1], cst[:, C_BN + 1:C_BN + 2], ALU.mult, ALU.add))
            b_(dve.tensor_scalar(zc[:], zc[:], 0.0, None, ALU.max))
            dve.wait_ge(sm["bn_act"], 2)
            b_(dve.tensor_tensor(amap[:, 1], amap[:, 1], amap[:, 0], ALU.subtract))

            def gated(t, j):
                xv = x3T[:, :, bass.ds(t * P, P)].rearrange("p k (b c) -> p k b c", c=S)
                mk = ctxT[:, :, bass.ds(t * P, P)].rearrange("p k (b c) -> p k b c", c=S)
                av = asel[j][:].rearrange("p k (b c) -> p k b c", c=S)
                if holds(t, 2):
                    dve.wait_ge(sm["y3t"], t - 1)
                for n, (o, a, b, op) in enumerate((
                        (av, mk, amap[:, 1, :, bass.ds(2 * t, 2)].unsqueeze(3).broadcast_to([P, KD, 2, S]), ALU.mult),
                        (av, av, amap[:, 0, :, bass.ds(2 * t, 2)].unsqueeze(3).broadcast_to([P, KD, 2, S]), ALU.add),
                        (av, av, xv, ALU.mult))):
                    dve.tensor_tensor(o, a, b, op).then_inc(sm["y3"], 1)
                    if n < 2:
                        dve.wait_ge(sm["y3"], 3 * t + n + 1)

            def residual3(t, j):
                dve.wait_ge(sm["y3t"], t + 1)
                xt = X[:, bass.ds(t, 1), :].rearrange("p a d -> p (a d)")
                dve.scalar_tensor_tensor(xt, bank[2 + j][:], tg[:, 1:2], xt, ALU.mult, ALU.add).then_inc(sm["x3_sum"], 1)
                dve.wait_ge(sm["x3_sum"], t + 1)
                ln_stats(t)

            def gated_step(t, j):
                if below(t, NT):
                    gated(t, j)
                if holds(t, 1):
                    residual3(t - 1, 1 - j)

            for t in range(2):
                gated_step(t, t)
            with dve.Fori(1, (NT - 2) // 2) as h:
                for j in range(2):
                    gated_step(2 * h + j, j)
            for t in range(NT - 2, NT + 1):
                gated_step(t, t % 2)

            ln_scale(0, NT, 4 * NT, 7)

            def x4n(t, j):
                if holds(t, 2):
                    dve.wait_ge(sm["f_tx"], t - 1)
                ln_apply(t, j, "l4")

            def f_lo(n, j):
                dve.wait_ge(sm["f_hi"], n + 1)
                dve.tensor_tensor(fl[j][:].rearrange("p k n -> p (k n)"), bank[j][:],
                                  fh[j][:].rearrange("p k n -> p (k n)").bitcast(F32), ALU.subtract)\
                    .then_inc(sm["f_lo"], 1)

            def f_route(n, j):
                dve.wait_ge(sm["f_h"], n + 1)
                carry(dve)
                hb = bank[4 + j]
                step = [0]

                def q(ins):
                    step[0] += 1
                    ins.then_inc(sm["f_step"], 1)
                    dve.wait_ge(sm["f_step"], NF * n + step[0])
                    if step[0] in (4, 8):
                        carry(dve)

                q(dve.max(m8[j][:], hb[:, P:P + LE]))
                q(dve.tensor_scalar(nm[j][:, 0:1], m8[j][:, 0:1], -1.0, None, ALU.mult))
                dve.wait_ge(sm["f_exp"], n + 1)
                q(dve.reciprocal(nm[j][:, 2:3], nm[j][:, 1:2]))
                q(dve.tensor_scalar(pr[j][:, 0:LE], pr[j][:, 0:LE], nm[j][:, 2:3], None, ALU.mult))
                q(dve.max(m8[j][:], pr[j][:, 0:LE]))
                q(dve.tensor_tensor(nm[j][:, 3:4], m8[j][:, 0:1], m8[j][:, 1:2], ALU.add))
                q(dve.memset(m8[j][:, 2:8], -1.0))
                q(dve.reciprocal(nm[j][:, 4:5], nm[j][:, 3:4]))
                q(dve.match_replace(prr[j][:], m8[j][:], pr[j][:], BIG))
                q(dve.scalar_tensor_tensor(lw[j][:], prr[j][:, 0:LE], 1e38, pr[j][:, 0:LE], ALU.is_gt, ALU.mult))
                q(dve.tensor_scalar(lw[j][:], lw[j][:], nm[j][:, 4:5], 2.0, ALU.mult, ALU.mult))
                assert step[0] == NF
                if holds(n, 2):
                    dve.wait_ge(sm["f_ht"], n - 1)
                dve.tensor_tensor(hw[j][:].rearrange("p (e r) -> p e r", e=LE), hb[:, 0:P].rearrange("p (e r) -> p e r", e=LE),
                                  lw[j][:].unsqueeze(2).broadcast_to([P, LE, LR]), ALU.mult).then_inc(sm["f_hw"], 1)

            def f_htl(n, j):
                dve.wait_ge(sm["f_hth"], n + 1)
                dve.tensor_tensor(htl[j][:], bank[6][:, 0:P], hth[j][:].bitcast(F32), ALU.subtract).then_inc(sm["f_htl"], 1)

            def f_final(n, j):
                dve.wait_ge(sm["f_fin"], n + 1)
                dve.wait_ge(sm["cpre"], n + 1)
                if holds(n, 2):
                    dve.wait_ge(sm[f"out_d{j}"], 16 * (n // 2))
                dve.scalar_tensor_tensor(fo[j][:], bank[2 + j][:], tg[:, 3:4],
                                         X[:, bass.ds(n, 1), :].rearrange("p a d -> p (a d)"), ALU.mult, ALU.add)\
                    .then_inc(sm["f_out"], 1)

            def lora_dve(n, j):
                if below(n, NT - 2):
                    x4n(n + 2, j)
                if below(n, NT - 1):
                    f_lo(n + 1, 1 - j)
                if holds(n, 2):
                    f_final(n - 2, j)
                if holds(n, 1) and below(n, NT + 1):
                    f_htl(n - 1, 1 - j)
                if below(n, NT):
                    f_route(n, j)

            x4n(0, 0)
            x4n(1, 1)
            f_lo(0, 0)
            for n in range(2):
                lora_dve(n, n)
            with dve.Fori(1, (NT - 2) // 2) as h:
                for j in range(2):
                    lora_dve(2 * h + j, j)
            for n in range(NT - 2, NT + 2):
                lora_dve(n, n % 2)

        @block.tensor
        def _(pe):
            pe.wait_ge(sm["konst"], KONST1)

            def turn(dst, src, wait_sem, count):
                for k in range(KD):
                    ins = pe.transpose(dst[:, k * P:(k + 1) * P], src[:, k * P:(k + 1) * P], ident[:])
                ins.then_inc(sm[wait_sem], 1)

            def stage1a(s):
                for i in range(4):
                    t = 4 * s + i
                    pe.wait_ge(sm["xn_ready"], t + 1)
                    if holds(t, 2):
                        pe.wait_ge(sm["xnT_ready"], t - 1)
                    turn(bank[2 + i % 2], xn[i % 2], "tx_done", t)
                pe.wait_ge(sm["xnT_ready"], 4 * s + 4)
                pe.wait_ge(sm["ctx_in"], 16 * s + 16)
                for q in range(6):
                    if q >= 2 or holds(s, 1):
                        pe.wait_ge(sm["proj_out"], 6 * s + q - 1)
                    for k in range(KD):
                        w = wq[:, k, q, :] if q < 4 else wkv[:, k, q - 4, :]
                        x = xnT[:, k, :] if q < 4 else ctxT[:, k, bass.ds(s * 512, 512)]
                        ins = pe.matmul(bank[q % 2][:], w, x, start=(k == 0), stop=(k == KD - 1))
                    ins.then_inc(sm["proj_done"], 1)

            pe.wait_ge(sm["watt_in"], 32)
            stage1a(0)
            with pe.Fori(1, 4) as s:
                stage1a(s)

            pe.wait_ge(sm["proj_out"], 24)
            pe.wait_ge(sm["watt_in"], 64)

            def scores(u, i):
                j = i % 2
                pe.wait_ge(sm["b_ready"], 3 * (u // 2) + 3)
                if holds(u, 2):
                    pe.wait_ge(sm["dif_ready"], u - 1)
                g, jb = 2 * (i % 2), i // 2 % 2
                pe.matmul(bank[j][:], qTb[jb][:, g:g + 2, :].rearrange("p g q -> p (g q)"),
                          kblk[jb][:].rearrange("p h k -> p (h k)"), start=True, stop=True).then_inc(sm["s_ready"], 1)

            def prob_turn(u, j):
                pe.wait_ge(sm["exp_done"], u + 1)
                if holds(u, 2):
                    pe.wait_ge(sm["ptc_done"], u - 1)
                turn(bank[2 + j], prob[j], "pt_done", u)

            def values(b, j):
                if holds(b, 1):
                    pe.wait_ge(sm["v_ready"], 2 * b)
                pe.wait_ge(sm["b_ready"], 3 * b + 3)
                pe.transpose(bank[5][:, 0:P], vTb[j][:].rearrange("p a k -> p (a k)"), ident[:]).then_inc(sm["v_done"], 1)

            def weigh(u, i):
                j = i % 2
                pe.wait_ge(sm["ptc_done"], u + 1)
                pe.wait_ge(sm["v_ready"], 2 * (u // 2) + 2)
                if holds(u, 1):
                    pe.wait_ge(sm["yn_ready"], u)
                for a in range(4):
                    ins = pe.matmul(bank[6][:, 34 * a:34 * a + 34], probT[j][:, a, :],
                                    vblk[i // 2 % 2][:, a, :], start=True, stop=True)
                ins.then_inc(sm["pv_done"], 1)

            def y_turn(u, j):
                pe.wait_ge(sm["yn_ready"], u + 1)
                if holds(u, 1):
                    pe.wait_ge(sm["ytc_done"], u)
                pe.transpose(bank[7][:, 0:P], yn[j][:].rearrange("p a h d -> p (a h d)"), ident[:])\
                    .then_inc(sm["yt_done"], 1)

            def project(t):
                pe.wait_ge(sm["ytc_done"], 4 * t + 4)
                if holds(t, 1):
                    pe.wait_ge(sm["x1_done"], t)
                for g in range(NG):
                    ins = pe.matmul(bank[4][:], yT[:, g, :], wo[:, g, :], start=(g == 0), stop=(g == NG - 1))
                ins.then_inc(sm["wo_done"], 1)

            def att_pe(u, i, t):
                if below(u, 2 * B):
                    prob_turn(u, i % 2)
                if i % 2 == 1 and below(u, 2 * B - 1):
                    values((u + 1) // 2, (i + 1) // 2 % 2)
                if holds(u, 1) and below(u, 2 * B + 1):
                    weigh(u - 1, (i - 1) % 4)
                if holds(u, 2) and below(u, 2 * B + 2):
                    y_turn(u - 2, i % 2)
                if below(u, 2 * B - 2):
                    scores(u + 2, (i + 2) % 4)
                if i == 2 and holds(u, 4):
                    project(t - 1)

            scores(0, 0)
            scores(1, 1)
            values(0, 0)
            for i in range(4):
                att_pe(i, i, 0)
            with pe.Fori(1, NT - 1) as t:
                for i in range(4):
                    att_pe(4 * t + i, i, t)
            for u in range(2 * B - 4, 2 * B + 2):
                att_pe(u, u % 4, u // 4)
            project(NT - 1)

            def parts(hi_, lo_):
                return (lambda k: hi_[:, k, :]), (lambda k: lo_[:, k, :])

            def gate_up(p, n, j, at, first):
                if first:
                    pe.wait_ge(sm[p + "lo"], n + 1)
                    if holds(n, 2):
                        pe.wait_ge(sm[p + "z"], n - 1)
                w = [(lambda k, m=m: m[:, at, k * D:(k + 1) * D]) for m in (wh, wl)]
                ins = split3(pe, bank[2 + j][:], parts(xh[j], xl[j]), w, (0, 1) if first else (2, 3), first, not first)
                if not first:
                    ins.then_inc(sm[p + "gu"], 1)

            def z_turn(p, n, j):
                pe.wait_ge(sm[p + "z"], n + 1)
                if holds(n, 1):
                    pe.wait_ge(sm[p + "zl"], n)
                for k in range(2):
                    ins = pe.transpose(bank[4][:, k * P:(k + 1) * P], zz[j][:, k * P:(k + 1) * P], ident[:])
                ins.then_inc(sm[p + "zt"], 1)

            def down(p, n, j, at, freed):
                pe.wait_ge(sm[p + "zl"], n + 1)
                if holds(n, 2):
                    pe.wait_ge(sm[freed], n - 1)
                w = [(lambda k, m=m: m[:, at, WGU + k * D:WGU + (k + 1) * D]) for m in (wh, wl)]
                split3(pe, bank[5 + j][:], parts(zh[j], zl[j]), w, (0, 1), True, True).then_inc(sm[p + "y"], 1)

            def logits(n, j):
                if holds(n, 1):
                    pe.wait_ge(sm["a_rtc"], n)
                split3(pe, bank[7][:, 0:E], parts(xh[j], xl[j]), parts(gwh, gwl), range(KD), True, True)\
                    .then_inc(sm["a_rt"], 1)

            def x_turn(n, j):
                pe.wait_ge(sm["n2"], n + 1)
                if holds(n, 2):
                    pe.wait_ge(sm["a_lo"], n - 1)
                turn(bank[j], xn[j], "a_tx", n)

            def shared_pe(n, j):
                if below(n, NT - 1):
                    x_turn(n + 1, 1 - j)
                if below(n, NT):
                    gate_up("a_", n, j, 2, True)
                if holds(n, 1) and below(n, NT + 1):
                    z_turn("a_", n - 1, 1 - j)
                if below(n, NT):
                    gate_up("a_", n, j, 2, False)
                    logits(n, j)
                if holds(n, 1) and below(n, NT + 1):
                    down("a_", n - 1, 1 - j, 2, "a_x")

            x_turn(0, 0)
            pe.wait_ge(sm["w_split"], 1)
            pe.wait_ge(sm["sum_step"], 3)
            for n in range(2):
                shared_pe(n, n)
            with pe.Fori(1, (NT - 2) // 2) as h:
                for j in range(2):
                    shared_pe(2 * h + j, j)
            for n in range(NT - 2, NT + 1):
                shared_pe(n, n % 2)

            pe.wait_ge(sm["sel_ready"], 1)
            pe.matmul(bank[0][:, 0:NT * E], lower[:], sel[:].rearrange("p t e -> p (t e)"), start=True, stop=True)
            pe.matmul(bank[1][:, 0:NT * E], onesm[:], sel[:].rearrange("p t e -> p (t e)"), start=True, stop=True)\
                .then_inc(sm["rmm"], 1)

            def g_turn(n, j):
                pe.wait_ge(sm[f"g_in{j}"], 16 * (n // 2) + 16)
                if holds(n, 2):
                    pe.wait_ge(sm["u_lo"], n - 1)
                turn(bank[j], xn[j], "u_tx", n)

            def unit_pe(n, j):
                if below(n, NU - 1):
                    g_turn(n + 1, 1 - j)
                if below(n, NU):
                    e = pe.value_load(uexp[0:1, bass.ds(n, 1)], min_val=0, max_val=E - 1)
                    at = pe.value_load(upar[0:1, bass.ds(n, 1)], min_val=0, max_val=2)
                    pe.wait_ge(sm["w_split"], e + 2)
                    gate_up("u_", n, j, at, True)
                if holds(n, 1) and below(n, NU + 1):
                    z_turn("u_", n - 1, 1 - j)
                if below(n, NU):
                    gate_up("u_", n, j, at, False)
                if holds(n, 1) and below(n, NU + 1):
                    at1 = pe.value_load(upar[0:1, bass.ds(n - 1, 1)], min_val=0, max_val=2)
                    down("u_", n - 1, 1 - j, at1, "u_yo")

            pe.wait_ge(sm["utab"], 1)
            g_turn(0, 0)
            for n in range(2):
                unit_pe(n, n)
            with pe.Fori(1, (NU - 2) // 2) as h:
                for j in range(2):
                    unit_pe(2 * h + j, j)
            for n in range(NU - 2, NU + 1):
                unit_pe(n, n % 2)

            def x3_turn(t, j):
                pe.wait_ge(sm["l3"], t + 1)
                if holds(t, 2):
                    pe.wait_ge(sm["x3_done"], t - 1)
                turn(bank[j], xn[j], "t_done", t)

            for t in range(2):
                x3_turn(t, t)
            with pe.Fori(1, NT // 2) as h:
                for j in range(2):
                    x3_turn(2 * h + j, j)
            pe.wait_ge(sm["as3"], 1)
            for ko in range(KD):
                terms = [(ch, ki) for ki in range(max(0, ko - 1), min(KD, ko + 2)) for ch in range(2)]
                for n, (ch, ki) in enumerate(terms):
                    off = P + P * (ko - ki)
                    ins = pe.matmul(bank[4][:, ko * 64:(ko + 1) * 64], band[:, ch, off:off + P],
                                    maps[:, ch, ki].rearrange("p r b -> p (r b)"),
                                    start=(n == 0), stop=(n == len(terms) - 1))
            ins.then_inc(sm["bn_mm"], 1)
            for step in (2, 7):
                pe.wait_ge(sm["bn_step"], step)
                pe.matmul(bank[5][:, 0:2], ones3[:], part[:], start=True, stop=True).then_inc(sm["bn_mm"], 1)

            def y3_turn(t, j):
                pe.wait_ge(sm["y3"], 3 * t + 3)
                if holds(t, 2):
                    pe.wait_ge(sm["x3_sum"], t - 1)
                turn(bank[2 + j], asel[j][:].rearrange("p k n -> p (k n)"), "y3t", t)

            for t in range(2):
                y3_turn(t, t)
            with pe.Fori(1, NT // 2) as h:
                for j in range(2):
                    y3_turn(2 * h + j, j)

            pe.wait_ge(sm["w4_split"], 6)

            def f_turn(n, j):
                pe.wait_ge(sm["l4"], n + 1)
                if holds(n, 2):
                    pe.wait_ge(sm["f_lo"], n - 1)
                turn(bank[j], xn[j], "f_tx", n)

            def f_low(n, j):
                pe.wait_ge(sm["f_lo"], n + 1)
                if holds(n, 2):
                    pe.wait_ge(sm["f_hw"], n - 1)
                split3(pe, bank[4 + j][:, 0:136], parts(fh[j], fl[j]), parts(*aws), range(KD), True, True)\
                    .then_inc(sm["f_h"], 1)

            def f_hw_turn(n, j):
                pe.wait_ge(sm["f_hw"], n + 1)
                if holds(n, 1):
                    pe.wait_ge(sm["f_htl"], n)
                pe.transpose(bank[6][:, 0:P], hw[j][:], ident[:]).then_inc(sm["f_ht"], 1)

            def f_base(n, j):
                if holds(n, 2):
                    pe.wait_ge(sm["f_out"], n - 1)
                split3(pe, bank[2 + j][:], parts(fh[j], fl[j]), parts(*wbs), range(KD), True, False)\
                    .then_inc(sm["f_base"], 1)

            def f_up(n, j):
                pe.wait_ge(sm["f_htl"], n + 1)
                split3(pe, bank[2 + j][:], (lambda k: hth[j][:], lambda k: htl[j][:]),
                       (lambda k: bms[0][:], lambda k: bms[1][:]), (0,), False, True).then_inc(sm["f_fin"], 1)

            def lora_pe(n, j):
                if below(n, NT - 1):
                    f_turn(n + 1, 1 - j)
                if below(n, NT):
                    f_low(n, j)
                if holds(n, 1) and below(n, NT + 1):
                    f_hw_turn(n - 1, 1 - j)
                if below(n, NT):
                    f_base(n, j)
                if holds(n, 1) and below(n, NT + 1):
                    f_up(n - 1, 1 - j)

            f_turn(0, 0)
            for n in range(2):
                lora_pe(n, n)
            with pe.Fori(1, (NT - 2) // 2) as h:
                for j in range(2):
                    lora_pe(2 * h + j, j)
            for n in range(NT - 2, NT + 1):
                lora_pe(n, n % 2)



def kernel(**inputs):
    import numpy as np
    import concourse.bacc as bacc
    from concourse.bass_utils import run_bass_kernel_spmd

    a = {k: np.asarray(v) for k, v in inputs.items()}
    rows = [a["g_xattn"], a["g_ffn"], a["L0_ffn_bias"], a["L1_xattn_conv_w"].reshape(14),
            a["L1_xattn_bn_gamma"], a["L1_xattn_bn_beta"]]
    head = a["L0_xattn_bq"].reshape(NKV, NG, HD).transpose(0, 2, 1).reshape(P, NG)
    cols = [head, a["L0_xattn_bk"][:, None], a["L0_xattn_bv"][:, None]]
    cst = np.concatenate([np.broadcast_to(np.concatenate(rows), (P, C_BQ))] + cols, axis=1)

    def pieces(w):
        e, k, n = w.shape
        return w.reshape(e, k // P, P, n).transpose(0, 2, 1, 3).reshape(e, P, -1)

    wg = np.concatenate([a["L0_ffn_Wg"], a["L0_ffn_Sg"][None]]).transpose(0, 2, 1)
    wu = np.concatenate([a["L0_ffn_Wu"], a["L0_ffn_Su"][None]]).transpose(0, 2, 1)
    wd = np.concatenate([a["L0_ffn_Wd"], a["L0_ffn_Sd"][None]]).transpose(0, 2, 1)
    arrays = {
        "x": a["x"].reshape(T, D),
        "ctxT": a["ctx_4096"].reshape(T, D).T,
        "cst": cst,
        "wq": a["L0_xattn_Wq"].reshape(D, NKV, NG, HD).transpose(0, 2, 1, 3).reshape(D, D),
        "wkv": np.concatenate([a["L0_xattn_Wk"], a["L0_xattn_Wv"]], axis=1),
        "wo": a["L0_xattn_Wo"].reshape(NKV, NG, HD, D).transpose(1, 0, 2, 3).reshape(NG, P, D),
        "bo": np.broadcast_to(a["L0_xattn_bo"], (P, D)),
        "gate": a["L0_ffn_gate_w"].T,
        "wall": np.concatenate([pieces(np.concatenate([wg, wu], axis=2)), pieces(wd)], axis=2),
        "wb": a["L1_ffn_Wb"].T,
        "aw": np.concatenate([a["L1_ffn_A"].reshape(LE * LR, D), a["L1_ffn_Wr"]]).T,
        "bm": a["L1_ffn_Bm"].transpose(0, 2, 1).reshape(LE * LR, D),
        "b1": np.broadcast_to(a["L1_ffn_bias"], (P, D)),
    }
    nc = bacc.Bacc("TRN2", target_bir_lowering=False, num_devices=1)
    arrays = {f"in_{k}": np.ascontiguousarray(v) for k, v in arrays.items()}
    io = [nc.dram_tensor(k, v.shape, mybir.dt.from_np(v.dtype), kind="ExternalInput").ap() for k, v in arrays.items()]
    io.append(nc.dram_tensor("out_0", (T, D), F32, kind="ExternalOutput").ap())
    block_program(nc, io)
    r = run_bass_kernel_spmd(nc, [arrays], core_ids=[0])
    return r.results[0]["out_0"].reshape(B, S, D)
```

```python
from contextlib import ExitStack

import concourse.bass as bass
from concourse import mybir

F32 = mybir.dt.float32
F32R = mybir.dt.float32r
I32 = mybir.dt.int32
ALU = mybir.AluOpType
ACT = mybir.ActivationFunctionType
AX = mybir.AxisListType.X

P = 128
B, S, D = 32, 64, 512
T = B * S
NT = T // P
KD = D // P
NKV, NG, HD = 8, 4, 16
E, I, TOPK = 16, 256, 4
WGU = KD * 2 * I
WALL = WGU + (I // P) * D
NU = T * TOPK // P + E
NSEL = 38
NSUB = S - NSEL
NF = 11
KONST1, KONST2 = 14, 25
LE, LR = 8, 16
EPS = 1e-5
BIG = 3.0e38

C_GATE, C_RB, C_CONV, C_BN, C_BQ, C_BK, C_BV = 0, 4, 20, 34, 36, 40, 41
C_ALL = 42


def holds(n, least):
    return n >= least if isinstance(n, int) else True


def below(n, limit):
    return n < limit if isinstance(n, int) else True


def block_program(nc, io):
    (x_in, ctxT_in, cst_in, wq_in, wkv_in, wo_in, bo_in, gate_in, wall_in,
     wb_in, aw_in, bm_in, b1_in, out) = io
    with ExitStack() as ctx:
        def sb(name, shape, dt=F32, stack=ctx):
            return stack.enter_context(nc.sbuf_tensor(name, shape, dt))

        def sem(name):
            return ctx.enter_context(nc.semaphore(name))

        bank = [ctx.enter_context(nc.psum_tensor(f"bank{i}", [P, 512], F32)) for i in range(8)]

        X = sb("X", [P, NT, D])
        ctxT = sb("ctxT", [P, KD, T])
        cst = sb("cst", [P, C_ALL])
        tg = sb("tg", [P, 4])
        eps = sb("eps", [P, 1])
        ident = sb("ident", [P, P])
        stats = sb("stats", [P, NT, 6])
        mu = sb("mu", [P, NT])
        va = sb("va", [P, NT])
        dm = sb("dm", [P, NT])
        sd = sb("sd", [P, NT])
        rs = sb("rs", [P, NT])
        xn = [sb(f"xn{j}", [P, D]) for j in range(2)]

        neg = sb("neg", [P, 8, S])
        best = sb("best", [P, 8, 8])
        band = sb("band", [P, 2, 384])

        with ExitStack() as s1:
            sb("wraw_kept", [P, WALL], F32, s1)
            QT = sb("QT", [P, NG, T], F32, s1)
            KT = sb("KT", [P, T], F32, s1)
            VT = sb("VT", [P, T], F32, s1)
            xnT = sb("xnT", [P, KD, 512], F32, s1)
            wq = sb("wq", [P, KD, NG, P], F32, s1)
            wkv = sb("wkv", [P, KD, 2, P], F32, s1)
            wo = sb("wo", [P, NG, D], F32, s1)
            bo = sb("bo", [P, D], F32, s1)
            hmask = sb("hmask", [P, NKV], F32, s1)
            wide = sb("wide", [P, 390], F32, s1)
            qTb = [sb(f"qTb{j}", [P, NG, S], F32, s1) for j in range(2)]
            kblk = [sb(f"kblk{j}", [P, NKV, S], F32, s1) for j in range(2)]
            vTb = [sb(f"vTb{j}", [P, 2, S], F32, s1) for j in range(2)]
            vblk = [sb(f"vblk{j}", [P, 4, 34], F32, s1) for j in range(2)]
            mx = [sb(f"mx{j}", [P, NKV], F32, s1) for j in range(2)]
            dif = [sb(f"dif{j}", [P, NKV, S], F32, s1) for j in range(2)]
            prob = [sb(f"prob{j}", [P, NKV * S], F32, s1) for j in range(2)]
            probT = [sb(f"probT{j}", [P, 4, P], F32, s1) for j in range(2)]
            rec = [sb(f"rec{j}", [P, 4, 2], F32, s1) for j in range(2)]
            yn = [sb(f"yn{j}", [P, 4, 2, HD], F32, s1) for j in range(2)]
            yT = sb("yT", [P, NG, P], F32, s1)

        with ExitStack() as sr:
            sb("wraw_kept2", [P, WALL], F32, sr)
            lg = sb("lg", [P, NT, E], F32, sr)
            sc = sb("sc", [P, NT, 24], F32, sr)
            scr = sb("scr", [P, NT, 24], F32, sr)
            v8 = sb("v8", [P, NT, 8], F32, sr)
            wsum = sb("wsum", [P, NT], F32, sr)
            wrec = sb("wrec", [P, NT], F32, sr)
            sel = sb("sel", [P, NT, E], F32, sr)
            pre = sb("pre", [P, NT + 1, E], F32, sr)
            slot = sb("slot", [P, NT, E], F32, sr)
            eq = sb("eq", [P, NT, E], F32, sr)
            k8 = sb("k8", [P, NT, 8], F32, sr)
            ucnt = sb("ucnt", [P, E], I32, sr)
            ushf = sb("ushf", [P, E], I32, sr)
            unum = sb("unum", [P, E], F32, sr)
            uend = sb("uend", [P, E], F32, sr)
            ubase = sb("ubase", [P, E], F32, sr)
            ones16 = sb("ones16", [P, E], F32, sr)
            uiota = sb("uiota", [1, NU], F32, sr)
            ueid = sb("ueid", [1, NU + 1], F32, sr)
            lower = sb("lower", [P, P], F32, sr)
            onesm = sb("onesm", [P, P], F32, sr)

        with ExitStack() as s2:
            wraw = sb("wraw", [P, 2, WALL], F32, s2)
            wh = sb("wh", [P, 3, WALL], F32R, s2)
            wl = sb("wl", [P, 3, WALL], F32R, s2)
            gw = sb("gw", [P, KD, E], F32, s2)
            gwh = sb("gwh", [P, KD, E], F32R, s2)
            gwl = sb("gwl", [P, KD, E], F32R, s2)
            xh = [sb(f"xh{j}", [P, KD, P], F32R, s2) for j in range(2)]
            xl = [sb(f"xl{j}", [P, KD, P], F32R, s2) for j in range(2)]
            sg = [sb(f"sg{j}", [P, I], F32, s2) for j in range(2)]
            zz = [sb(f"zz{j}", [P, I], F32, s2) for j in range(2)]
            zh = [sb(f"zh{j}", [P, 2, P], F32R, s2) for j in range(2)]
            zl = [sb(f"zl{j}", [P, 2, P], F32R, s2) for j in range(2)]
            yo = [sb(f"yo{j}", [P, D], F32, s2) for j in range(2)]
            tix = sb("tix", [P, NT, TOPK], I32, s2)
            tiy = sb("tiy", [P, NT, TOPK], I32, s2)
            wk = sb("wk", [P, NT, TOPK], F32, s2)
            sidx = sb("sidx", [P, NT, TOPK], I32, s2)
            tok = sb("tok", [P, NT], I32, s2)
            tw = sb("tw", [P, NT, TOPK, 2], I32, s2)
            ids = sb("ids", [P, NU, 2], I32, s2)
            zero = sb("zero", [P, D], F32, s2)
            gidx = [sb(f"gidx{j}", [P, 1], I32, s2) for j in range(2)]
            aidx = [sb(f"aidx{j}", [P, 1], I32, s2) for j in range(2)]
            ule = sb("ule", [1, NU, E], F32, s2)
            upar = sb("upar", [1, NU], I32, s2)
            uexp = sb("uexp", [1, NU + 1], I32, s2)
            unext = sb("unext", [1, NU], I32, s2)

        with ExitStack() as s3:
            x3T = sb("x3T", [P, KD, T], F32, s3)
            cf = [sb(f"cf{j}", [P, KD, P], F32, s3) for j in range(2)]
            sf = [sb(f"sf{j}", [P, KD, P], F32, s3) for j in range(2)]
            maps = sb("maps", [P, 2, KD, 2, B], F32, s3)
            bsel = sb("bsel", [P, 2], F32, s3)
            tot = sb("tot", [P, KD, B], F32, s3)
            ones3 = sb("ones3", [P, P], F32, s3)
            zc = sb("zc", [P, 2, KD, B], F32, s3)
            zq = sb("zq", [P, 2, KD, B], F32, s3)
            part = sb("part", [P, 2], F32, s3)
            mean = sb("mean", [P, 2], F32, s3)
            var = sb("var", [P, 2], F32, s3)
            gain = sb("gain", [P, 2], F32, s3)
            amap = sb("amap", [P, 2, KD, B], F32, s3)
            asel = [sb(f"asel{j}", [P, KD, P], F32, s3) for j in range(2)]
            wb = sb("wb", [P, KD, D], F32, s3)
            aw = sb("aw", [P, KD, 136], F32, s3)
            bm = sb("bm", [P, D], F32, s3)
            b1 = sb("b1", [P, D], F32, s3)
            wbs = [sb(f"wbs{i}", [P, KD, D], F32R, s3) for i in range(2)]
            aws = [sb(f"aws{i}", [P, KD, 136], F32R, s3) for i in range(2)]
            bms = [sb(f"bms{i}", [P, D], F32R, s3) for i in range(2)]
            fh = [sb(f"fh{j}", [P, KD, P], F32R, s3) for j in range(2)]
            fl = [sb(f"fl{j}", [P, KD, P], F32R, s3) for j in range(2)]
            pr = [sb(f"pr{j}", [P, 16], F32, s3) for j in range(2)]
            prr = [sb(f"prr{j}", [P, 16], F32, s3) for j in range(2)]
            m8 = [sb(f"m8{j}", [P, 8], F32, s3) for j in range(2)]
            nm = [sb(f"nm{j}", [P, 8], F32, s3) for j in range(2)]
            lw = [sb(f"lw{j}", [P, LE], F32, s3) for j in range(2)]
            hw = [sb(f"hw{j}", [P, P], F32, s3) for j in range(2)]
            hth = [sb(f"hth{j}", [P, P], F32R, s3) for j in range(2)]
            htl = [sb(f"htl{j}", [P, P], F32R, s3) for j in range(2)]
            fo = [sb(f"fo{j}", [P, D], F32, s3) for j in range(2)]

        xn_d = nc.dram_tensor("xn_d", (T + P, D), F32, kind="Internal").ap()
        acc_d = nc.dram_tensor("acc_d", (T + P, D), F32, kind="Internal").ap()
        tab_d = nc.dram_tensor("tab_d", (NU * P, 2), I32, kind="Internal").ap()

        names = """cst_in x_in ctx_in watt_in gw_in wraw_in w4_in konst gates
            lnstat lnvar lnsd lnrs
            xn_ready tx_done xnT_ready proj_done proj_out
            b_ready s_ready mx_ready dif_ready exp_done pt_done ptc_done pv_done rec_ready yn_ready
            yt_done ytc_done wo_done x1_done v_done v_ready
            w_split w_hi p_hi p_split n2 store_in0 store_in1 load_in0 load_in1 acc_out0 acc_out1 r_tx r_hi r_lo
            a_tx a_hi a_lo a_rt a_rtc a_gu a_sg a_z a_zt a_zh a_zl a_y a_x
            rsig rstep rmm tables scat tab0 ids_in pad_in
            g_in0 g_in1 gid aid u_tx u_hi u_lo u_gu u_sg u_z u_zt u_zh u_zl u_y u_yo add_out0 add_out1
            tstep xload cpre tot_ps tot_sb
            l3 t_done x3_done d3 c3 m3 r3 mstep carried sel_ready utab sum_step bn_step bn_mm bn_act cstep y3p y3 y3t x3_sum
            konst3 w4_split l4 f_tx f_hi f_lo f_h f_base f_step f_exp f_hw f_ht f_hth f_htl f_out f_fin out_d0 out_d1 x4b""".split()
        sm = {n: sem(n) for n in names}

        block = ctx.enter_context(nc.Block())

        def carry(eng):
            eng.sem_inc(sm["carried"], 1)

        def split3(eng, dst, a, b, k_list, first, last):
            n, m = 0, 3 * len(k_list)
            for k in k_list:
                for ia, ib in ((0, 0), (0, 1), (1, 0)):
                    ins = eng.matmul(dst, a[ia](k), b[ib](k), start=(first and n == 0), stop=(last and n == m - 1),
                                     skip_group_check=True)
                    n += 1
            return ins

        @block.sync
        def _(sp):
            sp.dma_start(cst[:], cst_in).then_inc(sm["cst_in"], 16)
            x_v = x_in.rearrange("(t p) d -> p t d", p=P)
            c_v = ctxT_in.rearrange("(k p) n -> p k n", p=P)
            sp.dma_start(X[:, 0:4, :], x_v[:, 0:4, :]).then_inc(sm["x_in"], 16)
            sp.dma_start(wq[:].rearrange("p k g m -> p k (g m)"), wq_in.rearrange("(k p) n -> p k n", p=P)).then_inc(sm["watt_in"], 16)
            sp.dma_start(wkv[:].rearrange("p k g m -> p k (g m)"), wkv_in.rearrange("(k p) n -> p k n", p=P)).then_inc(sm["watt_in"], 16)
            sp.dma_start(ctxT[:, :, 0:512], c_v[:, :, 0:512]).then_inc(sm["ctx_in"], 16)
            sp.wait_ge(sm["x_in"], 16)
            for q in range(1, 4):
                sp.wait_ge(sm["x_in"], 16 * q)
                sp.dma_start(X[:, 4 * q:4 * q + 4, :], x_v[:, 4 * q:4 * q + 4, :]).then_inc(sm["x_in"], 16)
                sp.wait_ge(sm["ctx_in"], 16 * q)
                sp.dma_start(ctxT[:, :, 512 * q:512 * q + 512], c_v[:, :, 512 * q:512 * q + 512]).then_inc(sm["ctx_in"], 16)
            sp.wait_ge(sm["watt_in"], 32)
            sp.dma_start(wo[:], wo_in.rearrange("g p n -> p g n")).then_inc(sm["watt_in"], 16)
            sp.dma_start(bo[:], bo_in).then_inc(sm["watt_in"], 16)
            sp.dma_start(wraw[:, 0], wall_in[E]).then_inc(sm["wraw_in"], 16)
            sp.wait_ge(sm["x1_done"], NT)
            sp.dma_start(gw[:], gate_in.rearrange("(k p) n -> p k n", p=P)).then_inc(sm["gw_in"], 16)
            sp.wait_ge(sm["w_split"], 1)
            sp.dma_start(wraw[:, 0], wall_in[0]).then_inc(sm["wraw_in"], 16)

            def store(n, j):
                sp.wait_ge(sm["n2"], n + 1)
                sp.dma_start(xn_d[bass.ds(n * P, P), :], xn[j][:]).then_inc(sm[f"store_in{j}"], 16)

            with sp.Fori(0, NT // 2) as h:
                for j in range(2):
                    store(2 * h + j, j)

            for j in range(2):
                sp.wait_ge(sm[f"store_in{j}"], 16 * (NT // 2))
            sp.wait_ge(sm["r_tx"], NT)

            def load(n, j):
                if holds(n, 2):
                    sp.wait_ge(sm["a_tx"], n - 1)
                sp.dma_start(xn[j][:], xn_d[bass.ds(n * P, P), :]).then_inc(sm[f"load_in{j}"], 16)

            def store_acc(n, j):
                sp.wait_ge(sm["a_x"], n + 1)
                sp.dma_start(acc_d[bass.ds(n * P, P), :], X[:, bass.ds(n, 1), :].rearrange("p a d -> p (a d)"))\
                    .then_inc(sm[f"acc_out{j}"], 16)

            def load_weights(f):
                sp.wait_ge(sm["wraw_in"], 16 * f + 16)
                src = wall_in[f] if isinstance(f, int) else wall_in[bass.ds(f, 1)].rearrange("a p n -> p (a n)")
                return sp.dma_start(wraw[:, f % 2] if isinstance(f, int) else
                                    wraw[:, bass.ds(f % 2, 1), :].rearrange("p a n -> p (a n)"), src)\
                    .then_inc(sm["wraw_in"], 16)

            for n in range(2):
                load(n, n)
            sp.wait_ge(sm["utab"], 1)
            load_weights(1)
            for n in range(2, 4):
                load(n, n % 2)
            with sp.Fori(2, NT // 2) as h:
                for j in range(2):
                    load(2 * h + j, j)
                    store_acc(2 * h + j - 4, j)
            sp.wait_ge(sm["p_split"], 1)
            load_weights(2)
            for n in range(NT - 4, NT):
                store_acc(n, n % 2)
            sp.wait_ge(sm["p_split"], 2)
            load_weights(3)
            with sp.Fori(4, E) as f:
                sp.wait_ge(sm["w_split"], f - 1)
                load_weights(f)
            for j in range(2):
                sp.wait_ge(sm[f"add_out{j}"], 16 * (NU // 2))
            a_v = acc_d[0:T, :].rearrange("(t p) d -> p t d", p=P)
            for q in range(4):
                if q:
                    sp.wait_ge(sm["xload"], 16 * q)
                sp.dma_start(X[:, 4 * q:4 * q + 4, :], a_v[:, 4 * q:4 * q + 4, :]).then_inc(sm["xload"], 16)
            sp.dma_start(wb[:], wb_in.rearrange("(k p) n -> p k n", p=P)).then_inc(sm["w4_in"], 16)
            sp.dma_start(aw[:], aw_in.rearrange("(k p) n -> p k n", p=P)).then_inc(sm["w4_in"], 16)
            sp.dma_start(bm[:], bm_in).then_inc(sm["w4_in"], 16)
            sp.dma_start(b1[:], b1_in).then_inc(sm["w4_in"], 16)

            def store_out(n, j):
                sp.wait_ge(sm["f_out"], n + 1)
                sp.dma_start(out[bass.ds(n * P, P), :], fo[j][:]).then_inc(sm[f"out_d{j}"], 16)

            with sp.Fori(0, NT // 2) as h:
                for j in range(2):
                    store_out(2 * h + j, j)
            for j in range(2):
                sp.wait_ge(sm[f"out_d{j}"], 16 * (NT // 2))

        @block.gpsimd
        def _(pool):
            kc = [0]

            def k0(ins):
                kc[0] += 1
                ins.then_inc(sm["konst"], 1)
                pool.wait_ge(sm["konst"], kc[0])

            k0(pool.memset(ident[:], 0.0))
            k0(pool.memset(eps[:], EPS))
            k0(pool.memset(wide[:], 0.0))
            k0(pool.affine_select(wide[:], wide[:], [[-1, 390]], ALU.not_equal, 1.0, base=P + 3, channel_multiplier=1))
            k0(pool.memset(hmask[:], 1.0))
            for j in range(2):
                k0(pool.memset(vblk[j][:], 0.0))
            k0(pool.affine_select(ident[:], ident[:], [[-1, P]], ALU.not_equal, 1.0, base=0, channel_multiplier=1))
            k0(pool.affine_select(hmask[:], hmask[:], [[-HD, NKV]], ALU.is_ge, 0.0, base=0, channel_multiplier=1))
            for j in range(2):
                k0(pool.memset(vblk[j][0:S, :, 32:33], 1.0))
                k0(pool.memset(vblk[j][S:P, :, 33:34], 1.0))
            k0(pool.affine_select(hmask[:], hmask[:], [[HD, NKV]], ALU.is_ge, 0.0, base=HD - 1, channel_multiplier=-1))
            pool.wait_ge(sm["gates"], 1)
            pool.wait_ge(sm["watt_in"], 64)
            k0(pool.tensor_scalar(bo[:], bo[:], tg[:, 0:1], None, ALU.mult))
            pool.wait_ge(sm["proj_out"], 24)

            def prepare(b, j):
                if holds(b, 2):
                    pool.wait_ge(sm["s_ready"], 2 * b - 2)
                    pool.wait_ge(sm["v_done"], b - 1)
                pool.tensor_copy(qTb[j][:], QT[:, :, bass.ds(b * S, S)]).then_inc(sm["b_ready"], 1)
                kv = KT[:, bass.ds(b * S, S)].unsqueeze(1).broadcast_to([P, NKV, S])
                pool.tensor_tensor(kblk[j][:], kv, hmask[:].unsqueeze(2).broadcast_to([P, NKV, S]),
                                   ALU.mult).then_inc(sm["b_ready"], 1)
                pool.tensor_copy(vTb[j][:], VT[:, bass.ds(b * S, S)].unsqueeze(1).broadcast_to([P, 2, S]))\
                    .then_inc(sm["b_ready"], 1)

            def add_bias(t):
                pool.tensor_tensor(X[:, bass.ds(t, 1), :], X[:, bass.ds(t, 1), :], bo[:].unsqueeze(1), ALU.add)\
                    .then_inc(sm["x4b"], 1)

            for b in range(2):
                prepare(b, b)
            add_bias(0)
            with pool.Fori(1, B // 2) as h:
                for j in range(2):
                    prepare(2 * h + j, j)
                add_bias(h)

            pool.wait_ge(sm["x1_done"], NT)
            k0(pool.memset(zero[:], 0.0))
            k0(pool.memset(ids[:], 0))
            k0(pool.iota(ids[:, :, 0], [[0, NU]], base=T, channel_multiplier=1))
            k0(pool.memset(lower[:], 1.0))
            k0(pool.memset(onesm[:], 1.0))
            k0(pool.memset(ones16[:], 1.0))
            k0(pool.iota(tok[:], [[P, NT]], base=0, channel_multiplier=1))
            k0(pool.iota(uiota[:], [[1, NU]], base=0, channel_multiplier=0, allow_small_or_imprecise_dtypes=True))
            k0(pool.memset(sc[:, :, E:24], -BIG))
            k0(pool.affine_select(lower[:], lower[:], [[1, P]], ALU.is_gt, 0.0, base=0, channel_multiplier=-1))
            pool.dma_start(tab_d.rearrange("(p u) o -> p (u o)", p=P), ids[:].rearrange("p u o -> p (u o)"))\
                .then_inc(sm["tab0"], 16)
            pool.dma_start(xn_d[T:T + P, :], zero[:]).then_inc(sm["pad_in"], 16)
            pool.dma_start(acc_d[T:T + P, :], zero[:]).then_inc(sm["pad_in"], 16)

            def pool_split(e):
                pool.wait_ge(sm["wraw_in"], 16 * (e + 2))
                pool.tensor_copy(wh[:, e, :], wraw[:, e]).then_inc(sm["p_hi"], 1)
                pool.wait_ge(sm["p_hi"], e + 1)
                pool.tensor_tensor(wl[:, e, :], wraw[:, e], wh[:, e, :].bitcast(F32), ALU.subtract)\
                    .then_inc(sm["p_split"], 1)
                pool.wait_ge(sm["p_split"], e + 1)

            pool_split(0)

            pool.wait_ge(sm["tab0"], 16)
            pool.wait_ge(sm["tables"], 1)
            for t in range(NT):
                if t == NT // 2:
                    pool_split(1)
                for k in range(TOPK):
                    pool.indirect_dma_start(tab_d, bass.IndirectOffsetOnAxis(ap=tix[:, t, k:k + 1], axis=0),
                                            tw[:, t, k, :], None).then_inc(sm["scat"], 16)
            pool.wait_ge(sm["scat"], 16 * NT * TOPK)
            pool.dma_start(ids[:].rearrange("p u o -> p (u o)"), tab_d.rearrange("(p u) o -> p (u o)", p=P))\
                .then_inc(sm["ids_in"], 16)
            pool.wait_ge(sm["ids_in"], 16)
            pool.wait_ge(sm["pad_in"], 32)
            pool.wait_ge(sm["a_tx"], NT)
            for j in range(2):
                pool.wait_ge(sm[f"acc_out{j}"], 16 * (NT // 2))

            def gather(n, j):
                if holds(n, 2):
                    pool.wait_ge(sm[f"g_in{j}"], 16 * (n // 2))
                    pool.wait_ge(sm["u_tx"], n - 1)
                pool.tensor_copy(gidx[j][:], ids[:, bass.ds(n, 1), 0]).then_inc(sm["gid"], 1)
                pool.wait_ge(sm["gid"], n + 1)
                carry(pool)
                pool.indirect_dma_start(xn[j][:], None, xn_d, bass.IndirectOffsetOnAxis(ap=gidx[j][:, 0:1], axis=0))\
                    .then_inc(sm[f"g_in{j}"], 16)

            def add_results(n, j):
                if holds(n, 2):
                    pool.wait_ge(sm[f"add_out{j}"], 16 * (n // 2))
                pool.tensor_copy(aidx[j][:], ids[:, bass.ds(n, 1), 0]).then_inc(sm["aid"], 1)
                pool.wait_ge(sm["aid"], n + 1)
                pool.wait_ge(sm["u_yo"], n + 1)
                if holds(n, 1):
                    pool.wait_ge(sm[f"add_out{1 - j}"], 16 * ((n + 1) // 2))
                carry(pool)
                pool.indirect_dma_start(acc_d, bass.IndirectOffsetOnAxis(ap=aidx[j][:, 0:1], axis=0), yo[j][:], None,
                                        compute_op=ALU.add).then_inc(sm[f"add_out{j}"], 16)

            for n in range(4):
                gather(n, n % 2)
            with pool.Fori(2, NU // 2) as h:
                for j in range(2):
                    gather(2 * h + j, j)
                    add_results(2 * h + j - 4, j)
            for n in range(NU - 4, NU):
                add_results(n, n % 2)

            for j in range(2):
                pool.wait_ge(sm[f"add_out{j}"], 16 * (NU // 2))
            kd = [0]

            def k3(ins, wait=True):
                kd[0] += 1
                ins.then_inc(sm["konst3"], 1)
                pool.wait_ge(sm["konst3"], kd[0])

            k3(pool.memset(ones3[:], 1.0))
            k3(pool.memset(bsel[:], 1.0))
            k3(pool.affine_select(bsel[:], bsel[:], [[-S, 2]], ALU.is_ge, 0.0, base=0, channel_multiplier=1))
            k3(pool.affine_select(bsel[:], bsel[:], [[S, 2]], ALU.is_ge, 0.0, base=S - 1, channel_multiplier=-1))
            k3(pool.memset(pr[0][:], -1.0))
            k3(pool.memset(pr[1][:], -1.0))

            def rest(t, j):
                pool.wait_ge(sm["c3"], t + 1)
                pool.tensor_tensor(sf[j][:], x3T[:, :, bass.ds(t * P, P)], cf[j][:], ALU.subtract).then_inc(sm["d3"], 1)

            for t in range(2):
                rest(t, t)
            with pool.Fori(1, NT // 2) as h:
                for j in range(2):
                    pool.wait_ge(sm["m3"], 2 * h + j - 1)
                    rest(2 * h + j, j)

            def blend(t, j):
                mk = ctxT[:, :, bass.ds(t * P, P)].rearrange("p k (b c) -> p k b c", c=S)
                av = asel[j][:].rearrange("p k (b c) -> p k b c", c=S)
                if holds(t, 2):
                    pool.wait_ge(sm["y3t"], t - 1)
                pool.tensor_tensor(av, mk, amap[:, 1, :, bass.ds(2 * t, 2)].unsqueeze(3).broadcast_to([P, KD, 2, S]),
                                   ALU.mult).then_inc(sm["y3p"], 1)
                pool.wait_ge(sm["y3p"], 2 * t + 1)
                pool.tensor_tensor(av, av, amap[:, 0, :, bass.ds(2 * t, 2)].unsqueeze(3).broadcast_to([P, KD, 2, S]),
                                   ALU.add).then_inc(sm["y3p"], 1)

            pool.wait_ge(sm["bn_step"], 14)
            for t in range(2):
                blend(t, t)
            with pool.Fori(1, NT // 2) as h:
                for j in range(2):
                    blend(2 * h + j, j)

            pool.wait_ge(sm["w4_in"], 64)
            for n, (raw, parts) in enumerate(((wb, wbs), (aw, aws), (bm, bms))):
                pool.tensor_copy(parts[0][:], raw[:]).then_inc(sm["w4_split"], 1)
                pool.wait_ge(sm["w4_split"], 2 * n + 1)
                pool.tensor_tensor(parts[1][:], raw[:], parts[0][:].bitcast(F32), ALU.subtract).then_inc(sm["w4_split"], 1)
                pool.wait_ge(sm["w4_split"], 2 * n + 2)
            k3(pool.tensor_scalar(b1[:], b1[:], tg[:, 3:4], None, ALU.mult))

            def add_bias4(t):
                pool.wait_ge(sm["l4"], t + 1)
                pool.tensor_tensor(X[:, bass.ds(t, 1), :], X[:, bass.ds(t, 1), :], b1[:].unsqueeze(1), ALU.add)\
                    .then_inc(sm["cpre"], 1)

            with pool.Fori(0, NT) as t:
                add_bias4(t)

        @block.scalar
        def _(act):
            act.wait_ge(sm["cst_in"], 16)
            act.activation(tg[:], cst[:, C_GATE:C_GATE + 4], ACT.Tanh).then_inc(sm["gates"], 1)

            def sqrt(lo, n, count):
                act.wait_ge(sm["lnvar"], 7 * count)
                act.activation(sd[:, bass.ds(lo, n)], va[:, bass.ds(lo, n)],
                               ACT.Sqrt, bias=eps[:, 0:1]).then_inc(sm["lnsd"], 1)

            act.wait_ge(sm["konst"], 2)

            def stage1a(s):
                sqrt(4 * s, 4, s + 1)
                for i in range(4):
                    t = 4 * s + i
                    act.wait_ge(sm["tx_done"], t + 1)
                    if i == 0 and holds(s, 1):
                        act.wait_ge(sm["proj_done"], 6 * s - 2)
                    act.copy(xnT[:, :, i * P:(i + 1) * P],
                             bank[2 + i % 2][:].rearrange("p (k n) -> p k n", k=KD)).then_inc(sm["xnT_ready"], 1)
                for q in range(6):
                    act.wait_ge(sm["proj_done"], 6 * s + q + 1)
                    if q < 4:
                        dst, bias, scale = QT[:, q, bass.ds(s * 512, 512)], cst[:, C_BQ + q:C_BQ + q + 1], 0.25
                    elif q == 4:
                        dst, bias, scale = KT[:, bass.ds(s * 512, 512)], cst[:, C_BK:C_BK + 1], 1.0
                    else:
                        dst, bias, scale = VT[:, bass.ds(s * 512, 512)], cst[:, C_BV:C_BV + 1], 1.0
                    act.activation(dst, bank[q % 2][:], ACT.Identity, bias=bias, scale=scale).then_inc(sm["proj_out"], 1)

            stage1a(0)
            with act.Fori(1, 4) as s:
                stage1a(s)

            def exps(u, j):
                act.wait_ge(sm["dif_ready"], u + 1)
                if holds(u, 2):
                    act.wait_ge(sm["pt_done"], u - 1)
                act.activation(prob[j][:], dif[j][:].rearrange("p h k -> p (h k)"), ACT.Exp).then_inc(sm["exp_done"], 1)

            def prob_out(u, j):
                act.wait_ge(sm["pt_done"], u + 1)
                if holds(u, 2):
                    act.wait_ge(sm["pv_done"], u - 1)
                act.copy(probT[j][:].rearrange("p a q -> p (a q)"), bank[2 + j][:]).then_inc(sm["ptc_done"], 1)

            def v_out(b, j):
                act.wait_ge(sm["v_done"], b + 1)
                if holds(b, 2):
                    act.wait_ge(sm["pv_done"], 2 * b - 2)
                v = bank[5][:, 0:P].rearrange("p (a h d) -> p a h d", a=4, h=2)
                act.copy(vblk[j][0:S, :, 0:HD], v[0:S, :, 0, :]).then_inc(sm["v_ready"], 1)
                act.copy(vblk[j][S:P, :, HD:2 * HD], v[S:P, :, 1, :]).then_inc(sm["v_ready"], 1)

            def yT_out(u, i):
                act.wait_ge(sm["yt_done"], u + 1)
                if i == 0 and holds(u, 4):
                    act.wait_ge(sm["wo_done"], u // 4)
                g, b = 2 * (i % 2), i // 2
                act.copy(yT[:, g:g + 2, b * S:(b + 1) * S],
                         bank[7][:, 0:P].rearrange("p (g q) -> p g q", g=2))\
                    .then_inc(sm["ytc_done"], 1)

            def att_act(u, i):
                if below(u, 2 * B - 1):
                    exps(u + 1, (i + 1) % 2)
                if below(u, 2 * B):
                    prob_out(u, i % 2)
                if i % 2 == 1 and below(u, 2 * B - 1):
                    v_out((u + 1) // 2, (i + 1) // 2 % 2)
                if holds(u, 2) and below(u, 2 * B + 2):
                    yT_out(u - 2, (i - 2) % 4)

            v_out(0, 0)
            exps(0, 0)
            for i in range(4):
                att_act(i, i)
            with act.Fori(1, NT - 1) as t:
                for i in range(4):
                    att_act(4 * t + i, i)
            for u in range(2 * B - 4, 2 * B + 2):
                att_act(u, u % 4)

            def hi(p, n, j):
                act.wait_ge(sm[p + "tx"], n + 1)
                if holds(n, 2):
                    act.wait_ge(sm[p + "gu"], n - 1)
                act.copy(xh[j][:].rearrange("p k n -> p (k n)"), bank[j][:]).then_inc(sm[p + "hi"], 1)

            def silu(p, n, j):
                act.wait_ge(sm[p + "gu"], n + 1)
                if holds(n, 2):
                    act.wait_ge(sm[p + "z"], n - 1)
                act.activation(sg[j][:], bank[2 + j][:, 0:I], ACT.Silu).then_inc(sm[p + "sg"], 1)

            def z_hi(p, n, j):
                act.wait_ge(sm[p + "zt"], n + 1)
                if holds(n, 2):
                    act.wait_ge(sm[p + "y"], n - 1)
                act.copy(zh[j][:].rearrange("p k n -> p (k n)"), bank[4][:, 0:I]).then_inc(sm[p + "zh"], 1)

            def logits_out(n):
                act.wait_ge(sm["a_rt"], n + 1)
                act.copy(lg[:, bass.ds(n, 1), :].rearrange("p a e -> p (a e)"), bank[7][:, 0:E]).then_inc(sm["a_rtc"], 1)

            def y_out(n, j):
                act.wait_ge(sm["u_y"], n + 1)
                if holds(n, 2):
                    act.wait_ge(sm[f"add_out{j}"], 16 * (n // 2))
                act.activation(yo[j][:], bank[5 + j][:], ACT.Copy,
                               scale=ids[:, bass.ds(n, 1), 1].bitcast(F32)).then_inc(sm["u_yo"], 1)

            act.wait_ge(sm["x1_done"], NT)
            act.wait_ge(sm["wraw_in"], 16)
            act.copy(wh[:, 2, :], wraw[:, 0]).then_inc(sm["w_hi"], 4)

            def route_act(n, j):
                if below(n, NT - 1):
                    r_hi(n + 1, 1 - j)
                logits_out(n)

            def r_hi(n, j):
                act.wait_ge(sm["r_tx"], n + 1)
                if holds(n, 2):
                    act.wait_ge(sm["a_rt"], n - 1)
                act.copy(xh[j][:].rearrange("p k n -> p (k n)"), bank[j][:]).then_inc(sm["r_hi"], 1)

            sqrt(0, NT, 5)
            r_hi(0, 0)
            for n in range(2):
                route_act(n, n)
            with act.Fori(1, (NT - 2) // 2) as h:
                for j in range(2):
                    route_act(2 * h + j, j)
            for n in range(NT - 2, NT):
                route_act(n, n % 2)
            act.wait_ge(sm["a_rtc"], NT)
            act.activation(sc[:, :, 0:E], lg[:], ACT.Sigmoid).then_inc(sm["rsig"], 1)

            def shared_act(n, j):
                if below(n, NT - 1):
                    hi("a_", n + 1, 1 - j)
                if holds(n, 1) and below(n, NT + 1):
                    z_hi("a_", n - 1, 1 - j)
                if below(n, NT):
                    silu("a_", n, j)

            act.wait_ge(sm["a_rt"], NT)
            hi("a_", 0, 0)
            for n in range(2):
                shared_act(n, n)
            with act.Fori(1, (NT - 2) // 2) as h:
                for j in range(2):
                    shared_act(2 * h + j, j)
            for n in range(NT - 2, NT + 1):
                shared_act(n, n % 2)

            def split_hi(nxt, half):
                with act.If(nxt > 0):
                    if half == 0:
                        act.wait_ge(sm["wraw_in"], 16 * nxt + 32)
                    cols = slice(half * WALL // 2, (half + 1) * WALL // 2)
                    act.copy(wh[:, bass.ds(nxt % 3, 1), cols].rearrange("p a n -> p (a n)"),
                             wraw[:, bass.ds(nxt % 2, 1), cols].rearrange("p a n -> p (a n)")).then_inc(sm["w_hi"], 1)

            def unit_act(n, j):
                if holds(n, 2) and below(n, NU + 2):
                    y_out(n - 2, j)
                if below(n, NU - 1):
                    hi("u_", n + 1, 1 - j)
                if holds(n, 1) and below(n, NU):
                    nxt = act.value_load(unext[0:1, bass.ds(n, 1)], min_val=0, max_val=E - 1)
                    split_hi(nxt, 0)
                if holds(n, 1) and below(n, NU + 1):
                    z_hi("u_", n - 1, 1 - j)
                if below(n, NU):
                    if holds(n, 1):
                        split_hi(nxt, 1)
                    silu("u_", n, j)

            act.wait_ge(sm["utab"], 1)
            act.wait_ge(sm["a_gu"], NT)
            act.wait_ge(sm["ids_in"], 16)
            hi("u_", 0, 0)
            for n in range(2):
                unit_act(n, n)
            with act.Fori(1, (NU - 2) // 2) as h:
                for j in range(2):
                    unit_act(2 * h + j, j)
            for n in range(NU - 2, NU + 2):
                unit_act(n, n % 2)

            for q in range(4):
                sqrt(4 * q, 4, 6 + q)

            def x3_out(t, j):
                act.wait_ge(sm["t_done"], t + 1)
                act.copy(x3T[:, :, bass.ds(t * P, P)], bank[j][:].rearrange("p (k n) -> p k n", k=KD))\
                    .then_inc(sm["x3_done"], 1)
                act.wait_ge(sm["tot_ps"], t + 1)
                act.copy(tot[:, :, bass.ds(2 * t, 2)], bank[6 + j][:, 0:8].rearrange("p (k b) -> p k b", k=KD))\
                    .then_inc(sm["tot_sb"], 1)

            with act.Fori(0, NT // 2) as h:
                for j in range(2):
                    x3_out(2 * h + j, j)
            act.wait_ge(sm["bn_step"], 8)
            act.activation(gain[:], var[:], ACT.Sqrt, bias=eps[:, 0:1]).then_inc(sm["bn_act"], 1)
            act.wait_ge(sm["bn_step"], 13)
            act.activation(amap[:], zc[:], ACT.Sigmoid).then_inc(sm["bn_act"], 1)

            sqrt(0, NT, 10)

            def f_hi(n, j):
                act.wait_ge(sm["f_tx"], n + 1)
                if holds(n, 2):
                    act.wait_ge(sm["f_base"], n - 1)
                act.copy(fh[j][:].rearrange("p k n -> p (k n)"), bank[j][:]).then_inc(sm["f_hi"], 1)

            def f_exp(n, j):
                act.wait_ge(sm["f_step"], NF * n + 2)
                act.activation(pr[j][:, 0:LE], bank[4 + j][:, P:P + LE], ACT.Exp, bias=nm[j][:, 0:1],
                               accum_out=nm[j][:, 1:2]).then_inc(sm["f_exp"], 1)

            def f_hth(n, j):
                act.wait_ge(sm["f_ht"], n + 1)
                if holds(n, 2):
                    act.wait_ge(sm["f_fin"], n - 1)
                act.copy(hth[j][:], bank[6][:, 0:P]).then_inc(sm["f_hth"], 1)

            def lora_act(n, j):
                if below(n, NT - 1):
                    f_hi(n + 1, 1 - j)
                if holds(n, 1) and below(n, NT + 1):
                    f_hth(n - 1, 1 - j)
                if below(n, NT):
                    f_exp(n, j)

            f_hi(0, 0)
            for n in range(2):
                lora_act(n, n)
            with act.Fori(1, (NT - 2) // 2) as h:
                for j in range(2):
                    lora_act(2 * h + j, j)
            for n in range(NT - 2, NT + 1):
                lora_act(n, n % 2)

        @block.vector
        def _(dve):
            def ln_stats(t):
                dve.bn_stats(stats[:, bass.ds(t, 1), :].rearrange("p a s -> p (a s)"),
                             X[:, bass.ds(t, 1), :].rearrange("p a d -> p (a d)")).then_inc(sm["lnstat"], 1)

            def ln_scale(lo, n, tiles, count):
                dve.wait_ge(sm["lnstat"], tiles)
                at = bass.ds(lo, n)
                m_e, v_e, m_o, v_o = (stats[:, at, c:c + 1].rearrange("p t o -> p (t o)") for c in (1, 2, 4, 5))
                for n_, ins in enumerate((
                        lambda: dve.tensor_tensor(mu[:, at], m_e, m_o, ALU.add),
                        lambda: dve.tensor_scalar(mu[:, at], mu[:, at], 0.5, None, ALU.mult),
                        lambda: dve.tensor_tensor(dm[:, at], m_e, m_o, ALU.subtract),
                        lambda: dve.tensor_tensor(dm[:, at], dm[:, at], dm[:, at], ALU.mult),
                        lambda: dve.tensor_tensor(va[:, at], v_e, v_o, ALU.add),
                        lambda: dve.tensor_scalar(va[:, at], va[:, at], 1.0 / D, None, ALU.mult),
                        lambda: dve.scalar_tensor_tensor(va[:, at], dm[:, at], 0.25, va[:, at], ALU.mult, ALU.add))):
                    ins().then_inc(sm["lnvar"], 1)
                    dve.wait_ge(sm["lnvar"], 7 * count - 6 + n_)
                dve.wait_ge(sm["lnsd"], count)
                dve.reciprocal(rs[:, at], sd[:, at]).then_inc(sm["lnrs"], 1)
                dve.wait_ge(sm["lnrs"], count)

            def ln_apply(t, j, done):
                return dve.tensor_scalar(xn[j][:], X[:, bass.ds(t, 1), :].rearrange("p a d -> p (a d)"),
                                         mu[:, bass.ds(t, 1)],
                                         rs[:, bass.ds(t, 1)], ALU.subtract, ALU.mult).then_inc(sm[done], 1)

            cc = [0]

            def c(ins):
                cc[0] += 1
                ins.then_inc(sm["cstep"], 1)
                dve.wait_ge(sm["cstep"], cc[0])

            dve.wait_ge(sm["cst_in"], 16)
            dve.wait_ge(sm["konst"], 4)
            for ch in range(2):
                for w in range(7):
                    tap = cst[:, C_CONV + 7 * ch + w:C_CONV + 7 * ch + w + 1]
                    if w == 0:
                        c(dve.tensor_scalar(band[:, ch, :], wide[:, 0:384], tap, None, ALU.mult))
                    else:
                        c(dve.scalar_tensor_tensor(band[:, ch, :], wide[:, w:w + 384], tap, band[:, ch, :],
                                                   ALU.mult, ALU.add))
            dve.tensor_scalar(cst[:, C_BQ:C_BQ + NG], cst[:, C_BQ:C_BQ + NG], 0.25, None, ALU.mult).then_inc(sm["sum_step"], 1)

            def stage1a(s):
                dve.wait_ge(sm["x_in"], 16 * s + 16)
                for i in range(4):
                    ln_stats(4 * s + i)
                ln_scale(4 * s, 4, 4 * s + 4, s + 1)
                for i in range(4):
                    t = 4 * s + i
                    if holds(t, 2):
                        dve.wait_ge(sm["tx_done"], t - 1)
                    ln_apply(t, i % 2, "xn_ready")

            def choose(g, k, blk, rnd):
                c0 = 10 * g + 2 * rnd
                src = ctxT[:, k, bass.ds(blk * 512, 512)] if isinstance(k, int) else \
                    ctxT[:, bass.ds(k, 1), bass.ds(blk * 512, 512)].rearrange("p a n -> p (a n)")
                src = src.rearrange("p (b c) -> p b c", c=S)
                if rnd == 0:
                    if holds(g, 1):
                        dve.wait_ge(sm["tstep"], 10 * g)
                    dve.tensor_scalar(neg[:, :, ::-1], src, -1.0, None, ALU.mult).then_inc(sm["mstep"], 1)
                    dve.wait_ge(sm["mstep"], g + 1)
                    carry(dve)
                for b in range(8):
                    ins = dve.max(best[:, b, :], neg[:, b, :])
                ins.then_inc(sm["tstep"], 1)
                dve.wait_ge(sm["tstep"], c0 + 1)
                if rnd < 3:
                    carry(dve)
                if rnd == 3:
                    dve.memset(best[:, :, NSUB - 24:8], -BIG).then_inc(sm["tstep"], 1)
                    c0 += 1
                    dve.wait_ge(sm["tstep"], c0 + 1)
                    carry(dve)
                for b in range(8):
                    ins = dve.match_replace(neg[:, b, :], best[:, b, :], neg[:, b, :], -BIG)
                ins.then_inc(sm["tstep"], 1)
                dve.wait_ge(sm["tstep"], c0 + 2)
                if rnd < 3:
                    carry(dve)
                if rnd == 3:
                    dve.tensor_scalar(src, neg[:, :, ::-1], -1e38, None, ALU.is_lt).then_inc(sm["tstep"], 1)

            stage1a(0)
            with dve.Fori(1, 4) as s:
                stage1a(s)
                dve.wait_ge(sm["proj_done"], 6 * s)
                for k in range(2):
                    for rnd in range(4):
                        choose(2 * s - 2 + k, k, s - 1, rnd)

            def shift(u, j):
                dve.wait_ge(sm["s_ready"], u + 1)
                sc_v = bank[j][:].rearrange("p (h k) -> p h k", h=NKV)
                dve.tensor_reduce(mx[j][:], sc_v, AX, ALU.max).then_inc(sm["mx_ready"], 1)
                dve.wait_ge(sm["mx_ready"], u + 1)
                if holds(u, 2):
                    dve.wait_ge(sm["exp_done"], u - 1)
                dve.tensor_tensor(dif[j][:], sc_v, mx[j][:].unsqueeze(2).broadcast_to([P, NKV, S]), ALU.subtract)\
                    .then_inc(sm["dif_ready"], 1)

            def normalise(u, j):
                dve.wait_ge(sm["pv_done"], u + 1)
                o = bank[6][:, 0:136].rearrange("p (a n) -> p a n", a=4)
                dve.reciprocal(rec[j][:], o[:, :, 32:34]).then_inc(sm["rec_ready"], 1)
                dve.wait_ge(sm["rec_ready"], u + 1)
                if holds(u, 2):
                    dve.wait_ge(sm["yt_done"], u - 1)
                dve.tensor_tensor(yn[j][:], o[:, :, 0:32].rearrange("p a (h d) -> p a h d", h=2),
                                  rec[j][:].unsqueeze(3).broadcast_to([P, 4, 2, HD]), ALU.mult)\
                    .then_inc(sm["yn_ready"], 1)

            def residual1(t):
                dve.wait_ge(sm["wo_done"], t + 1)
                dve.wait_ge(sm["x4b"], t + 1)
                dve.scalar_tensor_tensor(X[:, bass.ds(t, 1), :].rearrange("p a d -> p (a d)"), bank[4][:], tg[:, 0:1],
                                         X[:, bass.ds(t, 1), :].rearrange("p a d -> p (a d)"), ALU.mult, ALU.add)\
                    .then_inc(sm["x1_done"], 1)
                dve.wait_ge(sm["x1_done"], t + 1)
                ln_stats(t)

            def att_dve(u, i):
                if below(u, 2 * B - 1):
                    shift(u + 1, (i + 1) % 2)
                if holds(u, 1) and below(u, 2 * B + 1):
                    normalise(u - 1, (i - 1) % 2)
                if i == 2 and holds(u, 4):
                    residual1((u - 2) // 4 - 1)

            dve.wait_ge(sm["gates"], 1)
            shift(0, 0)
            for i in range(4):
                att_dve(i, i)
            with dve.Fori(1, NT - 1) as t:
                for i in range(4):
                    if below(t, NT):
                        shift(4 * t + i + 1, (i + 1) % 2)
                        normalise(4 * t + i - 1, (i - 1) % 2)
                        if i == 2:
                            residual1(t - 1)
            for u in range(2 * B - 4, 2 * B + 1):
                att_dve(u, u % 4)
            residual1(NT - 1)

            dve.wait_ge(sm["x1_done"], NT)
            dve.wait_ge(sm["w_hi"], 4)
            dve.tensor_tensor(wl[:, 2, :], wraw[:, 0], wh[:, 2, :].bitcast(F32), ALU.subtract).then_inc(sm["w_split"], 1)
            ln_scale(0, NT, 2 * NT, 5)
            for n, (o, i) in enumerate(((gwh, gw), (gwl, gw))):
                dve.wait_ge(sm["gw_in"], 16)
                if n == 0:
                    dve.tensor_copy(gwh[:], gw[:]).then_inc(sm["sum_step"], 1)
                    dve.wait_ge(sm["sum_step"], 2)
                else:
                    dve.tensor_tensor(gwl[:], gw[:], gwh[:].bitcast(F32), ALU.subtract).then_inc(sm["sum_step"], 1)

            def x2n(n, j):
                if holds(n, 2):
                    dve.wait_ge(sm["r_tx"], n - 1)
                    dve.wait_ge(sm[f"store_in{j}"], 16 * (n // 2))
                ln_apply(n, j, "n2")

            def lo(p, n, j):
                dve.wait_ge(sm[p + "hi"], n + 1)
                dve.tensor_tensor(xl[j][:].rearrange("p k n -> p (k n)"), bank[j][:],
                                  xh[j][:].rearrange("p k n -> p (k n)").bitcast(F32), ALU.subtract)\
                    .then_inc(sm[p + "lo"], 1)

            def z_lo(p, n, j):
                dve.wait_ge(sm[p + "zh"], n + 1)
                dve.tensor_tensor(zl[j][:].rearrange("p k n -> p (k n)"), bank[4][:, 0:I],
                                  zh[j][:].rearrange("p k n -> p (k n)").bitcast(F32), ALU.subtract)\
                    .then_inc(sm[p + "zl"], 1)

            def inner(p, n, j):
                dve.wait_ge(sm[p + "sg"], n + 1)
                if holds(n, 2):
                    dve.wait_ge(sm[p + "zt"], n - 1)
                dve.tensor_tensor(zz[j][:], bank[2 + j][:, I:2 * I], sg[j][:], ALU.mult).then_inc(sm[p + "z"], 1)

            def shared_out(n, j):
                dve.wait_ge(sm["a_y"], n + 1)
                xt = X[:, bass.ds(n, 1), :].rearrange("p a d -> p (a d)")
                dve.scalar_tensor_tensor(xt, bank[5 + j][:], tg[:, 2:3], xt, ALU.mult, ALU.add).then_inc(sm["a_x"], 1)

            def route_dve(n, j):
                if below(n, NT - 2):
                    x2n(n + 2, j)
                if below(n, NT - 1):
                    r_lo(n + 1, 1 - j)

            def r_lo(n, j):
                dve.wait_ge(sm["r_hi"], n + 1)
                dve.tensor_tensor(xl[j][:].rearrange("p k n -> p (k n)"), bank[j][:],
                                  xh[j][:].rearrange("p k n -> p (k n)").bitcast(F32), ALU.subtract)\
                    .then_inc(sm["r_lo"], 1)

            x2n(0, 0)
            x2n(1, 1)
            r_lo(0, 0)
            for n in range(2):
                route_dve(n, n)
            with dve.Fori(1, (NT - 2) // 2) as h:
                for j in range(2):
                    route_dve(2 * h + j, j)
            for n in range(NT - 2, NT):
                route_dve(n, n % 2)

            rc = [0]

            def r(ins, wait=True):
                rc[0] += 1
                ins.then_inc(sm["rstep"], 1)
                if wait:
                    dve.wait_ge(sm["rstep"], rc[0])

            dve.wait_ge(sm["rsig"], 1)
            dve.wait_ge(sm["konst"], KONST2)
            rb = cst[:, C_RB:C_RB + E].unsqueeze(1).broadcast_to([P, NT, E])
            r(dve.tensor_tensor(sc[:, :, 0:E], sc[:, :, 0:E], rb, ALU.add))
            for t in range(NT):
                r(dve.max(v8[:, t, :], sc[:, t, 0:E]), t == NT - 1)
            r(dve.tensor_reduce(wsum[:], v8[:, :, 0:TOPK], AX, ALU.add))
            r(dve.tensor_scalar(wsum[:], wsum[:], 1e-20, None, ALU.add))
            r(dve.reciprocal(wrec[:], wsum[:]))
            r(dve.tensor_scalar(wrec[:], wrec[:], tg[:, 2:3], None, ALU.mult))
            r(dve.memset(v8[:, :, TOPK:8], -BIG))
            for t in range(NT):
                r(dve.match_replace(scr[:, t, :], v8[:, t, :], sc[:, t, :], BIG), t == NT - 1)
            r(dve.tensor_scalar(sel[:], scr[:, :, 0:E], 1e38, None, ALU.is_gt), False)
            dve.wait_ge(sm["rstep"], rc[0])
            dve.sem_inc(sm["sel_ready"], 1)
            r(dve.memset(pre[:, 0, :], 0.0))
            dve.wait_ge(sm["rmm"], 1)
            for t in range(NT):
                r(dve.tensor_tensor(pre[:, t + 1, :], pre[:, t, :], bank[1][:, t * E:(t + 1) * E], ALU.add))
            r(dve.tensor_scalar(ucnt[:], pre[:, NT, :], float(P - 1), None, ALU.add))
            r(dve.tensor_scalar(ushf[:], ucnt[:], 7, None, ALU.arith_shift_right))
            r(dve.tensor_scalar(unum[:], ushf[:], 1.0, None, ALU.max))
            r(dve.tensor_tensor_scan(uend[:], ones16[:], unum[:], 0.0, ALU.mult, ALU.add))
            r(dve.tensor_tensor(ubase[:], uend[:], unum[:], ALU.subtract))
            r(dve.tensor_scalar(ubase[:], ubase[:], float(P), 1.0, ALU.mult, ALU.add))
            r(dve.tensor_tensor(slot[:], bank[0][:, 0:NT * E].rearrange("p (t e) -> p t e", e=E), pre[:, 0:NT, :], ALU.add))
            r(dve.tensor_tensor(slot[:], slot[:], ubase[:].unsqueeze(1).broadcast_to([P, NT, E]), ALU.add))
            r(dve.tensor_tensor(slot[:], slot[:], sel[:], ALU.mult))
            for t in range(NT):
                r(dve.max(k8[:, t, :], slot[:, t, :]), t == NT - 1)
            r(dve.tensor_scalar(sidx[:], k8[:, :, 0:TOPK], -1.0, None, ALU.add))
            for k in range(TOPK):
                r(dve.tensor_tensor(eq[:], slot[:], k8[:, :, k:k + 1].broadcast_to([P, NT, E]), ALU.is_equal))
                r(dve.tensor_tensor(eq[:], eq[:], sc[:, :, 0:E], ALU.mult))
                r(dve.tensor_reduce(wk[:, :, k], eq[:], AX, ALU.add))
            r(dve.tensor_tensor(wk[:], wk[:], wrec[:].unsqueeze(2).broadcast_to([P, NT, TOPK]), ALU.mult))
            r(dve.tensor_scalar(tix[:], sidx[:], P - 1, None, ALU.bitwise_and))
            r(dve.tensor_scalar(tiy[:], sidx[:], 7, None, ALU.arith_shift_right))
            r(dve.scalar_tensor_tensor(tix[:], tix[:], float(NU), tiy[:], ALU.mult, ALU.add))
            r(dve.tensor_copy(tw[:, :, :, 0], tok[:].unsqueeze(2).broadcast_to([P, NT, TOPK])))
            r(dve.tensor_copy(tw[:, :, :, 1].bitcast(F32), wk[:]))
            dve.sem_inc(sm["tables"], 1)
            r(dve.tensor_tensor(ule[:], uend[0:1, :].unsqueeze(1).broadcast_to([1, NU, E]),
                                uiota[:].unsqueeze(2).broadcast_to([1, NU, E]), ALU.is_le))
            r(dve.memset(ueid[:, 0:1], 0.0))
            r(dve.tensor_reduce(ueid[:, 1:NU + 1], ule[:], AX, ALU.add))
            r(dve.tensor_scalar(ueid[:, 1:NU + 1], ueid[:, 1:NU + 1], float(E - 1), None, ALU.min))
            r(dve.tensor_copy(uexp[:, 0:NU], ueid[:, 1:NU + 1]))
            gt = ule[:, 0:NU, 0]
            r(dve.tensor_tensor(gt, ueid[:, 1:NU + 1], ueid[:, 0:NU], ALU.is_gt))
            r(dve.scalar_tensor_tensor(gt, ueid[:, 1:NU + 1], E - 1.5, gt, ALU.is_lt, ALU.mult))
            r(dve.scalar_tensor_tensor(unext[:], ueid[:, 1:NU + 1], 1.0, gt, ALU.add, ALU.mult))
            r(dve.tensor_scalar(gt, ueid[:, 1:NU + 1], 3.0, None, ALU.is_ge))
            for m in range(6, E, 3):
                r(dve.scalar_tensor_tensor(gt, ueid[:, 1:NU + 1], float(m), gt, ALU.is_ge, ALU.add))
            r(dve.scalar_tensor_tensor(upar[:], gt, -3.0, ueid[:, 1:NU + 1], ALU.mult, ALU.add))
            dve.sem_inc(sm["utab"], 1)

            def shared_dve(n, j, g=None, rnd=0):
                if below(n, NT - 1):
                    lo("a_", n + 1, 1 - j)
                if holds(n, 2) and below(n, NT + 2):
                    shared_out(n - 2, j)
                if holds(n, 1) and below(n, NT + 1):
                    z_lo("a_", n - 1, 1 - j)
                if below(n, NT):
                    inner("a_", n, j)
                if g is not None:
                    choose(g, g - 6, 3, rnd)

            lo("a_", 0, 0)
            for n in range(4):
                shared_dve(n, n % 2, 6, n)
            with dve.Fori(1, 3) as h:
                for i in range(4):
                    shared_dve(4 * h + i, i % 2, h + 6, i)
            for n in range(NT - 4, NT):
                shared_dve(n, n % 2, 9, n - NT + 4)
            for n in range(NT, NT + 2):
                shared_dve(n, n % 2)

            def split_lo(nxt, half):
                with dve.If(nxt > 0):
                    dve.wait_ge(sm["w_hi"], 2 * nxt + 1 + half)
                    cols = slice(half * WALL // 2, (half + 1) * WALL // 2)
                    three, two = bass.ds(nxt % 3, 1), bass.ds(nxt % 2, 1)
                    ins = dve.tensor_tensor(wl[:, three, cols].rearrange("p a n -> p (a n)"),
                                            wraw[:, two, cols].rearrange("p a n -> p (a n)"),
                                            wh[:, three, cols].rearrange("p a n -> p (a n)").bitcast(F32), ALU.subtract)
                    if half == 1:
                        ins.then_inc(sm["w_split"], 1)

            def unit_dve(n, j, g=None, k=0, blk=0, rnd=0):
                if below(n, NU - 1):
                    lo("u_", n + 1, 1 - j)
                if holds(n, 1) and below(n, NU):
                    nxt = dve.value_load(unext[0:1, bass.ds(n, 1)], min_val=0, max_val=E - 1)
                    split_lo(nxt, 0)
                if holds(n, 1) and below(n, NU + 1):
                    z_lo("u_", n - 1, 1 - j)
                if below(n, NU):
                    if holds(n, 1):
                        split_lo(nxt, 1)
                    inner("u_", n, j)
                if g is not None:
                    choose(g, k, blk, rnd)

            dve.wait_ge(sm["p_split"], 2)
            dve.sem_inc(sm["w_split"], 1)
            lo("u_", 0, 0)
            for i in range(8):
                unit_dve(i, i % 2, 10 if i % 2 == 0 else None, 2, 0, i // 2)
            with dve.Fori(1, 6) as h:
                for i in range(8):
                    unit_dve(8 * h + i, i % 2, h + 10 if i % 2 == 0 else None, h // 3 + 2, h % 3, i // 2)
            with dve.Fori(24, (NU - 2) // 2) as h:
                for j in range(2):
                    unit_dve(2 * h + j, j)
            for n in range(NU - 2, NU + 1):
                unit_dve(n, n % 2)

            for q in range(4):
                dve.wait_ge(sm["xload"], 16 * q + 16)
                for i in range(4):
                    ln_stats(4 * q + i)
                ln_scale(4 * q, 4, 2 * NT + 4 * q + 4, 6 + q)

            def x3n(t, j):
                if holds(t, 2):
                    dve.wait_ge(sm["t_done"], t - 1)
                ln_apply(t, j, "l3")

            def features(t, j):
                dve.wait_ge(sm["x3_done"], t + 1)
                if holds(t, 2):
                    dve.wait_ge(sm["d3"], t - 1)
                m = ctxT[:, :, bass.ds(t * P, P)]
                dve.scalar_tensor_tensor(cf[j][:], m, 0.5, x3T[:, :, bass.ds(t * P, P)], ALU.is_lt, ALU.mult)\
                    .then_inc(sm["c3"], 1)
                dve.wait_ge(sm["c3"], t + 1)
                cv = cf[j][:].rearrange("p k (b c) -> p k b c", c=S)
                dve.tensor_reduce(maps[:, 0, :, 0, bass.ds(2 * t, 2)], cv, AX, ALU.max).then_inc(sm["r3"], 1)
                dve.tensor_reduce(maps[:, 1, :, 0, bass.ds(2 * t, 2)], cv, AX, ALU.add).then_inc(sm["r3"], 1)

            def features_rest(t, j):
                dve.wait_ge(sm["d3"], t + 1)
                sv = sf[j][:].rearrange("p k (b c) -> p k b c", c=S)
                dve.tensor_reduce(maps[:, 0, :, 1, bass.ds(2 * t, 2)], sv, AX, ALU.max).then_inc(sm["m3"], 1)

            def gate_dve(t, j):
                if below(t, NT - 2):
                    x3n(t + 2, j)
                if below(t, NT):
                    features(t, j)
                if holds(t, 1):
                    features_rest(t - 1, 1 - j)

            x3n(0, 0)
            x3n(1, 1)
            for t in range(2):
                gate_dve(t, t)
            with dve.Fori(1, (NT - 2) // 2) as h:
                for j in range(2):
                    gate_dve(2 * h + j, j)
            for t in range(NT - 2, NT + 1):
                gate_dve(t, t % 2)
            dve.wait_ge(sm["m3"], NT)
            dve.wait_ge(sm["r3"], 2 * NT)
            dve.wait_ge(sm["tot_sb"], NT)
            c(dve.tensor_tensor(maps[:, 1, :, 1, :], tot[:], maps[:, 1, :, 0, :], ALU.subtract))
            c(dve.tensor_scalar(maps[:, 1, :, 0, :], maps[:, 1, :, 0, :], 1.0 / NSEL, None, ALU.mult))
            c(dve.tensor_scalar(maps[:, 1, :, 1, :], maps[:, 1, :, 1, :], 1.0 / NSUB, None, ALU.mult))

            bc = [0]

            def b_(ins):
                bc[0] += 1
                ins.then_inc(sm["bn_step"], 1)
                dve.wait_ge(sm["bn_step"], bc[0])

            dve.wait_ge(sm["bn_mm"], 1)
            b_(dve.tensor_copy(zc[:], bank[4][:, 0:2 * KD * B].rearrange("p (k r b) -> p r k b", k=KD, r=2)))
            b_(dve.tensor_reduce(part[:], zc[:].rearrange("p r k b -> p r (k b)"), AX, ALU.add))
            dve.wait_ge(sm["bn_mm"], 2)
            b_(dve.tensor_scalar(mean[:], bank[5][:, 0:2], 1.0 / (B * D), None, ALU.mult))
            for rr in range(2):
                b_(dve.tensor_scalar(zc[:, rr], zc[:, rr], mean[:, rr:rr + 1], None, ALU.subtract))
            b_(dve.tensor_tensor(zq[:], zc[:], zc[:], ALU.mult))
            b_(dve.tensor_reduce(part[:], zq[:].rearrange("p r k b -> p r (k b)"), AX, ALU.add))
            dve.wait_ge(sm["bn_mm"], 3)
            b_(dve.tensor_scalar(var[:], bank[5][:, 0:2], 1.0 / (B * D), None, ALU.mult))
            dve.wait_ge(sm["bn_act"], 1)
            b_(dve.reciprocal(gain[:], gain[:]))
            b_(dve.tensor_scalar(gain[:], gain[:], cst[:, C_BN:C_BN + 1], None, ALU.mult))
            for rr in range(2):
                b_(dve.tensor_scalar(zc[:, rr], zc[:, rr], gain[:, rr:rr + 1], cst[:, C_BN + 1:C_BN + 2], ALU.mult, ALU.add))
            b_(dve.tensor_scalar(zc[:], zc[:], 0.0, None, ALU.max))
            dve.wait_ge(sm["bn_act"], 2)
            b_(dve.tensor_tensor(amap[:, 1], amap[:, 1], amap[:, 0], ALU.subtract))

            def gated(t, j):
                dve.wait_ge(sm["y3p"], 2 * t + 2)
                dve.tensor_tensor(asel[j][:], asel[j][:], x3T[:, :, bass.ds(t * P, P)], ALU.mult).then_inc(sm["y3"], 1)

            def residual3(t, j):
                dve.wait_ge(sm["y3t"], t + 1)
                xt = X[:, bass.ds(t, 1), :].rearrange("p a d -> p (a d)")
                dve.scalar_tensor_tensor(xt, bank[2 + j][:], tg[:, 1:2], xt, ALU.mult, ALU.add).then_inc(sm["x3_sum"], 1)
                dve.wait_ge(sm["x3_sum"], t + 1)
                ln_stats(t)

            def gated_step(t, j):
                if below(t, NT):
                    gated(t, j)
                if holds(t, 1):
                    residual3(t - 1, 1 - j)

            for t in range(2):
                gated_step(t, t)
            with dve.Fori(1, (NT - 2) // 2) as h:
                for j in range(2):
                    gated_step(2 * h + j, j)
            for t in range(NT - 2, NT + 1):
                gated_step(t, t % 2)

            ln_scale(0, NT, 4 * NT, 10)

            def x4n(t, j):
                if holds(t, 2):
                    dve.wait_ge(sm["f_tx"], t - 1)
                ln_apply(t, j, "l4")

            def f_lo(n, j):
                dve.wait_ge(sm["f_hi"], n + 1)
                dve.tensor_tensor(fl[j][:].rearrange("p k n -> p (k n)"), bank[j][:],
                                  fh[j][:].rearrange("p k n -> p (k n)").bitcast(F32), ALU.subtract)\
                    .then_inc(sm["f_lo"], 1)

            def f_route(n, j):
                dve.wait_ge(sm["f_h"], n + 1)
                carry(dve)
                hb = bank[4 + j]
                step = [0]

                def q(ins):
                    step[0] += 1
                    ins.then_inc(sm["f_step"], 1)
                    dve.wait_ge(sm["f_step"], NF * n + step[0])
                    if step[0] in (4, 8):
                        carry(dve)

                q(dve.max(m8[j][:], hb[:, P:P + LE]))
                q(dve.tensor_scalar(nm[j][:, 0:1], m8[j][:, 0:1], -1.0, None, ALU.mult))
                dve.wait_ge(sm["f_exp"], n + 1)
                q(dve.reciprocal(nm[j][:, 2:3], nm[j][:, 1:2]))
                q(dve.tensor_scalar(pr[j][:, 0:LE], pr[j][:, 0:LE], nm[j][:, 2:3], None, ALU.mult))
                q(dve.max(m8[j][:], pr[j][:, 0:LE]))
                q(dve.tensor_tensor(nm[j][:, 3:4], m8[j][:, 0:1], m8[j][:, 1:2], ALU.add))
                q(dve.memset(m8[j][:, 2:8], -1.0))
                q(dve.reciprocal(nm[j][:, 4:5], nm[j][:, 3:4]))
                q(dve.match_replace(prr[j][:], m8[j][:], pr[j][:], BIG))
                q(dve.scalar_tensor_tensor(lw[j][:], prr[j][:, 0:LE], 1e38, pr[j][:, 0:LE], ALU.is_gt, ALU.mult))
                q(dve.tensor_scalar(lw[j][:], lw[j][:], nm[j][:, 4:5], 2.0, ALU.mult, ALU.mult))
                assert step[0] == NF
                if holds(n, 2):
                    dve.wait_ge(sm["f_ht"], n - 1)
                dve.tensor_tensor(hw[j][:].rearrange("p (e r) -> p e r", e=LE), hb[:, 0:P].rearrange("p (e r) -> p e r", e=LE),
                                  lw[j][:].unsqueeze(2).broadcast_to([P, LE, LR]), ALU.mult).then_inc(sm["f_hw"], 1)

            def f_htl(n, j):
                dve.wait_ge(sm["f_hth"], n + 1)
                dve.tensor_tensor(htl[j][:], bank[6][:, 0:P], hth[j][:].bitcast(F32), ALU.subtract).then_inc(sm["f_htl"], 1)

            def f_final(n, j):
                dve.wait_ge(sm["f_fin"], n + 1)
                dve.wait_ge(sm["cpre"], n + 1)
                if holds(n, 2):
                    dve.wait_ge(sm[f"out_d{j}"], 16 * (n // 2))
                dve.scalar_tensor_tensor(fo[j][:], bank[2 + j][:], tg[:, 3:4],
                                         X[:, bass.ds(n, 1), :].rearrange("p a d -> p (a d)"), ALU.mult, ALU.add)\
                    .then_inc(sm["f_out"], 1)

            def lora_dve(n, j):
                if below(n, NT - 2):
                    x4n(n + 2, j)
                if below(n, NT - 1):
                    f_lo(n + 1, 1 - j)
                if holds(n, 2):
                    f_final(n - 2, j)
                if holds(n, 1) and below(n, NT + 1):
                    f_htl(n - 1, 1 - j)
                if below(n, NT):
                    f_route(n, j)

            x4n(0, 0)
            x4n(1, 1)
            f_lo(0, 0)
            for n in range(2):
                lora_dve(n, n)
            with dve.Fori(1, (NT - 2) // 2) as h:
                for j in range(2):
                    lora_dve(2 * h + j, j)
            for n in range(NT - 2, NT + 2):
                lora_dve(n, n % 2)

        @block.tensor
        def _(pe):
            pe.wait_ge(sm["konst"], KONST1)

            def turn(dst, src, wait_sem, count):
                for k in range(KD):
                    ins = pe.transpose(dst[:, k * P:(k + 1) * P], src[:, k * P:(k + 1) * P], ident[:])
                ins.then_inc(sm[wait_sem], 1)

            def stage1a(s):
                for i in range(4):
                    t = 4 * s + i
                    pe.wait_ge(sm["xn_ready"], t + 1)
                    if holds(t, 2):
                        pe.wait_ge(sm["xnT_ready"], t - 1)
                    turn(bank[2 + i % 2], xn[i % 2], "tx_done", t)
                pe.wait_ge(sm["xnT_ready"], 4 * s + 4)
                pe.wait_ge(sm["ctx_in"], 16 * s + 16)
                for q in range(6):
                    if q >= 2 or holds(s, 1):
                        pe.wait_ge(sm["proj_out"], 6 * s + q - 1)
                    for k in range(KD):
                        w = wq[:, k, q, :] if q < 4 else wkv[:, k, q - 4, :]
                        x = xnT[:, k, :] if q < 4 else ctxT[:, k, bass.ds(s * 512, 512)]
                        ins = pe.matmul(bank[q % 2][:], w, x, start=(k == 0), stop=(k == KD - 1))
                    ins.then_inc(sm["proj_done"], 1)

            pe.wait_ge(sm["watt_in"], 32)
            stage1a(0)
            with pe.Fori(1, 4) as s:
                stage1a(s)

            pe.wait_ge(sm["proj_out"], 24)
            pe.wait_ge(sm["watt_in"], 64)

            def scores(u, i):
                j = i % 2
                pe.wait_ge(sm["b_ready"], 3 * (u // 2) + 3)
                if holds(u, 2):
                    pe.wait_ge(sm["dif_ready"], u - 1)
                g, jb = 2 * (i % 2), i // 2 % 2
                pe.matmul(bank[j][:], qTb[jb][:, g:g + 2, :].rearrange("p g q -> p (g q)"),
                          kblk[jb][:].rearrange("p h k -> p (h k)"), start=True, stop=True).then_inc(sm["s_ready"], 1)

            def prob_turn(u, j):
                pe.wait_ge(sm["exp_done"], u + 1)
                if holds(u, 2):
                    pe.wait_ge(sm["ptc_done"], u - 1)
                turn(bank[2 + j], prob[j], "pt_done", u)

            def values(b, j):
                if holds(b, 1):
                    pe.wait_ge(sm["v_ready"], 2 * b)
                pe.wait_ge(sm["b_ready"], 3 * b + 3)
                pe.transpose(bank[5][:, 0:P], vTb[j][:].rearrange("p a k -> p (a k)"), ident[:]).then_inc(sm["v_done"], 1)

            def weigh(u, i):
                j = i % 2
                pe.wait_ge(sm["ptc_done"], u + 1)
                pe.wait_ge(sm["v_ready"], 2 * (u // 2) + 2)
                if holds(u, 1):
                    pe.wait_ge(sm["yn_ready"], u)
                for a in range(4):
                    ins = pe.matmul(bank[6][:, 34 * a:34 * a + 34], probT[j][:, a, :],
                                    vblk[i // 2 % 2][:, a, :], start=True, stop=True)
                ins.then_inc(sm["pv_done"], 1)

            def y_turn(u, j):
                pe.wait_ge(sm["yn_ready"], u + 1)
                if holds(u, 1):
                    pe.wait_ge(sm["ytc_done"], u)
                pe.transpose(bank[7][:, 0:P], yn[j][:].rearrange("p a h d -> p (a h d)"), ident[:])\
                    .then_inc(sm["yt_done"], 1)

            def project(t):
                pe.wait_ge(sm["ytc_done"], 4 * t + 4)
                if holds(t, 1):
                    pe.wait_ge(sm["x1_done"], t)
                for g in range(NG):
                    ins = pe.matmul(bank[4][:], yT[:, g, :], wo[:, g, :], start=(g == 0), stop=(g == NG - 1))
                ins.then_inc(sm["wo_done"], 1)

            def att_pe(u, i, t):
                if below(u, 2 * B):
                    prob_turn(u, i % 2)
                if i == 2 and holds(u, 4):
                    project(t - 1)
                if i % 2 == 1 and below(u, 2 * B - 1):
                    values((u + 1) // 2, (i + 1) // 2 % 2)
                if holds(u, 1) and below(u, 2 * B + 1):
                    weigh(u - 1, (i - 1) % 4)
                if holds(u, 2) and below(u, 2 * B + 2):
                    y_turn(u - 2, i % 2)
                if below(u, 2 * B - 2):
                    scores(u + 2, (i + 2) % 4)

            scores(0, 0)
            scores(1, 1)
            values(0, 0)
            for i in range(4):
                att_pe(i, i, 0)
            with pe.Fori(1, NT - 1) as t:
                for i in range(4):
                    att_pe(4 * t + i, i, t)
            for u in range(2 * B - 4, 2 * B + 2):
                att_pe(u, u % 4, u // 4)
            project(NT - 1)

            def parts(hi_, lo_):
                return (lambda k: hi_[:, k, :]), (lambda k: lo_[:, k, :])

            def gate_up(p, n, j, at, first):
                if first:
                    pe.wait_ge(sm[p + "lo"], n + 1)
                    if holds(n, 2):
                        pe.wait_ge(sm[p + "z"], n - 1)
                w = [(lambda k, m=m: m[:, at, k * D:(k + 1) * D]) for m in (wh, wl)]
                ins = split3(pe, bank[2 + j][:], parts(xh[j], xl[j]), w, (0, 1) if first else (2, 3), first, not first)
                if not first:
                    ins.then_inc(sm[p + "gu"], 1)

            def z_turn(p, n, j):
                pe.wait_ge(sm[p + "z"], n + 1)
                if holds(n, 1):
                    pe.wait_ge(sm[p + "zl"], n)
                for k in range(2):
                    ins = pe.transpose(bank[4][:, k * P:(k + 1) * P], zz[j][:, k * P:(k + 1) * P], ident[:])
                ins.then_inc(sm[p + "zt"], 1)

            def down(p, n, j, at, freed):
                pe.wait_ge(sm[p + "zl"], n + 1)
                if holds(n, 2):
                    pe.wait_ge(sm[freed], n - 1)
                w = [(lambda k, m=m: m[:, at, WGU + k * D:WGU + (k + 1) * D]) for m in (wh, wl)]
                split3(pe, bank[5 + j][:], parts(zh[j], zl[j]), w, (0, 1), True, True).then_inc(sm[p + "y"], 1)

            def logits(n, j):
                if holds(n, 1):
                    pe.wait_ge(sm["a_rtc"], n)
                pe.wait_ge(sm["r_lo"], n + 1)
                split3(pe, bank[7][:, 0:E], parts(xh[j], xl[j]), parts(gwh, gwl), range(KD), True, True)\
                    .then_inc(sm["a_rt"], 1)

            def r_turn(n, j):
                pe.wait_ge(sm["n2"], n + 1)
                if holds(n, 2):
                    pe.wait_ge(sm["r_lo"], n - 1)
                turn(bank[j], xn[j], "r_tx", n)

            def route_pe(n, j):
                if below(n, NT - 1):
                    r_turn(n + 1, 1 - j)
                logits(n, j)

            r_turn(0, 0)
            pe.wait_ge(sm["sum_step"], 3)
            for n in range(2):
                route_pe(n, n)
            with pe.Fori(1, (NT - 2) // 2) as h:
                for j in range(2):
                    route_pe(2 * h + j, j)
            for n in range(NT - 2, NT):
                route_pe(n, n % 2)

            pe.wait_ge(sm["sel_ready"], 1)
            pe.matmul(bank[0][:, 0:NT * E], lower[:], sel[:].rearrange("p t e -> p (t e)"), start=True, stop=True)
            pe.matmul(bank[1][:, 0:NT * E], onesm[:], sel[:].rearrange("p t e -> p (t e)"), start=True, stop=True)\
                .then_inc(sm["rmm"], 1)

            def x_turn(n, j):
                pe.wait_ge(sm[f"load_in{j}"], 16 * (n // 2) + 16)
                if holds(n, 2):
                    pe.wait_ge(sm["a_lo"], n - 1)
                turn(bank[j], xn[j], "a_tx", n)

            def shared_pe(n, j):
                if below(n, NT - 1):
                    x_turn(n + 1, 1 - j)
                if below(n, NT):
                    gate_up("a_", n, j, 2, True)
                if holds(n, 1) and below(n, NT + 1):
                    z_turn("a_", n - 1, 1 - j)
                if below(n, NT):
                    gate_up("a_", n, j, 2, False)
                if holds(n, 1) and below(n, NT + 1):
                    down("a_", n - 1, 1 - j, 2, "a_x")

            pe.wait_ge(sm["tables"], 1)
            x_turn(0, 0)
            pe.wait_ge(sm["w_split"], 1)
            for n in range(2):
                shared_pe(n, n)
            with pe.Fori(1, (NT - 2) // 2) as h:
                for j in range(2):
                    shared_pe(2 * h + j, j)
            for n in range(NT - 2, NT + 1):
                shared_pe(n, n % 2)

            def g_turn(n, j):
                pe.wait_ge(sm[f"g_in{j}"], 16 * (n // 2) + 16)
                if holds(n, 2):
                    pe.wait_ge(sm["u_lo"], n - 1)
                turn(bank[j], xn[j], "u_tx", n)

            def unit_of(n):
                if not below(n, NU):
                    return None, None
                e = pe.value_load(uexp[0:1, bass.ds(n, 1)], min_val=0, max_val=E - 1)
                return e, e % 3

            def unit_pe(n, j, before, now, then):
                if below(n, NU - 1):
                    g_turn(n + 1, 1 - j)
                if below(n, NU):
                    pe.wait_ge(sm["w_split"], now[0] + 1)
                    gate_up("u_", n, j, now[1], True)
                if holds(n, 1) and below(n, NU + 1):
                    z_turn("u_", n - 1, 1 - j)
                if below(n, NU):
                    gate_up("u_", n, j, now[1], False)
                after = unit_of(n + 1) if then else None
                if holds(n, 1) and below(n, NU + 1):
                    down("u_", n - 1, 1 - j, before[1], "u_yo")
                return now, after

            def units_pe(at, count):
                before = unit_of(at - 1) if holds(at, 1) else None
                now = unit_of(at)
                for i in range(count):
                    before, now = unit_pe(at + i, i % 2, before, now, i < count - 1)

            pe.wait_ge(sm["utab"], 1)
            g_turn(0, 0)
            units_pe(0, 4)
            with pe.Fori(1, NU // 4 - 1) as h:
                units_pe(4 * h, 4)
            units_pe(NU - 4, 5)

            def x3_turn(t, j):
                pe.wait_ge(sm["l3"], t + 1)
                if holds(t, 2):
                    pe.wait_ge(sm["x3_done"], t - 1)
                if holds(t, 2):
                    pe.wait_ge(sm["tot_sb"], t - 1)
                for k in range(KD):
                    ins = pe.matmul(bank[6 + j][:, 2 * k:2 * k + 2], xn[j][:, k * P:(k + 1) * P], bsel[:], start=True, stop=True)
                ins.then_inc(sm["tot_ps"], 1)
                turn(bank[j], xn[j], "t_done", t)

            pe.wait_ge(sm["konst3"], 4)
            for t in range(2):
                x3_turn(t, t)
            with pe.Fori(1, NT // 2) as h:
                for j in range(2):
                    x3_turn(2 * h + j, j)
            pe.wait_ge(sm["cstep"], 17)
            for ko in range(KD):
                terms = [(ch, ki) for ki in range(max(0, ko - 1), min(KD, ko + 2)) for ch in range(2)]
                for n, (ch, ki) in enumerate(terms):
                    off = P + P * (ko - ki)
                    ins = pe.matmul(bank[4][:, ko * 64:(ko + 1) * 64], band[:, ch, off:off + P],
                                    maps[:, ch, ki].rearrange("p r b -> p (r b)"),
                                    start=(n == 0), stop=(n == len(terms) - 1))
            ins.then_inc(sm["bn_mm"], 1)
            for step in (2, 7):
                pe.wait_ge(sm["bn_step"], step)
                pe.matmul(bank[5][:, 0:2], ones3[:], part[:], start=True, stop=True).then_inc(sm["bn_mm"], 1)

            def y3_turn(t, j):
                pe.wait_ge(sm["y3"], t + 1)
                if holds(t, 2):
                    pe.wait_ge(sm["x3_sum"], t - 1)
                turn(bank[2 + j], asel[j][:].rearrange("p k n -> p (k n)"), "y3t", t)

            for t in range(2):
                y3_turn(t, t)
            with pe.Fori(1, NT // 2) as h:
                for j in range(2):
                    y3_turn(2 * h + j, j)

            pe.wait_ge(sm["w4_split"], 6)

            def f_turn(n, j):
                pe.wait_ge(sm["l4"], n + 1)
                if holds(n, 2):
                    pe.wait_ge(sm["f_lo"], n - 1)
                turn(bank[j], xn[j], "f_tx", n)

            def f_low(n, j):
                pe.wait_ge(sm["f_lo"], n + 1)
                if holds(n, 2):
                    pe.wait_ge(sm["f_hw"], n - 1)
                split3(pe, bank[4 + j][:, 0:136], parts(fh[j], fl[j]), parts(*aws), range(KD), True, True)\
                    .then_inc(sm["f_h"], 1)

            def f_hw_turn(n, j):
                pe.wait_ge(sm["f_hw"], n + 1)
                if holds(n, 1):
                    pe.wait_ge(sm["f_htl"], n)
                pe.transpose(bank[6][:, 0:P], hw[j][:], ident[:]).then_inc(sm["f_ht"], 1)

            def f_base(n, j):
                if holds(n, 2):
                    pe.wait_ge(sm["f_out"], n - 1)
                split3(pe, bank[2 + j][:], parts(fh[j], fl[j]), parts(*wbs), range(KD), True, False)\
                    .then_inc(sm["f_base"], 1)

            def f_up(n, j):
                pe.wait_ge(sm["f_htl"], n + 1)
                split3(pe, bank[2 + j][:], (lambda k: hth[j][:], lambda k: htl[j][:]),
                       (lambda k: bms[0][:], lambda k: bms[1][:]), (0,), False, True).then_inc(sm["f_fin"], 1)

            def lora_pe(n, j):
                if below(n, NT - 1):
                    f_turn(n + 1, 1 - j)
                if below(n, NT):
                    f_low(n, j)
                if holds(n, 1) and below(n, NT + 1):
                    f_hw_turn(n - 1, 1 - j)
                if below(n, NT):
                    f_base(n, j)
                if holds(n, 1) and below(n, NT + 1):
                    f_up(n - 1, 1 - j)

            f_turn(0, 0)
            for n in range(2):
                lora_pe(n, n)
            with pe.Fori(1, (NT - 2) // 2) as h:
                for j in range(2):
                    lora_pe(2 * h + j, j)
            for n in range(NT - 2, NT + 1):
                lora_pe(n, n % 2)



def kernel(**inputs):
    import numpy as np
    import concourse.bacc as bacc
    from concourse.bass_utils import run_bass_kernel_spmd

    a = {k: np.asarray(v) for k, v in inputs.items()}
    rows = [a["g_xattn"], a["g_ffn"], a["L0_ffn_bias"], a["L1_xattn_conv_w"].reshape(14),
            a["L1_xattn_bn_gamma"], a["L1_xattn_bn_beta"]]
    head = a["L0_xattn_bq"].reshape(NKV, NG, HD).transpose(0, 2, 1).reshape(P, NG)
    cols = [head, a["L0_xattn_bk"][:, None], a["L0_xattn_bv"][:, None]]
    cst = np.concatenate([np.broadcast_to(np.concatenate(rows), (P, C_BQ))] + cols, axis=1)

    def pieces(w):
        e, k, n = w.shape
        return w.reshape(e, k // P, P, n).transpose(0, 2, 1, 3).reshape(e, P, -1)

    wg = np.concatenate([a["L0_ffn_Wg"], a["L0_ffn_Sg"][None]]).transpose(0, 2, 1)
    wu = np.concatenate([a["L0_ffn_Wu"], a["L0_ffn_Su"][None]]).transpose(0, 2, 1)
    wd = np.concatenate([a["L0_ffn_Wd"], a["L0_ffn_Sd"][None]]).transpose(0, 2, 1)
    arrays = {
        "x": a["x"].reshape(T, D),
        "ctxT": a["ctx_4096"].reshape(T, D).T,
        "cst": cst,
        "wq": a["L0_xattn_Wq"].reshape(D, NKV, NG, HD).transpose(0, 2, 1, 3).reshape(D, D),
        "wkv": np.concatenate([a["L0_xattn_Wk"], a["L0_xattn_Wv"]], axis=1),
        "wo": a["L0_xattn_Wo"].reshape(NKV, NG, HD, D).transpose(1, 0, 2, 3).reshape(NG, P, D),
        "bo": np.broadcast_to(a["L0_xattn_bo"], (P, D)),
        "gate": a["L0_ffn_gate_w"].T,
        "wall": np.concatenate([pieces(np.concatenate([wg, wu], axis=2)), pieces(wd)], axis=2),
        "wb": a["L1_ffn_Wb"].T,
        "aw": np.concatenate([a["L1_ffn_A"].reshape(LE * LR, D), a["L1_ffn_Wr"]]).T,
        "bm": a["L1_ffn_Bm"].transpose(0, 2, 1).reshape(LE * LR, D),
        "b1": np.broadcast_to(a["L1_ffn_bias"], (P, D)),
    }
    nc = bacc.Bacc("TRN2", target_bir_lowering=False, num_devices=1)
    arrays = {f"in_{k}": np.ascontiguousarray(v) for k, v in arrays.items()}
    io = [nc.dram_tensor(k, v.shape, mybir.dt.from_np(v.dtype), kind="ExternalInput").ap() for k, v in arrays.items()]
    io.append(nc.dram_tensor("out_0", (T, D), F32, kind="ExternalOutput").ap())
    block_program(nc, io)
    r = run_bass_kernel_spmd(nc, [arrays], core_ids=[0])
    return r.results[0]["out_0"].reshape(B, S, D)
```

```python
from contextlib import ExitStack

import concourse.bass as bass
from concourse import mybir

F32 = mybir.dt.float32
F32R = mybir.dt.float32r
I32 = mybir.dt.int32
ALU = mybir.AluOpType
ACT = mybir.ActivationFunctionType
AX = mybir.AxisListType.X

P = 128
B, S, D = 32, 64, 512
T = B * S
NT = T // P
KD = D // P
NKV, NG, HD = 8, 4, 16
E, I, TOPK = 16, 256, 4
WGU = KD * 2 * I
WALL = WGU + (I // P) * D
NU = T * TOPK // P + E
NSEL = 38
NSUB = S - NSEL
NF = 11
KONST1, KONST2 = 14, 25
LE, LR = 8, 16
EPS = 1e-5
BIG = 3.0e38

C_GATE, C_RB, C_CONV, C_BN, C_BQ, C_BK, C_BV = 0, 4, 20, 34, 36, 40, 41
C_ALL = 42


def holds(n, least):
    return n >= least if isinstance(n, int) else True


def below(n, limit):
    return n < limit if isinstance(n, int) else True


def block_program(nc, io):
    (x_in, ctxT_in, cst_in, wq_in, wkv_in, wo_in, bo_in, gate_in, wall_in,
     wb_in, aw_in, bm_in, b1_in, out) = io
    with ExitStack() as ctx:
        def sb(name, shape, dt=F32, stack=ctx):
            return stack.enter_context(nc.sbuf_tensor(name, shape, dt))

        def sem(name):
            return ctx.enter_context(nc.semaphore(name))

        bank = [ctx.enter_context(nc.psum_tensor(f"bank{i}", [P, 512], F32)) for i in range(8)]

        X = sb("X", [P, NT, D])
        ctxT = sb("ctxT", [P, KD, T])
        cst = sb("cst", [P, C_ALL])
        tg = sb("tg", [P, 4])
        eps = sb("eps", [P, 1])
        ident = sb("ident", [P, P])
        stats = sb("stats", [P, NT, 6])
        mu = sb("mu", [P, NT])
        va = sb("va", [P, NT])
        dm = sb("dm", [P, NT])
        sd = sb("sd", [P, NT])
        rs = sb("rs", [P, NT])
        nb = sb("nb", [P, NT])
        xn = [sb(f"xn{j}", [P, D]) for j in range(2)]

        neg = sb("neg", [P, 8, S])
        best = sb("best", [P, 8, 8])
        band = sb("band", [P, 2, 384])

        with ExitStack() as s1:
            sb("wraw_kept", [P, WALL], F32, s1)
            QT = sb("QT", [P, NG, T], F32, s1)
            KT = sb("KT", [P, T], F32, s1)
            VT = sb("VT", [P, T], F32, s1)
            xnT = sb("xnT", [P, KD, 512], F32, s1)
            wq = sb("wq", [P, KD, NG, P], F32, s1)
            wkv = sb("wkv", [P, KD, 2, P], F32, s1)
            wo = sb("wo", [P, NG, D], F32, s1)
            bo = sb("bo", [P, D], F32, s1)
            hmask = sb("hmask", [P, NKV], F32, s1)
            wide = sb("wide", [P, 390], F32, s1)
            qTb = [sb(f"qTb{j}", [P, NG, S], F32, s1) for j in range(2)]
            kblk = [sb(f"kblk{j}", [P, NKV, S], F32, s1) for j in range(2)]
            vTb = [sb(f"vTb{j}", [P, 2, S], F32, s1) for j in range(2)]
            vblk = [sb(f"vblk{j}", [P, 4, 34], F32, s1) for j in range(2)]
            mx = [sb(f"mx{j}", [P, NKV], F32, s1) for j in range(2)]
            dif = [sb(f"dif{j}", [P, NKV, S], F32, s1) for j in range(2)]
            prob = [sb(f"prob{j}", [P, NKV * S], F32, s1) for j in range(2)]
            probT = [sb(f"probT{j}", [P, 4, P], F32, s1) for j in range(2)]
            rec = [sb(f"rec{j}", [P, 4, 2], F32, s1) for j in range(2)]
            yn = [sb(f"yn{j}", [P, 4, 2, HD], F32, s1) for j in range(2)]
            yT = sb("yT", [P, NG, P], F32, s1)

        with ExitStack() as sr:
            sb("wraw_kept2", [P, WALL], F32, sr)
            lgT = [sb(f"lgT{j}", [E, P], F32, sr) for j in range(2)]
            sc = sb("sc", [P, NT, 24], F32, sr)
            scr = sb("scr", [P, NT, 24], F32, sr)
            v8 = sb("v8", [P, NT, 8], F32, sr)
            wsum = sb("wsum", [P, NT], F32, sr)
            wrec = sb("wrec", [P, NT], F32, sr)
            sel = sb("sel", [P, NT, E], F32, sr)
            pre = sb("pre", [P, E, NT + 1], F32, sr)
            scan = sb("scan", [P, E * NT], F32, sr)
            slot = sb("slot", [P, NT, E], F32, sr)
            eq = sb("eq", [P, NT, E], F32, sr)
            k8 = sb("k8", [P, NT, 8], F32, sr)
            ucnt = sb("ucnt", [P, E], I32, sr)
            ushf = sb("ushf", [P, E], I32, sr)
            unum = sb("unum", [P, E], F32, sr)
            uend = sb("uend", [P, E], F32, sr)
            ubase = sb("ubase", [P, E], F32, sr)
            ones16 = sb("ones16", [P, E], F32, sr)
            uiota = sb("uiota", [1, NU], F32, sr)
            ueid = sb("ueid", [1, NU + 1], F32, sr)
            lower = sb("lower", [P, P], F32, sr)
            onesm = sb("onesm", [P, P], F32, sr)

        with ExitStack() as s2:
            wraw = sb("wraw", [P, 2, WALL], F32, s2)
            wh = sb("wh", [P, 3, WALL], F32R, s2)
            wl = sb("wl", [P, 3, WALL], F32R, s2)
            gw = sb("gw", [P, KD, E], F32, s2)
            gwh = sb("gwh", [P, KD, E], F32R, s2)
            gwl = sb("gwl", [P, KD, E], F32R, s2)
            xh = [sb(f"xh{j}", [P, KD, P], F32R, s2) for j in range(2)]
            xl = [sb(f"xl{j}", [P, KD, P], F32R, s2) for j in range(2)]
            sg = [sb(f"sg{j}", [P, I], F32, s2) for j in range(2)]
            zz = [sb(f"zz{j}", [P, I], F32, s2) for j in range(2)]
            zh = [sb(f"zh{j}", [P, 2, P], F32R, s2) for j in range(2)]
            zl = [sb(f"zl{j}", [P, 2, P], F32R, s2) for j in range(2)]
            yo = [sb(f"yo{j}", [P, D], F32, s2) for j in range(2)]
            tix = sb("tix", [P, NT, TOPK], I32, s2)
            tiy = sb("tiy", [P, NT, TOPK], I32, s2)
            wk = sb("wk", [P, NT, TOPK], F32, s2)
            sidx = sb("sidx", [P, NT, TOPK], I32, s2)
            tok = sb("tok", [P, NT], I32, s2)
            tw = sb("tw", [P, NT, TOPK, 2], I32, s2)
            ids = sb("ids", [P, NU, 2], I32, s2)
            zero = sb("zero", [P, D], F32, s2)
            gidx = [sb(f"gidx{j}", [P, 1], I32, s2) for j in range(2)]
            aidx = [sb(f"aidx{j}", [P, 1], I32, s2) for j in range(2)]
            ule = sb("ule", [1, NU, E], F32, s2)
            upar = sb("upar", [1, NU], I32, s2)
            uexp = sb("uexp", [1, NU + 1], I32, s2)
            unext = sb("unext", [1, NU], I32, s2)

        with ExitStack() as s3:
            x3T = sb("x3T", [P, KD, T], F32, s3)
            cf = [sb(f"cf{j}", [P, KD, P], F32, s3) for j in range(2)]
            sf = [sb(f"sf{j}", [P, KD, P], F32, s3) for j in range(2)]
            maps = sb("maps", [P, 2, KD, 2, B], F32, s3)
            bsel = sb("bsel", [P, 2], F32, s3)
            tot = sb("tot", [P, KD, B], F32, s3)
            ones3 = sb("ones3", [P, P], F32, s3)
            zc = sb("zc", [P, 2, KD, B], F32, s3)
            zq = sb("zq", [P, 2, KD, B], F32, s3)
            part = sb("part", [P, 2], F32, s3)
            mean = sb("mean", [P, 2], F32, s3)
            var = sb("var", [P, 2], F32, s3)
            gain = sb("gain", [P, 2], F32, s3)
            amap = sb("amap", [P, 2, KD, B], F32, s3)
            asel = [sb(f"asel{j}", [P, KD, P], F32, s3) for j in range(2)]
            wb = sb("wb", [P, KD, D], F32, s3)
            aw = sb("aw", [P, KD, 136], F32, s3)
            bm = sb("bm", [P, D], F32, s3)
            b1 = sb("b1", [P, D], F32, s3)
            wbs = [sb(f"wbs{i}", [P, KD, D], F32R, s3) for i in range(2)]
            aws = [sb(f"aws{i}", [P, KD, 136], F32R, s3) for i in range(2)]
            bms = [sb(f"bms{i}", [P, D], F32R, s3) for i in range(2)]
            fh = [sb(f"fh{j}", [P, KD, P], F32R, s3) for j in range(2)]
            fl = [sb(f"fl{j}", [P, KD, P], F32R, s3) for j in range(2)]
            pr = [sb(f"pr{j}", [P, 16], F32, s3) for j in range(2)]
            prr = [sb(f"prr{j}", [P, 16], F32, s3) for j in range(2)]
            m8 = [sb(f"m8{j}", [P, 8], F32, s3) for j in range(2)]
            nm = [sb(f"nm{j}", [P, 8], F32, s3) for j in range(2)]
            lw = [sb(f"lw{j}", [P, LE], F32, s3) for j in range(2)]
            hw = [sb(f"hw{j}", [P, P], F32, s3) for j in range(2)]
            hth = [sb(f"hth{j}", [P, P], F32R, s3) for j in range(2)]
            htl = [sb(f"htl{j}", [P, P], F32R, s3) for j in range(2)]
            fo = [sb(f"fo{j}", [P, D], F32, s3) for j in range(2)]

        xn_d = nc.dram_tensor("xn_d", (T + P, D), F32, kind="Internal").ap()
        acc_d = nc.dram_tensor("acc_d", (T + P, D), F32, kind="Internal").ap()
        tab_d = nc.dram_tensor("tab_d", (NU * P, 2), I32, kind="Internal").ap()

        names = """cst_in x_in ctx_in watt_in wkv_in gw_in wraw_in w4_in konst gates
            lnstat lnvar lnsd lnrs
            xn_ready tx_done xnT_ready proj_done proj_out
            b_ready s_ready mx_ready dif_ready exp_done pt_done ptc_done pv_done rec_ready yn_ready
            yt_done ytc_done wo_done x1_done v_done v_ready
            s_hi s_split w_split w_hi n2 store_in0 store_in1 load_in0 load_in1 acc_out0 acc_out1 r_tx r_hi r_lo
            a_tx a_hi a_lo a_rt a_rtc lg_t a_gu a_sg a_z a_zt a_zh a_zl a_y a_x
            rsig rstep rmm tables scat tab0 ids_in pad_in
            g_in0 g_in1 gid aid u_tx u_hi u_lo u_gu u_sg u_z u_zt u_zh u_zl u_y u_yo add_out0 add_out1
            tstep xload nb_ready y3a w4_hi cpre tot_ps tot_sb
            l3 t_done x3_done d3 c3 m3 r3 mstep carried sel_ready utab sum_step bn_step bn_mm bn_act cstep y3p y3 y3t x3_sum
            konst3 w4_split l4 f_tx f_hi f_lo f_h f_base f_step f_exp f_hw f_ht f_hth f_htl f_out f_fin out_d0 out_d1 x4b""".split()
        sm = {n: sem(n) for n in names}

        block = ctx.enter_context(nc.Block())

        def carry(eng):
            eng.sem_inc(sm["carried"], 1)

        def split3(eng, dst, a, b, k_list, first, last):
            n, m = 0, 3 * len(k_list)
            for k in k_list:
                for ia, ib in ((0, 0), (0, 1), (1, 0)):
                    ins = eng.matmul(dst, a[ia](k), b[ib](k), start=(first and n == 0), stop=(last and n == m - 1),
                                     skip_group_check=True)
                    n += 1
            return ins

        @block.sync
        def _(sp):
            sp.dma_start(cst[:], cst_in).then_inc(sm["cst_in"], 16)
            x_v = x_in.rearrange("(t p) d -> p t d", p=P)
            c_v = ctxT_in.rearrange("(k p) n -> p k n", p=P)
            sp.dma_start(wkv[:].rearrange("p k g m -> p k (g m)"), wkv_in.rearrange("(k p) n -> p k n", p=P)).then_inc(sm["wkv_in"], 16)
            sp.dma_start(ctxT[:, :, 0:512], c_v[:, :, 0:512]).then_inc(sm["ctx_in"], 16)
            sp.dma_start(X[:, 0:4, :], x_v[:, 0:4, :]).then_inc(sm["x_in"], 16)
            sp.dma_start(wq[:].rearrange("p k g m -> p k (g m)"), wq_in.rearrange("(k p) n -> p k n", p=P)).then_inc(sm["watt_in"], 16)
            sp.wait_ge(sm["x_in"], 16)
            for q in range(1, 4):
                sp.wait_ge(sm["x_in"], 16 * q)
                sp.dma_start(X[:, 4 * q:4 * q + 4, :], x_v[:, 4 * q:4 * q + 4, :]).then_inc(sm["x_in"], 16)
                sp.wait_ge(sm["ctx_in"], 16 * q)
                sp.dma_start(ctxT[:, :, 512 * q:512 * q + 512], c_v[:, :, 512 * q:512 * q + 512]).then_inc(sm["ctx_in"], 16)
            sp.wait_ge(sm["watt_in"], 16)
            sp.dma_start(wo[:], wo_in.rearrange("g p n -> p g n")).then_inc(sm["watt_in"], 16)
            sp.dma_start(bo[:], bo_in).then_inc(sm["watt_in"], 16)
            sp.dma_start(wraw[:, 0], wall_in[E]).then_inc(sm["wraw_in"], 16)
            sp.wait_ge(sm["x1_done"], NT)
            sp.dma_start(gw[:], gate_in.rearrange("(k p) n -> p k n", p=P)).then_inc(sm["gw_in"], 16)

            def store(n, j):
                sp.wait_ge(sm["n2"], n + 1)
                sp.dma_start(xn_d[bass.ds(n * P, P), :], xn[j][:]).then_inc(sm[f"store_in{j}"], 16)

            with sp.Fori(0, NT // 2) as h:
                for j in range(2):
                    store(2 * h + j, j)

            sp.wait_ge(sm["s_split"], 1)
            sp.dma_start(wraw[:, 0], wall_in[0]).then_inc(sm["wraw_in"], 16)

            for j in range(2):
                sp.wait_ge(sm[f"store_in{j}"], 16 * (NT // 2))
            sp.wait_ge(sm["r_tx"], NT)

            def load(n, j):
                if holds(n, 2):
                    sp.wait_ge(sm["a_tx"], n - 1)
                sp.dma_start(xn[j][:], xn_d[bass.ds(n * P, P), :]).then_inc(sm[f"load_in{j}"], 16)

            def store_acc(n, j):
                sp.wait_ge(sm["a_x"], n + 1)
                sp.dma_start(acc_d[bass.ds(n * P, P), :], X[:, bass.ds(n, 1), :].rearrange("p a d -> p (a d)"))\
                    .then_inc(sm[f"acc_out{j}"], 16)

            def load_weights(f):
                sp.wait_ge(sm["wraw_in"], 16 * f + 16)
                src = wall_in[f] if isinstance(f, int) else wall_in[bass.ds(f, 1)].rearrange("a p n -> p (a n)")
                return sp.dma_start(wraw[:, f % 2] if isinstance(f, int) else
                                    wraw[:, bass.ds(f % 2, 1), :].rearrange("p a n -> p (a n)"), src)\
                    .then_inc(sm["wraw_in"], 16)

            for n in range(4):
                load(n, n % 2)
            sp.wait_ge(sm["utab"], 1)
            load_weights(1)
            with sp.Fori(2, NT // 2) as h:
                for j in range(2):
                    load(2 * h + j, j)
                    store_acc(2 * h + j - 4, j)
            sp.wait_ge(sm["w_split"], 1)
            load_weights(2)
            for n in range(NT - 4, NT):
                store_acc(n, n % 2)
            with sp.Fori(3, E) as f:
                sp.wait_ge(sm["w_split"], f - 1)
                load_weights(f)
            for j in range(2):
                sp.wait_ge(sm[f"add_out{j}"], 16 * (NU // 2))
            a_v = acc_d[0:T, :].rearrange("(t p) d -> p t d", p=P)
            for q in range(4):
                if q:
                    sp.wait_ge(sm["xload"], 16 * q)
                sp.dma_start(X[:, 4 * q:4 * q + 4, :], a_v[:, 4 * q:4 * q + 4, :]).then_inc(sm["xload"], 16)
            sp.dma_start(wb[:], wb_in.rearrange("(k p) n -> p k n", p=P)).then_inc(sm["w4_in"], 16)
            sp.dma_start(aw[:], aw_in.rearrange("(k p) n -> p k n", p=P)).then_inc(sm["w4_in"], 16)
            sp.dma_start(bm[:], bm_in).then_inc(sm["w4_in"], 16)
            sp.dma_start(b1[:], b1_in).then_inc(sm["w4_in"], 16)

            def store_out(n, j):
                sp.wait_ge(sm["f_out"], n + 1)
                sp.dma_start(out[bass.ds(n * P, P), :], fo[j][:]).then_inc(sm[f"out_d{j}"], 16)

            with sp.Fori(0, NT // 2) as h:
                for j in range(2):
                    store_out(2 * h + j, j)
            for j in range(2):
                sp.wait_ge(sm[f"out_d{j}"], 16 * (NT // 2))

        @block.gpsimd
        def _(pool):
            kc = [0]

            def k0(ins):
                kc[0] += 1
                ins.then_inc(sm["konst"], 1)
                pool.wait_ge(sm["konst"], kc[0])

            k0(pool.memset(ident[:], 0.0))
            k0(pool.memset(eps[:], EPS))
            k0(pool.memset(wide[:], 0.0))
            k0(pool.affine_select(wide[:], wide[:], [[-1, 390]], ALU.not_equal, 1.0, base=P + 3, channel_multiplier=1))
            k0(pool.memset(hmask[:], 1.0))
            for j in range(2):
                k0(pool.memset(vblk[j][:], 0.0))
            k0(pool.affine_select(ident[:], ident[:], [[-1, P]], ALU.not_equal, 1.0, base=0, channel_multiplier=1))
            k0(pool.affine_select(hmask[:], hmask[:], [[-HD, NKV]], ALU.is_ge, 0.0, base=0, channel_multiplier=1))
            for j in range(2):
                k0(pool.memset(vblk[j][0:S, :, 32:33], 1.0))
                k0(pool.memset(vblk[j][S:P, :, 33:34], 1.0))
            k0(pool.affine_select(hmask[:], hmask[:], [[HD, NKV]], ALU.is_ge, 0.0, base=HD - 1, channel_multiplier=-1))
            pool.wait_ge(sm["gates"], 1)
            pool.wait_ge(sm["watt_in"], 48)
            k0(pool.tensor_scalar(bo[:], bo[:], tg[:, 0:1], None, ALU.mult))
            pool.wait_ge(sm["proj_out"], 24)

            def prepare(b, j):
                if holds(b, 2):
                    pool.wait_ge(sm["s_ready"], 2 * b - 2)
                    pool.wait_ge(sm["v_done"], b - 1)
                pool.tensor_copy(qTb[j][:], QT[:, :, bass.ds(b * S, S)]).then_inc(sm["b_ready"], 1)
                kv = KT[:, bass.ds(b * S, S)].unsqueeze(1).broadcast_to([P, NKV, S])
                pool.tensor_tensor(kblk[j][:], kv, hmask[:].unsqueeze(2).broadcast_to([P, NKV, S]),
                                   ALU.mult).then_inc(sm["b_ready"], 1)
                pool.tensor_copy(vTb[j][:], VT[:, bass.ds(b * S, S)].unsqueeze(1).broadcast_to([P, 2, S]))\
                    .then_inc(sm["b_ready"], 1)

            def add_bias(t):
                pool.tensor_tensor(X[:, bass.ds(t, 1), :], X[:, bass.ds(t, 1), :], bo[:].unsqueeze(1), ALU.add)\
                    .then_inc(sm["x4b"], 1)

            for b in range(2):
                prepare(b, b)
            add_bias(0)
            with pool.Fori(1, B // 2) as h:
                for j in range(2):
                    prepare(2 * h + j, j)
                add_bias(h)

            pool.wait_ge(sm["x1_done"], NT)
            k0(pool.memset(zero[:], 0.0))
            k0(pool.memset(ids[:], 0))
            k0(pool.iota(ids[:, :, 0], [[0, NU]], base=T, channel_multiplier=1))
            k0(pool.memset(lower[:], 1.0))
            k0(pool.memset(onesm[:], 1.0))
            k0(pool.memset(ones16[:], 1.0))
            k0(pool.iota(tok[:], [[P, NT]], base=0, channel_multiplier=1))
            k0(pool.iota(uiota[:], [[1, NU]], base=0, channel_multiplier=0, allow_small_or_imprecise_dtypes=True))
            k0(pool.memset(sc[:, :, E:24], -BIG))
            k0(pool.affine_select(lower[:], lower[:], [[1, P]], ALU.is_gt, 0.0, base=0, channel_multiplier=-1))
            pool.dma_start(tab_d.rearrange("(p u) o -> p (u o)", p=P), ids[:].rearrange("p u o -> p (u o)"))\
                .then_inc(sm["tab0"], 16)
            pool.dma_start(xn_d[T:T + P, :], zero[:]).then_inc(sm["pad_in"], 16)
            pool.dma_start(acc_d[T:T + P, :], zero[:]).then_inc(sm["pad_in"], 16)


            pool.wait_ge(sm["s_hi"], 1)
            pool.tensor_tensor(wl[:, 2, :], wraw[:, 0], wh[:, 2, :].bitcast(F32), ALU.subtract).then_inc(sm["s_split"], 1)

            pool.wait_ge(sm["tab0"], 16)
            pool.wait_ge(sm["tables"], 1)
            for t in range(NT):
                for k in range(TOPK):
                    pool.indirect_dma_start(tab_d, bass.IndirectOffsetOnAxis(ap=tix[:, t, k:k + 1], axis=0),
                                            tw[:, t, k, :], None).then_inc(sm["scat"], 16)
            pool.wait_ge(sm["scat"], 16 * NT * TOPK)
            pool.dma_start(ids[:].rearrange("p u o -> p (u o)"), tab_d.rearrange("(p u) o -> p (u o)", p=P))\
                .then_inc(sm["ids_in"], 16)
            pool.wait_ge(sm["ids_in"], 16)
            pool.wait_ge(sm["pad_in"], 32)

            def gather(n, j):
                if holds(n, 2):
                    pool.wait_ge(sm[f"g_in{j}"], 16 * (n // 2))
                    pool.wait_ge(sm["u_tx"], n - 1)
                else:
                    pool.wait_ge(sm["a_tx"], NT - 1 + n)
                pool.tensor_copy(gidx[j][:], ids[:, bass.ds(n, 1), 0]).then_inc(sm["gid"], 1)
                pool.wait_ge(sm["gid"], n + 1)
                carry(pool)
                pool.indirect_dma_start(xn[j][:], None, xn_d, bass.IndirectOffsetOnAxis(ap=gidx[j][:, 0:1], axis=0))\
                    .then_inc(sm[f"g_in{j}"], 16)

            def add_results(n, j):
                if holds(n, 2):
                    pool.wait_ge(sm[f"add_out{j}"], 16 * (n // 2))
                pool.tensor_copy(aidx[j][:], ids[:, bass.ds(n, 1), 0]).then_inc(sm["aid"], 1)
                pool.wait_ge(sm["aid"], n + 1)
                pool.wait_ge(sm["u_yo"], n + 1)
                if holds(n, 1):
                    pool.wait_ge(sm[f"add_out{1 - j}"], 16 * ((n + 1) // 2))
                carry(pool)
                pool.indirect_dma_start(acc_d, bass.IndirectOffsetOnAxis(ap=aidx[j][:, 0:1], axis=0), yo[j][:], None,
                                        compute_op=ALU.add).then_inc(sm[f"add_out{j}"], 16)

            for n in range(4):
                gather(n, n % 2)
            for j in range(2):
                pool.wait_ge(sm[f"acc_out{j}"], 16 * (NT // 2))
            with pool.Fori(2, NU // 2) as h:
                for j in range(2):
                    gather(2 * h + j, j)
                    add_results(2 * h + j - 4, j)
            for n in range(NU - 4, NU):
                add_results(n, n % 2)

            for j in range(2):
                pool.wait_ge(sm[f"add_out{j}"], 16 * (NU // 2))
            kd = [0]

            def k3(ins, wait=True):
                kd[0] += 1
                ins.then_inc(sm["konst3"], 1)
                pool.wait_ge(sm["konst3"], kd[0])

            k3(pool.memset(ones3[:], 1.0))
            k3(pool.memset(bsel[:], 1.0))
            k3(pool.affine_select(bsel[:], bsel[:], [[-S, 2]], ALU.is_ge, 0.0, base=0, channel_multiplier=1))
            k3(pool.affine_select(bsel[:], bsel[:], [[S, 2]], ALU.is_ge, 0.0, base=S - 1, channel_multiplier=-1))
            k3(pool.memset(pr[0][:], -1.0))
            k3(pool.memset(pr[1][:], -1.0))

            def rest(t, j):
                pool.wait_ge(sm["c3"], t + 1)
                if holds(t, 2):
                    pool.wait_ge(sm["m3"], t - 1)
                pool.tensor_tensor(sf[j][:], x3T[:, :, bass.ds(t * P, P)], cf[j][:], ALU.subtract).then_inc(sm["d3"], 1)

            for t in range(2):
                rest(t, t)
            with pool.Fori(1, NT // 2) as h:
                for j in range(2):
                    rest(2 * h + j, j)

            for n, (raw, parts) in enumerate(((wb, wbs), (aw, aws), (bm, bms))):
                pool.wait_ge(sm["w4_hi"], n + 1)
                pool.tensor_tensor(parts[1][:], raw[:], parts[0][:].bitcast(F32), ALU.subtract).then_inc(sm["w4_split"], 1)
            k3(pool.tensor_scalar(b1[:], b1[:], tg[:, 3:4], None, ALU.mult))

            def blend(h):
                t = 2 * h
                mk = ctxT[:, :, bass.ds(t * P, P)].rearrange("p k (b c) -> p k b c", c=S)
                av = asel[0][:].rearrange("p k (b c) -> p k b c", c=S)
                if holds(t, 2):
                    pool.wait_ge(sm["y3"], t - 1)
                pool.tensor_tensor(av, mk, amap[:, 1, :, bass.ds(2 * t, 2)].unsqueeze(3).broadcast_to([P, KD, 2, S]),
                                   ALU.mult).then_inc(sm["y3p"], 1)
                pool.wait_ge(sm["y3p"], t + 1)
                pool.tensor_tensor(av, av, amap[:, 0, :, bass.ds(2 * t, 2)].unsqueeze(3).broadcast_to([P, KD, 2, S]),
                                   ALU.add).then_inc(sm["y3p"], 1)

            pool.wait_ge(sm["bn_step"], 14)
            blend(0)
            with pool.Fori(1, NT // 2) as h:
                blend(h)

            def add_bias4(t):
                pool.wait_ge(sm["l4"], t + 1)
                pool.tensor_tensor(X[:, bass.ds(t, 1), :], X[:, bass.ds(t, 1), :], b1[:].unsqueeze(1), ALU.add)\
                    .then_inc(sm["cpre"], 1)

            with pool.Fori(0, NT) as t:
                add_bias4(t)

        @block.scalar
        def _(act):
            act.wait_ge(sm["cst_in"], 16)
            act.activation(tg[:], cst[:, C_GATE:C_GATE + 4], ACT.Tanh).then_inc(sm["gates"], 1)

            def sqrt(lo, n, count):
                act.wait_ge(sm["lnvar"], 7 * count)
                act.activation(sd[:, bass.ds(lo, n)], va[:, bass.ds(lo, n)],
                               ACT.Sqrt, bias=eps[:, 0:1]).then_inc(sm["lnsd"], 1)

            act.wait_ge(sm["konst"], 2)

            def proj_out(s, r):
                act.wait_ge(sm["proj_done"], 6 * s + r + 1)
                cols = bass.ds(s * 512, 512)
                dst, at, scale = ((KT[:, cols], C_BK, 1.0), (VT[:, cols], C_BV, 1.0))[r] if r < 2 else \
                    (QT[:, r - 2, cols], C_BQ + r - 2, 0.25)
                act.activation(dst, bank[r % 2][:], ACT.Identity, bias=cst[:, at:at + 1], scale=scale)\
                    .then_inc(sm["proj_out"], 1)

            def stage1a(s):
                if holds(s, 1):
                    sqrt(4 * s, 4, s + 1)
                for r in range(2):
                    proj_out(s, r)
                if not holds(s, 1):
                    sqrt(4 * s, 4, s + 1)
                for i in range(4):
                    t = 4 * s + i
                    act.wait_ge(sm["tx_done"], t + 1)
                    if i == 0 and holds(s, 1):
                        act.wait_ge(sm["proj_done"], 6 * s)
                    act.copy(xnT[:, :, i * P:(i + 1) * P],
                             bank[2 + i % 2][:].rearrange("p (k n) -> p k n", k=KD)).then_inc(sm["xnT_ready"], 1)
                for r in range(2, 6):
                    proj_out(s, r)

            stage1a(0)
            with act.Fori(1, 4) as s:
                stage1a(s)

            def exps(u, j):
                act.wait_ge(sm["dif_ready"], u + 1)
                if holds(u, 2):
                    act.wait_ge(sm["pt_done"], u - 1)
                act.activation(prob[j][:], dif[j][:].rearrange("p h k -> p (h k)"), ACT.Exp).then_inc(sm["exp_done"], 1)

            def prob_out(u, j):
                act.wait_ge(sm["pt_done"], u + 1)
                if holds(u, 2):
                    act.wait_ge(sm["pv_done"], u - 1)
                act.copy(probT[j][:].rearrange("p a q -> p (a q)"), bank[2 + j][:]).then_inc(sm["ptc_done"], 1)

            def v_out(b, j):
                act.wait_ge(sm["v_done"], b + 1)
                if holds(b, 2):
                    act.wait_ge(sm["pv_done"], 2 * b - 2)
                v = bank[5][:, 0:P].rearrange("p (a h d) -> p a h d", a=4, h=2)
                act.copy(vblk[j][0:S, :, 0:HD], v[0:S, :, 0, :]).then_inc(sm["v_ready"], 1)
                act.copy(vblk[j][S:P, :, HD:2 * HD], v[S:P, :, 1, :]).then_inc(sm["v_ready"], 1)

            def yT_out(u, i):
                act.wait_ge(sm["yt_done"], u + 1)
                if i == 0 and holds(u, 4):
                    act.wait_ge(sm["wo_done"], u // 4)
                g, b = 2 * (i % 2), i // 2
                act.copy(yT[:, g:g + 2, b * S:(b + 1) * S],
                         bank[7][:, 0:P].rearrange("p (g q) -> p g q", g=2))\
                    .then_inc(sm["ytc_done"], 1)

            def att_act(u, i):
                if below(u, 2 * B - 1):
                    exps(u + 1, (i + 1) % 2)
                if below(u, 2 * B):
                    prob_out(u, i % 2)
                if i % 2 == 1 and below(u, 2 * B - 1):
                    v_out((u + 1) // 2, (i + 1) // 2 % 2)
                if holds(u, 2) and below(u, 2 * B + 2):
                    yT_out(u - 2, (i - 2) % 4)

            v_out(0, 0)
            exps(0, 0)
            for i in range(4):
                att_act(i, i)
            with act.Fori(1, NT - 1) as t:
                for i in range(4):
                    att_act(4 * t + i, i)
            for u in range(2 * B - 4, 2 * B + 2):
                att_act(u, u % 4)

            def hi(p, n, j):
                act.wait_ge(sm[p + "tx"], n + 1)
                if holds(n, 2):
                    act.wait_ge(sm[p + "gu"], n - 1)
                act.copy(xh[j][:].rearrange("p k n -> p (k n)"), bank[j][:]).then_inc(sm[p + "hi"], 1)

            def silu(p, n, j):
                act.wait_ge(sm[p + "gu"], n + 1)
                if holds(n, 2):
                    act.wait_ge(sm[p + "z"], n - 1)
                act.activation(sg[j][:], bank[2 + j][:, 0:I], ACT.Silu).then_inc(sm[p + "sg"], 1)

            def z_hi(p, n, j):
                act.wait_ge(sm[p + "zt"], n + 1)
                if holds(n, 2):
                    act.wait_ge(sm[p + "y"], n - 1)
                act.copy(zh[j][:].rearrange("p k n -> p (k n)"), bank[4][:, 0:I]).then_inc(sm[p + "zh"], 1)

            def logits_out(n, j):
                act.wait_ge(sm["a_rt"], n + 1)
                if holds(n, 2):
                    act.wait_ge(sm["lg_t"], n - 1)
                act.copy(lgT[j][:], bank[4 + j][0:E, 0:P]).then_inc(sm["a_rtc"], 1)

            def y_out(n, j):
                act.wait_ge(sm["u_y"], n + 1)
                if holds(n, 2):
                    act.wait_ge(sm[f"add_out{j}"], 16 * (n // 2))
                act.activation(yo[j][:], bank[5 + j][:], ACT.Copy,
                               scale=ids[:, bass.ds(n, 1), 1].bitcast(F32)).then_inc(sm["u_yo"], 1)

            sqrt(0, NT, 5)
            act.wait_ge(sm["x1_done"], NT)
            act.wait_ge(sm["wraw_in"], 16)
            act.copy(wh[:, 2, :], wraw[:, 0]).then_inc(sm["s_hi"], 1)

            def route_act(n, j):
                if below(n, NT - 1):
                    r_hi(n + 1, 1 - j)
                logits_out(n, j)

            def r_hi(n, j):
                act.wait_ge(sm["r_tx"], n + 1)
                if holds(n, 2):
                    act.wait_ge(sm["a_rt"], n - 1)
                act.copy(xh[j][:].rearrange("p k n -> p (k n)"), bank[j][:]).then_inc(sm["r_hi"], 1)

            r_hi(0, 0)
            for n in range(2):
                route_act(n, n)
            with act.Fori(1, (NT - 2) // 2) as h:
                for j in range(2):
                    route_act(2 * h + j, j)
            for n in range(NT - 2, NT):
                route_act(n, n % 2)
            act.wait_ge(sm["lg_t"], NT)
            act.activation(sc[:, :, 0:E], bank[7][:, 0:NT * E].rearrange("p (t e) -> p t e", e=E), ACT.Sigmoid)\
                .then_inc(sm["rsig"], 1)

            def hi_parts(f):
                act.wait_ge(sm["wraw_in"], 16 * f + 32)
                for half in range(2):
                    cols = slice(half * WALL // 2, (half + 1) * WALL // 2)
                    act.copy(wh[:, bass.ds(f % 3, 1), cols].rearrange("p a n -> p (a n)"),
                             wraw[:, bass.ds(f % 2, 1), cols].rearrange("p a n -> p (a n)")).then_inc(sm["w_hi"], 1)

            def shared_act(n, j):
                if below(n, NT - 1):
                    hi("a_", n + 1, 1 - j)
                if holds(n, 1) and below(n, NT + 1):
                    z_hi("a_", n - 1, 1 - j)
                if below(n, NT):
                    silu("a_", n, j)

            act.wait_ge(sm["a_rt"], NT)
            hi("a_", 0, 0)
            for n in range(2):
                shared_act(n, n)
            hi_parts(0)
            with act.Fori(1, (NT - 2) // 2) as h:
                for j in range(2):
                    shared_act(2 * h + j, j)
            for n in range(NT - 2, NT + 1):
                shared_act(n, n % 2)
                if n == NT - 2:
                    hi_parts(1)

            def split_hi(n):
                nxt = act.value_load(unext[0:1, bass.ds(n, 1)], min_val=0, max_val=E - 1)
                with act.If(nxt > 0):
                    hi_parts(nxt)

            def unit_act(n, j):
                if holds(n, 2) and below(n, NU + 2):
                    y_out(n - 2, j)
                if below(n, NU - 1):
                    hi("u_", n + 1, 1 - j)
                if holds(n, 1) and below(n, NU + 1):
                    z_hi("u_", n - 1, 1 - j)
                if holds(n, 1) and below(n, NU):
                    split_hi(n)
                if below(n, NU):
                    silu("u_", n, j)

            act.wait_ge(sm["utab"], 1)
            act.wait_ge(sm["a_gu"], NT)
            act.wait_ge(sm["ids_in"], 16)
            hi("u_", 0, 0)
            for n in range(2):
                unit_act(n, n)
            with act.Fori(1, (NU - 2) // 2) as h:
                for j in range(2):
                    unit_act(2 * h + j, j)
            for n in range(NU - 2, NU + 2):
                unit_act(n, n % 2)

            def x3n(t, j):
                act.wait_ge(sm["nb_ready"], t // 4 + 1)
                if holds(t, 2):
                    act.wait_ge(sm["t_done"], t - 1)
                act.activation(xn[j][:], X[:, bass.ds(t, 1), :].rearrange("p a d -> p (a d)"), ACT.Identity,
                               bias=nb[:, bass.ds(t, 1)], scale=rs[:, bass.ds(t, 1)]).then_inc(sm["l3"], 1)

            def x3_out(t, j):
                act.wait_ge(sm["t_done"], t + 1)
                act.copy(x3T[:, :, bass.ds(t * P, P)], bank[j][:].rearrange("p (k n) -> p k n", k=KD))\
                    .then_inc(sm["x3_done"], 1)
                act.wait_ge(sm["tot_ps"], t + 1)
                act.copy(tot[:, :, bass.ds(2 * t, 2)], bank[6 + j][:, 0:8].rearrange("p (k b) -> p k b", k=KD))\
                    .then_inc(sm["tot_sb"], 1)

            def group3(q):
                for i in range(4):
                    if i == 2 and below(q, 3):
                        sqrt(4 * q + 4, 4, q + 7)
                    if i < 2 or below(q, 3):
                        x3n(4 * q + i + 2, i % 2)
                    x3_out(4 * q + i, i % 2)

            sqrt(0, 4, 6)
            x3n(0, 0)
            x3n(1, 1)
            with act.Fori(0, 3) as q:
                group3(q)
            group3(3)
            act.wait_ge(sm["w4_in"], 64)
            for raw, parts in ((wb, wbs), (aw, aws), (bm, bms)):
                act.copy(parts[0][:], raw[:]).then_inc(sm["w4_hi"], 1)
            act.wait_ge(sm["bn_step"], 8)
            act.activation(gain[:], var[:], ACT.Sqrt, bias=eps[:, 0:1]).then_inc(sm["bn_act"], 1)
            act.wait_ge(sm["bn_step"], 13)
            act.activation(amap[:], zc[:], ACT.Sigmoid).then_inc(sm["bn_act"], 1)

            def blend_odd(h):
                t = 2 * h + 1
                if holds(h, 1):
                    act.wait_ge(sm["y3"], t - 1)
                for k in range(KD):
                    for b in range(2):
                        ins = act.activation(asel[1][:, k, b * S:(b + 1) * S],
                                             ctxT[:, k, bass.ds(t * P + b * S, S)], ACT.Identity,
                                             bias=amap[:, 0, k, bass.ds(2 * t + b, 1)],
                                             scale=amap[:, 1, k, bass.ds(2 * t + b, 1)])
                ins.then_inc(sm["y3a"], 1)

            act.wait_ge(sm["bn_step"], 14)
            blend_odd(0)
            with act.Fori(1, NT // 2) as h:
                blend_odd(h)

            sqrt(0, NT, 10)

            def f_hi(n, j):
                act.wait_ge(sm["f_tx"], n + 1)
                if holds(n, 2):
                    act.wait_ge(sm["f_base"], n - 1)
                act.copy(fh[j][:].rearrange("p k n -> p (k n)"), bank[j][:]).then_inc(sm["f_hi"], 1)

            def f_exp(n, j):
                act.wait_ge(sm["f_step"], NF * n + 2)
                act.activation(pr[j][:, 0:LE], bank[4 + j][:, P:P + LE], ACT.Exp, bias=nm[j][:, 0:1],
                               accum_out=nm[j][:, 1:2]).then_inc(sm["f_exp"], 1)

            def f_hth(n, j):
                act.wait_ge(sm["f_ht"], n + 1)
                if holds(n, 2):
                    act.wait_ge(sm["f_fin"], n - 1)
                act.copy(hth[j][:], bank[6][:, 0:P]).then_inc(sm["f_hth"], 1)

            def lora_act(n, j):
                if below(n, NT - 1):
                    f_hi(n + 1, 1 - j)
                if holds(n, 1) and below(n, NT + 1):
                    f_hth(n - 1, 1 - j)
                if below(n, NT):
                    f_exp(n, j)

            f_hi(0, 0)
            for n in range(2):
                lora_act(n, n)
            with act.Fori(1, (NT - 2) // 2) as h:
                for j in range(2):
                    lora_act(2 * h + j, j)
            for n in range(NT - 2, NT + 1):
                lora_act(n, n % 2)

        @block.vector
        def _(dve):
            def ln_stats(t):
                dve.bn_stats(stats[:, bass.ds(t, 1), :].rearrange("p a s -> p (a s)"),
                             X[:, bass.ds(t, 1), :].rearrange("p a d -> p (a d)")).then_inc(sm["lnstat"], 1)

            def ln_scale(lo, n, tiles, count):
                dve.wait_ge(sm["lnstat"], tiles)
                at = bass.ds(lo, n)
                m_e, v_e, m_o, v_o = (stats[:, at, c:c + 1].rearrange("p t o -> p (t o)") for c in (1, 2, 4, 5))
                for n_, ins in enumerate((
                        lambda: dve.tensor_tensor(mu[:, at], m_e, m_o, ALU.add),
                        lambda: dve.tensor_scalar(mu[:, at], mu[:, at], 0.5, None, ALU.mult),
                        lambda: dve.tensor_tensor(dm[:, at], m_e, m_o, ALU.subtract),
                        lambda: dve.tensor_tensor(dm[:, at], dm[:, at], dm[:, at], ALU.mult),
                        lambda: dve.tensor_tensor(va[:, at], v_e, v_o, ALU.add),
                        lambda: dve.tensor_scalar(va[:, at], va[:, at], 1.0 / D, None, ALU.mult),
                        lambda: dve.scalar_tensor_tensor(va[:, at], dm[:, at], 0.25, va[:, at], ALU.mult, ALU.add))):
                    ins().then_inc(sm["lnvar"], 1)
                    dve.wait_ge(sm["lnvar"], 7 * count - 6 + n_)
                dve.wait_ge(sm["lnsd"], count)
                dve.reciprocal(rs[:, at], sd[:, at]).then_inc(sm["lnrs"], 1)
                dve.wait_ge(sm["lnrs"], count)

            def ln_apply(t, j, done):
                return dve.tensor_scalar(xn[j][:], X[:, bass.ds(t, 1), :].rearrange("p a d -> p (a d)"),
                                         mu[:, bass.ds(t, 1)],
                                         rs[:, bass.ds(t, 1)], ALU.subtract, ALU.mult).then_inc(sm[done], 1)

            cc = [0]

            def c(ins):
                cc[0] += 1
                ins.then_inc(sm["cstep"], 1)
                dve.wait_ge(sm["cstep"], cc[0])

            dve.wait_ge(sm["cst_in"], 16)
            dve.wait_ge(sm["konst"], 4)
            for ch in range(2):
                for w in range(7):
                    tap = cst[:, C_CONV + 7 * ch + w:C_CONV + 7 * ch + w + 1]
                    if w == 0:
                        c(dve.tensor_scalar(band[:, ch, :], wide[:, 0:384], tap, None, ALU.mult))
                    else:
                        c(dve.scalar_tensor_tensor(band[:, ch, :], wide[:, w:w + 384], tap, band[:, ch, :],
                                                   ALU.mult, ALU.add))
            dve.tensor_scalar(cst[:, C_BQ:C_BQ + NG], cst[:, C_BQ:C_BQ + NG], 0.25, None, ALU.mult).then_inc(sm["sum_step"], 1)

            def stage1a(s):
                dve.wait_ge(sm["x_in"], 16 * s + 16)
                for i in range(4):
                    ln_stats(4 * s + i)
                ln_scale(4 * s, 4, 4 * s + 4, s + 1)
                for i in range(4):
                    t = 4 * s + i
                    if holds(t, 2):
                        dve.wait_ge(sm["tx_done"], t - 1)
                    ln_apply(t, i % 2, "xn_ready")

            def choose(g, k, blk, rnd, find=True, take=True):
                c0 = 10 * g + 2 * rnd
                src = ctxT[:, k, bass.ds(blk * 512, 512)] if isinstance(k, int) else \
                    ctxT[:, bass.ds(k, 1), bass.ds(blk * 512, 512)].rearrange("p a n -> p (a n)")
                src = src.rearrange("p (b c) -> p b c", c=S)
                if find and rnd == 0:
                    if holds(g, 1):
                        dve.wait_ge(sm["tstep"], 10 * g)
                    dve.tensor_scalar(neg[:, :, ::-1], src, -1.0, None, ALU.mult).then_inc(sm["mstep"], 1)
                    dve.wait_ge(sm["mstep"], g + 1)
                    carry(dve)
                if find:
                    for b in range(8):
                        ins = dve.max(best[:, b, :], neg[:, b, :])
                    ins.then_inc(sm["tstep"], 1)
                if not take:
                    return
                dve.wait_ge(sm["tstep"], c0 + 1)
                if rnd < 3:
                    carry(dve)
                if rnd == 3:
                    dve.memset(best[:, :, NSUB - 24:8], -BIG).then_inc(sm["tstep"], 1)
                    c0 += 1
                    dve.wait_ge(sm["tstep"], c0 + 1)
                    carry(dve)
                for b in range(8):
                    ins = dve.match_replace(neg[:, b, :], best[:, b, :], neg[:, b, :], -BIG)
                ins.then_inc(sm["tstep"], 1)
                dve.wait_ge(sm["tstep"], c0 + 2)
                if rnd < 3:
                    carry(dve)
                if rnd == 3:
                    dve.tensor_scalar(src, neg[:, :, ::-1], -1e38, None, ALU.is_lt).then_inc(sm["tstep"], 1)

            stage1a(0)
            with dve.Fori(1, 4) as s:
                stage1a(s)
                dve.wait_ge(sm["proj_done"], 6 * s)
                for rnd in range(4):
                    choose(s - 1, 0, s - 1, rnd)

            def shift(u, j):
                dve.wait_ge(sm["s_ready"], u + 1)
                sc_v = bank[j][:].rearrange("p (h k) -> p h k", h=NKV)
                dve.tensor_reduce(mx[j][:], sc_v, AX, ALU.max).then_inc(sm["mx_ready"], 1)
                dve.wait_ge(sm["mx_ready"], u + 1)
                if holds(u, 2):
                    dve.wait_ge(sm["exp_done"], u - 1)
                dve.tensor_tensor(dif[j][:], sc_v, mx[j][:].unsqueeze(2).broadcast_to([P, NKV, S]), ALU.subtract)\
                    .then_inc(sm["dif_ready"], 1)

            def normalise(u, j):
                dve.wait_ge(sm["pv_done"], u + 1)
                o = bank[6][:, 0:136].rearrange("p (a n) -> p a n", a=4)
                dve.reciprocal(rec[j][:], o[:, :, 32:34]).then_inc(sm["rec_ready"], 1)
                dve.wait_ge(sm["rec_ready"], u + 1)
                if holds(u, 2):
                    dve.wait_ge(sm["yt_done"], u - 1)
                dve.tensor_tensor(yn[j][:], o[:, :, 0:32].rearrange("p a (h d) -> p a h d", h=2),
                                  rec[j][:].unsqueeze(3).broadcast_to([P, 4, 2, HD]), ALU.mult)\
                    .then_inc(sm["yn_ready"], 1)

            def residual1(t):
                dve.wait_ge(sm["wo_done"], t + 1)
                dve.wait_ge(sm["x4b"], t + 1)
                dve.scalar_tensor_tensor(X[:, bass.ds(t, 1), :].rearrange("p a d -> p (a d)"), bank[4][:], tg[:, 0:1],
                                         X[:, bass.ds(t, 1), :].rearrange("p a d -> p (a d)"), ALU.mult, ALU.add)\
                    .then_inc(sm["x1_done"], 1)
                dve.wait_ge(sm["x1_done"], t + 1)
                ln_stats(t)

            def att_dve(u, i):
                if below(u, 2 * B - 1):
                    shift(u + 1, (i + 1) % 2)
                if holds(u, 1) and below(u, 2 * B + 1):
                    normalise(u - 1, (i - 1) % 2)
                if i == 3 and holds(u, 4):
                    residual1(u // 4 - 1)

            dve.wait_ge(sm["gates"], 1)
            shift(0, 0)
            for i in range(4):
                att_dve(i, i)
            with dve.Fori(1, NT - 1) as t:
                for i in range(4):
                    if below(t, NT):
                        shift(4 * t + i + 1, (i + 1) % 2)
                        normalise(4 * t + i - 1, (i - 1) % 2)
                        if i == 3:
                            residual1(t - 1)
            for u in range(2 * B - 4, 2 * B + 1):
                att_dve(u, u % 4)
            residual1(NT - 1)

            dve.wait_ge(sm["x1_done"], NT)
            ln_scale(0, NT, 2 * NT, 5)
            for n, (o, i) in enumerate(((gwh, gw), (gwl, gw))):
                dve.wait_ge(sm["gw_in"], 16)
                if n == 0:
                    dve.tensor_copy(gwh[:], gw[:]).then_inc(sm["sum_step"], 1)
                    dve.wait_ge(sm["sum_step"], 2)
                else:
                    dve.tensor_tensor(gwl[:], gw[:], gwh[:].bitcast(F32), ALU.subtract).then_inc(sm["sum_step"], 1)

            def x2n(n, j):
                if holds(n, 2):
                    dve.wait_ge(sm["r_tx"], n - 1)
                    dve.wait_ge(sm[f"store_in{j}"], 16 * (n // 2))
                ln_apply(n, j, "n2")

            def lo(p, n, j):
                dve.wait_ge(sm[p + "hi"], n + 1)
                dve.tensor_tensor(xl[j][:].rearrange("p k n -> p (k n)"), bank[j][:],
                                  xh[j][:].rearrange("p k n -> p (k n)").bitcast(F32), ALU.subtract)\
                    .then_inc(sm[p + "lo"], 1)

            def z_lo(p, n, j):
                dve.wait_ge(sm[p + "zh"], n + 1)
                dve.tensor_tensor(zl[j][:].rearrange("p k n -> p (k n)"), bank[4][:, 0:I],
                                  zh[j][:].rearrange("p k n -> p (k n)").bitcast(F32), ALU.subtract)\
                    .then_inc(sm[p + "zl"], 1)

            def inner(p, n, j):
                dve.wait_ge(sm[p + "sg"], n + 1)
                if holds(n, 2):
                    dve.wait_ge(sm[p + "zt"], n - 1)
                dve.tensor_tensor(zz[j][:], bank[2 + j][:, I:2 * I], sg[j][:], ALU.mult).then_inc(sm[p + "z"], 1)

            def shared_out(n, j):
                dve.wait_ge(sm["a_y"], n + 1)
                xt = X[:, bass.ds(n, 1), :].rearrange("p a d -> p (a d)")
                dve.scalar_tensor_tensor(xt, bank[5 + j][:], tg[:, 2:3], xt, ALU.mult, ALU.add).then_inc(sm["a_x"], 1)

            def route_dve(n, j):
                if below(n, NT - 2):
                    x2n(n + 2, j)
                if below(n, NT - 1):
                    r_lo(n + 1, 1 - j)

            def r_lo(n, j):
                dve.wait_ge(sm["r_hi"], n + 1)
                dve.tensor_tensor(xl[j][:].rearrange("p k n -> p (k n)"), bank[j][:],
                                  xh[j][:].rearrange("p k n -> p (k n)").bitcast(F32), ALU.subtract)\
                    .then_inc(sm["r_lo"], 1)

            x2n(0, 0)
            x2n(1, 1)
            r_lo(0, 0)
            for n in range(2):
                route_dve(n, n)
            with dve.Fori(1, (NT - 2) // 2) as h:
                for j in range(2):
                    route_dve(2 * h + j, j)
            for n in range(NT - 2, NT):
                route_dve(n, n % 2)

            def lo_parts(f):
                for half in range(2):
                    dve.wait_ge(sm["w_hi"], 2 * f + 1 + half)
                    cols = slice(half * WALL // 2, (half + 1) * WALL // 2)
                    three, two = bass.ds(f % 3, 1), bass.ds(f % 2, 1)
                    ins = dve.tensor_tensor(wl[:, three, cols].rearrange("p a n -> p (a n)"),
                                            wraw[:, two, cols].rearrange("p a n -> p (a n)"),
                                            wh[:, three, cols].rearrange("p a n -> p (a n)").bitcast(F32), ALU.subtract)
                ins.then_inc(sm["w_split"], 1)

            def unit_tables():
                r(dve.tensor_tensor(ule[:], uend[0:1, :].unsqueeze(1).broadcast_to([1, NU, E]),
                                    uiota[:].unsqueeze(2).broadcast_to([1, NU, E]), ALU.is_le))
                r(dve.memset(ueid[:, 0:1], 0.0))
                r(dve.tensor_reduce(ueid[:, 1:NU + 1], ule[:], AX, ALU.add))
                r(dve.tensor_scalar(ueid[:, 1:NU + 1], ueid[:, 1:NU + 1], float(E - 1), None, ALU.min))
                r(dve.tensor_copy(uexp[:, 0:NU], ueid[:, 1:NU + 1]))
                gt = ule[:, 0:NU, 0]
                r(dve.tensor_tensor(gt, ueid[:, 1:NU + 1], ueid[:, 0:NU], ALU.is_gt))
                r(dve.scalar_tensor_tensor(gt, ueid[:, 1:NU + 1], E - 1.5, gt, ALU.is_lt, ALU.mult))
                r(dve.scalar_tensor_tensor(unext[:], ueid[:, 1:NU + 1], 1.0, gt, ALU.add, ALU.mult))
                r(dve.tensor_scalar(gt, ueid[:, 1:NU + 1], 3.0, None, ALU.is_ge))
                for m in range(6, E, 3):
                    r(dve.scalar_tensor_tensor(gt, ueid[:, 1:NU + 1], float(m), gt, ALU.is_ge, ALU.add))
                r(dve.scalar_tensor_tensor(upar[:], gt, -3.0, ueid[:, 1:NU + 1], ALU.mult, ALU.add))
                dve.sem_inc(sm["utab"], 1)

            def shared_dve(n, j, between=None):
                if below(n, NT - 1):
                    lo("a_", n + 1, 1 - j)
                if holds(n, 2) and below(n, NT + 2):
                    shared_out(n - 2, j)
                if holds(n, 1) and below(n, NT + 1):
                    z_lo("a_", n - 1, 1 - j)
                if between:
                    choose(*between, take=False)
                if below(n, NT):
                    inner("a_", n, j)
                if between:
                    choose(*between, find=False)

            rc = [0]

            def r(ins, wait=True):
                rc[0] += 1
                ins.then_inc(sm["rstep"], 1)
                if wait:
                    dve.wait_ge(sm["rstep"], rc[0])

            dve.wait_ge(sm["rsig"], 1)
            dve.wait_ge(sm["konst"], KONST2)
            rb = cst[:, C_RB:C_RB + E].unsqueeze(1).broadcast_to([P, NT, E])
            r(dve.tensor_tensor(sc[:, :, 0:E], sc[:, :, 0:E], rb, ALU.add))
            for t in range(NT):
                r(dve.max(v8[:, t, :], sc[:, t, 0:E]), t == NT - 1)
            r(dve.tensor_reduce(wsum[:], v8[:, :, 0:TOPK], AX, ALU.add))
            r(dve.tensor_scalar(wsum[:], wsum[:], 1e-20, None, ALU.add))
            r(dve.reciprocal(wrec[:], wsum[:]))
            r(dve.tensor_scalar(wrec[:], wrec[:], tg[:, 2:3], None, ALU.mult))
            r(dve.memset(v8[:, :, TOPK:8], -BIG))
            for t in range(NT):
                r(dve.match_replace(scr[:, t, :], v8[:, t, :], sc[:, t, :], BIG), t == NT - 1)
            r(dve.tensor_scalar(sel[:], scr[:, :, 0:E], 1e38, None, ALU.is_gt), False)
            dve.wait_ge(sm["rstep"], rc[0])
            dve.sem_inc(sm["sel_ready"], 1)
            r(dve.memset(eq[:], 1.0))
            r(dve.memset(eq[:].rearrange("p t e -> p (t e)")[:, ::NT], 0.0))
            r(dve.memset(pre[:, :, 0], 0.0))
            lo("a_", 0, 0)
            dve.wait_ge(sm["rmm"], 1)
            r(dve.tensor_copy(slot[:].rearrange("p t e -> p (t e)").rearrange("p (e t) -> p e t", t=NT),
                              bank[7][:, NT * E:2 * NT * E].rearrange("p (t e) -> p e t", e=E)))
            r(dve.tensor_tensor_scan(scan[:], eq[:].rearrange("p t e -> p (t e)"), slot[:].rearrange("p t e -> p (t e)"),
                                     0.0, ALU.mult, ALU.add))
            r(dve.tensor_copy(pre[:, :, 1:NT + 1], scan[:].rearrange("p (e t) -> p e t", t=NT)))
            r(dve.tensor_scalar(ucnt[:], pre[:, :, NT], float(P - 1), None, ALU.add))
            r(dve.tensor_scalar(ushf[:], ucnt[:], 7, None, ALU.arith_shift_right))
            r(dve.tensor_scalar(unum[:], ushf[:], 1.0, None, ALU.max))
            r(dve.tensor_tensor_scan(uend[:], ones16[:], unum[:], 0.0, ALU.mult, ALU.add))
            r(dve.tensor_tensor(ubase[:], uend[:], unum[:], ALU.subtract))
            r(dve.tensor_scalar(ubase[:], ubase[:], float(P), 1.0, ALU.mult, ALU.add))
            r(dve.tensor_tensor(slot[:], bank[7][:, 0:NT * E].rearrange("p (t e) -> p t e", e=E),
                                pre[:, :, 0:NT].rearrange("p e t -> p t e"), ALU.add))
            r(dve.tensor_tensor(slot[:], slot[:], ubase[:].unsqueeze(1).broadcast_to([P, NT, E]), ALU.add))
            r(dve.tensor_tensor(slot[:], slot[:], sel[:], ALU.mult))
            for t in range(NT):
                r(dve.max(k8[:, t, :], slot[:, t, :]), t == NT - 1)
            shared_dve(0, 0)
            r(dve.tensor_scalar(sidx[:], k8[:, :, 0:TOPK], -1.0, None, ALU.add))
            for k in range(TOPK):
                r(dve.tensor_tensor(eq[:], slot[:], k8[:, :, k:k + 1].broadcast_to([P, NT, E]), ALU.is_equal))
                r(dve.tensor_tensor(eq[:], eq[:], sc[:, :, 0:E], ALU.mult))
                r(dve.tensor_reduce(wk[:, :, k], eq[:], AX, ALU.add))
            r(dve.tensor_tensor(wk[:], wk[:], wrec[:].unsqueeze(2).broadcast_to([P, NT, TOPK]), ALU.mult))
            r(dve.tensor_scalar(tix[:], sidx[:], P - 1, None, ALU.bitwise_and))
            r(dve.tensor_scalar(tiy[:], sidx[:], 7, None, ALU.arith_shift_right))
            r(dve.scalar_tensor_tensor(tix[:], tix[:], float(NU), tiy[:], ALU.mult, ALU.add))
            r(dve.tensor_copy(tw[:, :, :, 0], tok[:].unsqueeze(2).broadcast_to([P, NT, TOPK])))
            r(dve.tensor_copy(tw[:, :, :, 1].bitcast(F32), wk[:]))
            dve.sem_inc(sm["tables"], 1)
            shared_dve(1, 1)
            unit_tables()
            lo_parts(0)
            with dve.Fori(1, 4) as h:
                for i in range(4):
                    shared_dve(4 * h + i - 2, i % 2, (h + 2, 1, h - 1, i))
            for n in range(NT - 2, NT + 2):
                shared_dve(n, n % 2)
                if n == NT - 2:
                    lo_parts(1)

            def split_lo(n):
                nxt = dve.value_load(unext[0:1, bass.ds(n, 1)], min_val=0, max_val=E - 1)
                with dve.If(nxt > 0):
                    lo_parts(nxt)

            def unit_dve(n, j, g=None, k=0, blk=0, rnd=0):
                if below(n, NU - 1):
                    lo("u_", n + 1, 1 - j)
                if holds(n, 1) and below(n, NU + 1):
                    z_lo("u_", n - 1, 1 - j)
                if holds(n, 1) and below(n, NU):
                    split_lo(n)
                if below(n, NU):
                    inner("u_", n, j)
                if g is not None:
                    choose(g, k, blk, rnd, find=j == 0, take=j == 1)

            lo("u_", 0, 0)
            for i in range(8):
                unit_dve(i, i % 2, 6, 2, 0, i // 2)
            with dve.Fori(1, 6) as h:
                for i in range(8):
                    unit_dve(8 * h + i, i % 2, h + 6, h // 3 + 2, h % 3, i // 2)
            with dve.Fori(6, NU // 8 - 1) as h:
                for i in range(8):
                    unit_dve(8 * h + i, i % 2, h + 6, h - 6, 3, i // 2)
            for n in range(NU - 8, NU + 1):
                unit_dve(n, n % 2, NU // 8 + 5 if n < NU else None, 3, 3, n % 8 // 2)

            def stats3(q):
                dve.wait_ge(sm["xload"], 16 * q + 16)
                for i in range(4):
                    ln_stats(4 * q + i)
                ln_scale(4 * q, 4, 2 * NT + 4 * q + 4, 6 + q)
                at = bass.ds(4 * q, 4)
                dve.scalar_tensor_tensor(nb[:, at], mu[:, at], -1.0, rs[:, at], ALU.mult, ALU.mult).then_inc(sm["nb_ready"], 1)

            def features_rest(t, j):
                dve.wait_ge(sm["d3"], t + 1)
                dve.tensor_reduce(maps[:, 0, :, 1, bass.ds(2 * t, 2)], sf[j][:].rearrange("p k (b c) -> p k b c", c=S),
                                  AX, ALU.max).then_inc(sm["m3"], 1)

            def features(t, j):
                dve.wait_ge(sm["x3_done"], t + 1)
                m = ctxT[:, :, bass.ds(t * P, P)]
                dve.scalar_tensor_tensor(cf[j][:], m, 0.5, x3T[:, :, bass.ds(t * P, P)], ALU.is_lt, ALU.mult)\
                    .then_inc(sm["c3"], 1)
                if holds(t, 1):
                    features_rest(t - 1, 1 - j)
                dve.wait_ge(sm["c3"], t + 1)
                cv = cf[j][:].rearrange("p k (b c) -> p k b c", c=S)
                dve.tensor_reduce(maps[:, 0, :, 0, bass.ds(2 * t, 2)], cv, AX, ALU.max).then_inc(sm["r3"], 1)
                dve.tensor_reduce(maps[:, 1, :, 0, bass.ds(2 * t, 2)], cv, AX, ALU.add).then_inc(sm["r3"], 1)

            def features4(q):
                for i in range(4):
                    features(4 * q + i, i % 2)
                    if i == 0 and below(q, 3):
                        stats3(q + 1)

            stats3(0)
            features4(0)
            with dve.Fori(1, 3) as q:
                features4(q)
            features4(3)
            features_rest(NT - 1, 1)
            dve.wait_ge(sm["m3"], NT)
            dve.wait_ge(sm["r3"], 2 * NT)
            dve.wait_ge(sm["tot_sb"], NT)
            c(dve.tensor_tensor(maps[:, 1, :, 1, :], tot[:], maps[:, 1, :, 0, :], ALU.subtract))
            c(dve.tensor_scalar(maps[:, 1, :, 0, :], maps[:, 1, :, 0, :], 1.0 / NSEL, None, ALU.mult))
            c(dve.tensor_scalar(maps[:, 1, :, 1, :], maps[:, 1, :, 1, :], 1.0 / NSUB, None, ALU.mult))

            bc = [0]

            def b_(ins):
                bc[0] += 1
                ins.then_inc(sm["bn_step"], 1)
                dve.wait_ge(sm["bn_step"], bc[0])

            dve.wait_ge(sm["bn_mm"], 1)
            b_(dve.tensor_copy(zc[:], bank[4][:, 0:2 * KD * B].rearrange("p (k r b) -> p r k b", k=KD, r=2)))
            b_(dve.tensor_reduce(part[:], zc[:].rearrange("p r k b -> p r (k b)"), AX, ALU.add))
            dve.wait_ge(sm["bn_mm"], 2)
            b_(dve.tensor_scalar(mean[:], bank[5][:, 0:2], 1.0 / (B * D), None, ALU.mult))
            for rr in range(2):
                b_(dve.tensor_scalar(zc[:, rr], zc[:, rr], mean[:, rr:rr + 1], None, ALU.subtract))
            b_(dve.tensor_tensor(zq[:], zc[:], zc[:], ALU.mult))
            b_(dve.tensor_reduce(part[:], zq[:].rearrange("p r k b -> p r (k b)"), AX, ALU.add))
            dve.wait_ge(sm["bn_mm"], 3)
            b_(dve.tensor_scalar(var[:], bank[5][:, 0:2], 1.0 / (B * D), None, ALU.mult))
            dve.wait_ge(sm["bn_act"], 1)
            b_(dve.reciprocal(gain[:], gain[:]))
            b_(dve.tensor_scalar(gain[:], gain[:], cst[:, C_BN:C_BN + 1], None, ALU.mult))
            for rr in range(2):
                b_(dve.tensor_scalar(zc[:, rr], zc[:, rr], gain[:, rr:rr + 1], cst[:, C_BN + 1:C_BN + 2], ALU.mult, ALU.add))
            b_(dve.tensor_scalar(zc[:], zc[:], 0.0, None, ALU.max))
            dve.wait_ge(sm["bn_act"], 2)
            b_(dve.tensor_tensor(amap[:, 1], amap[:, 1], amap[:, 0], ALU.subtract))

            def gated(t, j):
                if j == 0:
                    dve.wait_ge(sm["y3p"], t + 2)
                else:
                    dve.wait_ge(sm["y3a"], t // 2 + 1)
                if holds(t, 2):
                    dve.wait_ge(sm["y3t"], t - 1)
                dve.tensor_tensor(cf[j][:], asel[j][:], x3T[:, :, bass.ds(t * P, P)], ALU.mult).then_inc(sm["y3"], 1)

            def residual3(t, j):
                dve.wait_ge(sm["y3t"], t + 1)
                xt = X[:, bass.ds(t, 1), :].rearrange("p a d -> p (a d)")
                dve.scalar_tensor_tensor(xt, bank[2 + j][:], tg[:, 1:2], xt, ALU.mult, ALU.add).then_inc(sm["x3_sum"], 1)
                dve.wait_ge(sm["x3_sum"], t + 1)
                ln_stats(t)

            def gated_step(t, j):
                if below(t, NT):
                    gated(t, j)
                if holds(t, 1):
                    residual3(t - 1, 1 - j)

            for t in range(2):
                gated_step(t, t)
            with dve.Fori(1, (NT - 2) // 2) as h:
                for j in range(2):
                    gated_step(2 * h + j, j)
            for t in range(NT - 2, NT + 1):
                gated_step(t, t % 2)

            ln_scale(0, NT, 4 * NT, 10)

            def x4n(t, j):
                if holds(t, 2):
                    dve.wait_ge(sm["f_tx"], t - 1)
                ln_apply(t, j, "l4")

            def f_lo(n, j):
                dve.wait_ge(sm["f_hi"], n + 1)
                dve.tensor_tensor(fl[j][:].rearrange("p k n -> p (k n)"), bank[j][:],
                                  fh[j][:].rearrange("p k n -> p (k n)").bitcast(F32), ALU.subtract)\
                    .then_inc(sm["f_lo"], 1)

            def f_route(n, j):
                dve.wait_ge(sm["f_h"], n + 1)
                carry(dve)
                hb = bank[4 + j]
                step = [0]

                def q(ins):
                    step[0] += 1
                    ins.then_inc(sm["f_step"], 1)
                    dve.wait_ge(sm["f_step"], NF * n + step[0])
                    if step[0] in (4, 8):
                        carry(dve)

                q(dve.max(m8[j][:], hb[:, P:P + LE]))
                q(dve.tensor_scalar(nm[j][:, 0:1], m8[j][:, 0:1], -1.0, None, ALU.mult))
                dve.wait_ge(sm["f_exp"], n + 1)
                q(dve.reciprocal(nm[j][:, 2:3], nm[j][:, 1:2]))
                q(dve.tensor_scalar(pr[j][:, 0:LE], pr[j][:, 0:LE], nm[j][:, 2:3], None, ALU.mult))
                q(dve.max(m8[j][:], pr[j][:, 0:LE]))
                q(dve.tensor_tensor(nm[j][:, 3:4], m8[j][:, 0:1], m8[j][:, 1:2], ALU.add))
                q(dve.memset(m8[j][:, 2:8], -1.0))
                q(dve.reciprocal(nm[j][:, 4:5], nm[j][:, 3:4]))
                q(dve.match_replace(prr[j][:], m8[j][:], pr[j][:], BIG))
                q(dve.scalar_tensor_tensor(lw[j][:], prr[j][:, 0:LE], 1e38, pr[j][:, 0:LE], ALU.is_gt, ALU.mult))
                q(dve.tensor_scalar(lw[j][:], lw[j][:], nm[j][:, 4:5], 2.0, ALU.mult, ALU.mult))
                assert step[0] == NF
                if holds(n, 2):
                    dve.wait_ge(sm["f_ht"], n - 1)
                dve.tensor_tensor(hw[j][:].rearrange("p (e r) -> p e r", e=LE), hb[:, 0:P].rearrange("p (e r) -> p e r", e=LE),
                                  lw[j][:].unsqueeze(2).broadcast_to([P, LE, LR]), ALU.mult).then_inc(sm["f_hw"], 1)

            def f_htl(n, j):
                dve.wait_ge(sm["f_hth"], n + 1)
                dve.tensor_tensor(htl[j][:], bank[6][:, 0:P], hth[j][:].bitcast(F32), ALU.subtract).then_inc(sm["f_htl"], 1)

            def f_final(n, j):
                dve.wait_ge(sm["f_fin"], n + 1)
                dve.wait_ge(sm["cpre"], n + 1)
                if holds(n, 2):
                    dve.wait_ge(sm[f"out_d{j}"], 16 * (n // 2))
                dve.scalar_tensor_tensor(fo[j][:], bank[2 + j][:], tg[:, 3:4],
                                         X[:, bass.ds(n, 1), :].rearrange("p a d -> p (a d)"), ALU.mult, ALU.add)\
                    .then_inc(sm["f_out"], 1)

            def lora_dve(n, j):
                if below(n, NT - 2):
                    x4n(n + 2, j)
                if below(n, NT - 1):
                    f_lo(n + 1, 1 - j)
                if holds(n, 2):
                    f_final(n - 2, j)
                if holds(n, 1) and below(n, NT + 1):
                    f_htl(n - 1, 1 - j)
                if below(n, NT):
                    f_route(n, j)

            x4n(0, 0)
            x4n(1, 1)
            f_lo(0, 0)
            for n in range(2):
                lora_dve(n, n)
            with dve.Fori(1, (NT - 2) // 2) as h:
                for j in range(2):
                    lora_dve(2 * h + j, j)
            for n in range(NT - 2, NT + 2):
                lora_dve(n, n % 2)

        @block.tensor
        def _(pe):
            pe.wait_ge(sm["konst"], KONST1)

            def turn(dst, src, wait_sem, count):
                for k in range(KD):
                    ins = pe.transpose(dst[:, k * P:(k + 1) * P], src[:, k * P:(k + 1) * P], ident[:])
                ins.then_inc(sm[wait_sem], 1)

            def proj(s, r):
                if r >= 2 or holds(s, 1):
                    pe.wait_ge(sm["proj_out"], 6 * s + r - 1)
                for k in range(KD):
                    w = wkv[:, k, r, :] if r < 2 else wq[:, k, r - 2, :]
                    x = ctxT[:, k, bass.ds(s * 512, 512)] if r < 2 else xnT[:, k, :]
                    ins = pe.matmul(bank[r % 2][:], w, x, start=(k == 0), stop=(k == KD - 1))
                ins.then_inc(sm["proj_done"], 1)

            def stage1a(s):
                pe.wait_ge(sm["ctx_in"], 16 * s + 16)
                for r in range(2):
                    proj(s, r)
                for i in range(4):
                    t = 4 * s + i
                    pe.wait_ge(sm["xn_ready"], t + 1)
                    if holds(t, 2):
                        pe.wait_ge(sm["xnT_ready"], t - 1)
                    turn(bank[2 + i % 2], xn[i % 2], "tx_done", t)
                pe.wait_ge(sm["xnT_ready"], 4 * s + 4)
                if not holds(s, 1):
                    pe.wait_ge(sm["watt_in"], 16)
                for r in range(2, 6):
                    proj(s, r)

            pe.wait_ge(sm["wkv_in"], 16)
            stage1a(0)
            with pe.Fori(1, 4) as s:
                stage1a(s)

            pe.wait_ge(sm["proj_out"], 24)
            pe.wait_ge(sm["watt_in"], 48)

            def scores(u, i):
                j = i % 2
                pe.wait_ge(sm["b_ready"], 3 * (u // 2) + 3)
                if holds(u, 2):
                    pe.wait_ge(sm["dif_ready"], u - 1)
                g, jb = 2 * (i % 2), i // 2 % 2
                pe.matmul(bank[j][:], qTb[jb][:, g:g + 2, :].rearrange("p g q -> p (g q)"),
                          kblk[jb][:].rearrange("p h k -> p (h k)"), start=True, stop=True).then_inc(sm["s_ready"], 1)

            def prob_turn(u, j):
                pe.wait_ge(sm["exp_done"], u + 1)
                if holds(u, 2):
                    pe.wait_ge(sm["ptc_done"], u - 1)
                turn(bank[2 + j], prob[j], "pt_done", u)

            def values(b, j):
                if holds(b, 1):
                    pe.wait_ge(sm["v_ready"], 2 * b)
                pe.wait_ge(sm["b_ready"], 3 * b + 3)
                pe.transpose(bank[5][:, 0:P], vTb[j][:].rearrange("p a k -> p (a k)"), ident[:]).then_inc(sm["v_done"], 1)

            def weigh(u, i):
                j = i % 2
                pe.wait_ge(sm["ptc_done"], u + 1)
                pe.wait_ge(sm["v_ready"], 2 * (u // 2) + 2)
                if holds(u, 1):
                    pe.wait_ge(sm["yn_ready"], u)
                for a in range(4):
                    ins = pe.matmul(bank[6][:, 34 * a:34 * a + 34], probT[j][:, a, :],
                                    vblk[i // 2 % 2][:, a, :], start=True, stop=True)
                ins.then_inc(sm["pv_done"], 1)

            def y_turn(u, j):
                pe.wait_ge(sm["yn_ready"], u + 1)
                if holds(u, 1):
                    pe.wait_ge(sm["ytc_done"], u)
                pe.transpose(bank[7][:, 0:P], yn[j][:].rearrange("p a h d -> p (a h d)"), ident[:])\
                    .then_inc(sm["yt_done"], 1)

            def project(t):
                pe.wait_ge(sm["ytc_done"], 4 * t + 4)
                if holds(t, 1):
                    pe.wait_ge(sm["x1_done"], t)
                for g in range(NG):
                    ins = pe.matmul(bank[4][:], yT[:, g, :], wo[:, g, :], start=(g == 0), stop=(g == NG - 1))
                ins.then_inc(sm["wo_done"], 1)

            def att_pe(u, i, t):
                if below(u, 2 * B):
                    prob_turn(u, i % 2)
                if i % 2 == 1 and below(u, 2 * B - 1):
                    values((u + 1) // 2, (i + 1) // 2 % 2)
                if holds(u, 1) and below(u, 2 * B + 1):
                    weigh(u - 1, (i - 1) % 4)
                if holds(u, 2) and below(u, 2 * B + 2):
                    y_turn(u - 2, i % 2)
                if below(u, 2 * B - 2):
                    scores(u + 2, (i + 2) % 4)
                if i == 2 and holds(u, 4):
                    project(t - 1)

            scores(0, 0)
            scores(1, 1)
            values(0, 0)
            for i in range(4):
                att_pe(i, i, 0)
            with pe.Fori(0, (NT - 2) // 2) as h:
                for t in (2 * h + 1, 2 * h + 2):
                    for i in range(4):
                        att_pe(4 * t + i, i, t)
            for u in range(2 * B - 4, 2 * B + 2):
                att_pe(u, u % 4, u // 4)
            project(NT - 1)

            def parts(hi_, lo_):
                return (lambda k: hi_[:, k, :]), (lambda k: lo_[:, k, :])

            def gate_up(p, n, j, at):
                pe.wait_ge(sm[p + "lo"], n + 1)
                if holds(n, 2):
                    pe.wait_ge(sm[p + "z"], n - 1)
                w = [(lambda k, m=m: m[:, at, k * D:(k + 1) * D]) for m in (wh, wl)]
                split3(pe, bank[2 + j][:], parts(xh[j], xl[j]), w, range(KD), True, True).then_inc(sm[p + "gu"], 1)

            def z_turn(p, n, j):
                pe.wait_ge(sm[p + "z"], n + 1)
                if holds(n, 1):
                    pe.wait_ge(sm[p + "zl"], n)
                for k in range(2):
                    ins = pe.transpose(bank[4][:, k * P:(k + 1) * P], zz[j][:, k * P:(k + 1) * P], ident[:])
                ins.then_inc(sm[p + "zt"], 1)

            def down(p, n, j, at, freed):
                pe.wait_ge(sm[p + "zl"], n + 1)
                if holds(n, 2):
                    pe.wait_ge(sm[freed], n - 1)
                w = [(lambda k, m=m: m[:, at, WGU + k * D:WGU + (k + 1) * D]) for m in (wh, wl)]
                split3(pe, bank[5 + j][:], parts(zh[j], zl[j]), w, (0, 1), True, True).then_inc(sm[p + "y"], 1)

            def logits(n, j):
                if holds(n, 2):
                    pe.wait_ge(sm["a_rtc"], n - 1)
                pe.wait_ge(sm["r_lo"], n + 1)
                split3(pe, bank[4 + j][0:E, 0:P], parts(gwh, gwl), parts(xh[j], xl[j]), range(KD), True, True)\
                    .then_inc(sm["a_rt"], 1)

            def logits_turn(n, j):
                pe.wait_ge(sm["a_rtc"], n + 1)
                pe.matmul(bank[7][:, bass.ds(n * E, E)], lgT[j][:], ident[0:E, 0:E], start=True, stop=True).then_inc(sm["lg_t"], 1)

            def r_turn(n, j):
                pe.wait_ge(sm["n2"], n + 1)
                if holds(n, 2):
                    pe.wait_ge(sm["r_lo"], n - 1)
                turn(bank[j], xn[j], "r_tx", n)

            def route_pe(n, j):
                if below(n, NT - 1):
                    r_turn(n + 1, 1 - j)
                if below(n, NT):
                    logits(n, j)
                if holds(n, 1):
                    logits_turn(n - 1, 1 - j)

            r_turn(0, 0)
            pe.wait_ge(sm["sum_step"], 3)
            for n in range(2):
                route_pe(n, n)
            with pe.Fori(0, (NT - 4) // 4) as h:
                for i in range(4):
                    route_pe(4 * h + 2 + i, i % 2)
            for n in range(NT - 2, NT + 1):
                route_pe(n, n % 2)

            def x_turn(n, j):
                pe.wait_ge(sm[f"load_in{j}"], 16 * (n // 2) + 16)
                if holds(n, 2):
                    pe.wait_ge(sm["a_lo"], n - 1)
                turn(bank[j], xn[j], "a_tx", n)

            x_turn(0, 0)

            pe.wait_ge(sm["sel_ready"], 1)
            pe.matmul(bank[7][:, 0:NT * E], lower[:], sel[:].rearrange("p t e -> p (t e)"), start=True, stop=True)
            pe.matmul(bank[7][:, NT * E:2 * NT * E], onesm[:], sel[:].rearrange("p t e -> p (t e)"), start=True, stop=True)\
                .then_inc(sm["rmm"], 1)

            def shared_pe(n, j):
                if below(n, NT - 1):
                    x_turn(n + 1, 1 - j)
                if holds(n, 1) and below(n, NT + 1):
                    z_turn("a_", n - 1, 1 - j)
                if below(n, NT):
                    gate_up("a_", n, j, 2)
                if holds(n, 1) and below(n, NT + 1):
                    down("a_", n - 1, 1 - j, 2, "a_x")

            pe.wait_ge(sm["s_split"], 1)
            for n in range(2):
                shared_pe(n, n)
            with pe.Fori(0, (NT - 4) // 4) as h:
                for i in range(4):
                    shared_pe(4 * h + 2 + i, i % 2)
            for n in range(NT - 2, NT + 1):
                shared_pe(n, n % 2)

            def g_turn(n, j):
                pe.wait_ge(sm[f"g_in{j}"], 16 * (n // 2) + 16)
                if holds(n, 2):
                    pe.wait_ge(sm["u_lo"], n - 1)
                turn(bank[j], xn[j], "u_tx", n)

            def unit_of(n):
                if not below(n, NU):
                    return None, None
                e = pe.value_load(uexp[0:1, bass.ds(n, 1)], min_val=0, max_val=E - 1)
                return e, e % 3

            def units_pe(at, count):
                for i in range(count):
                    n, j = at + i, i % 2
                    if below(n, NU - 1):
                        g_turn(n + 1, 1 - j)
                    if i == 0:
                        before = unit_of(n - 1) if holds(n, 1) else None
                        now = unit_of(n)
                    if holds(n, 1) and below(n, NU + 1):
                        z_turn("u_", n - 1, 1 - j)
                    if below(n, NU):
                        pe.wait_ge(sm["w_split"], now[0] + 1)
                        gate_up("u_", n, j, now[1])
                    after = unit_of(n + 1) if i < count - 1 else None
                    if holds(n, 1) and below(n, NU + 1):
                        down("u_", n - 1, 1 - j, before[1], "u_yo")
                    before, now = now, after

            pe.wait_ge(sm["utab"], 1)
            g_turn(0, 0)
            units_pe(0, 8)
            with pe.Fori(1, NU // 8 - 1) as h:
                units_pe(8 * h, 8)
            units_pe(NU - 8, 9)

            def x3_turn(t, j):
                pe.wait_ge(sm["l3"], t + 1)
                if holds(t, 2):
                    pe.wait_ge(sm["x3_done"], t - 1)
                if holds(t, 2):
                    pe.wait_ge(sm["tot_sb"], t - 1)
                for k in range(KD):
                    ins = pe.matmul(bank[6 + j][:, 2 * k:2 * k + 2], xn[j][:, k * P:(k + 1) * P], bsel[:], start=True, stop=True)
                ins.then_inc(sm["tot_ps"], 1)
                turn(bank[j], xn[j], "t_done", t)

            pe.wait_ge(sm["konst3"], 4)
            for t in range(2):
                x3_turn(t, t)
            with pe.Fori(1, NT // 2) as h:
                for j in range(2):
                    x3_turn(2 * h + j, j)
            pe.wait_ge(sm["cstep"], 17)
            for ko in range(KD):
                terms = [(ch, ki) for ki in range(max(0, ko - 1), min(KD, ko + 2)) for ch in range(2)]
                for n, (ch, ki) in enumerate(terms):
                    off = P + P * (ko - ki)
                    ins = pe.matmul(bank[4][:, ko * 64:(ko + 1) * 64], band[:, ch, off:off + P],
                                    maps[:, ch, ki].rearrange("p r b -> p (r b)"),
                                    start=(n == 0), stop=(n == len(terms) - 1))
            ins.then_inc(sm["bn_mm"], 1)
            for step in (2, 7):
                pe.wait_ge(sm["bn_step"], step)
                pe.matmul(bank[5][:, 0:2], ones3[:], part[:], start=True, stop=True).then_inc(sm["bn_mm"], 1)

            def y3_turn(t, j):
                pe.wait_ge(sm["y3"], t + 1)
                if holds(t, 2):
                    pe.wait_ge(sm["x3_sum"], t - 1)
                turn(bank[2 + j], cf[j][:].rearrange("p k n -> p (k n)"), "y3t", t)

            for t in range(2):
                y3_turn(t, t)
            with pe.Fori(1, NT // 2) as h:
                for j in range(2):
                    y3_turn(2 * h + j, j)

            pe.wait_ge(sm["w4_split"], 3)

            def f_turn(n, j):
                pe.wait_ge(sm["l4"], n + 1)
                if holds(n, 2):
                    pe.wait_ge(sm["f_lo"], n - 1)
                turn(bank[j], xn[j], "f_tx", n)

            def f_low(n, j):
                pe.wait_ge(sm["f_lo"], n + 1)
                if holds(n, 2):
                    pe.wait_ge(sm["f_hw"], n - 1)
                split3(pe, bank[4 + j][:, 0:136], parts(fh[j], fl[j]), parts(*aws), range(KD), True, True)\
                    .then_inc(sm["f_h"], 1)

            def f_hw_turn(n, j):
                pe.wait_ge(sm["f_hw"], n + 1)
                if holds(n, 1):
                    pe.wait_ge(sm["f_htl"], n)
                pe.transpose(bank[6][:, 0:P], hw[j][:], ident[:]).then_inc(sm["f_ht"], 1)

            def f_base(n, j):
                if holds(n, 2):
                    pe.wait_ge(sm["f_out"], n - 1)
                split3(pe, bank[2 + j][:], parts(fh[j], fl[j]), parts(*wbs), range(KD), True, False)\
                    .then_inc(sm["f_base"], 1)

            def f_up(n, j):
                pe.wait_ge(sm["f_htl"], n + 1)
                split3(pe, bank[2 + j][:], (lambda k: hth[j][:], lambda k: htl[j][:]),
                       (lambda k: bms[0][:], lambda k: bms[1][:]), (0,), False, True).then_inc(sm["f_fin"], 1)

            def lora_pe(n, j):
                if below(n, NT - 1):
                    f_turn(n + 1, 1 - j)
                if below(n, NT):
                    f_low(n, j)
                if holds(n, 1) and below(n, NT + 1):
                    f_hw_turn(n - 1, 1 - j)
                if below(n, NT):
                    f_base(n, j)
                if holds(n, 1) and below(n, NT + 1):
                    f_up(n - 1, 1 - j)

            f_turn(0, 0)
            for n in range(2):
                lora_pe(n, n)
            with pe.Fori(0, (NT - 4) // 4) as h:
                for i in range(4):
                    lora_pe(4 * h + 2 + i, i % 2)
            for n in range(NT - 2, NT + 1):
                lora_pe(n, n % 2)



def kernel(**inputs):
    import numpy as np
    import concourse.bacc as bacc
    from concourse.bass_utils import run_bass_kernel_spmd

    a = {k: np.asarray(v) for k, v in inputs.items()}
    rows = [a["g_xattn"], a["g_ffn"], a["L0_ffn_bias"], a["L1_xattn_conv_w"].reshape(14),
            a["L1_xattn_bn_gamma"], a["L1_xattn_bn_beta"]]
    head = a["L0_xattn_bq"].reshape(NKV, NG, HD).transpose(0, 2, 1).reshape(P, NG)
    cols = [head, a["L0_xattn_bk"][:, None], a["L0_xattn_bv"][:, None]]
    cst = np.concatenate([np.broadcast_to(np.concatenate(rows), (P, C_BQ))] + cols, axis=1)

    def pieces(w):
        e, k, n = w.shape
        return w.reshape(e, k // P, P, n).transpose(0, 2, 1, 3).reshape(e, P, -1)

    wg = np.concatenate([a["L0_ffn_Wg"], a["L0_ffn_Sg"][None]]).transpose(0, 2, 1)
    wu = np.concatenate([a["L0_ffn_Wu"], a["L0_ffn_Su"][None]]).transpose(0, 2, 1)
    wd = np.concatenate([a["L0_ffn_Wd"], a["L0_ffn_Sd"][None]]).transpose(0, 2, 1)
    arrays = {
        "x": a["x"].reshape(T, D),
        "ctxT": a["ctx_4096"].reshape(T, D).T,
        "cst": cst,
        "wq": a["L0_xattn_Wq"].reshape(D, NKV, NG, HD).transpose(0, 2, 1, 3).reshape(D, D),
        "wkv": np.concatenate([a["L0_xattn_Wk"], a["L0_xattn_Wv"]], axis=1),
        "wo": a["L0_xattn_Wo"].reshape(NKV, NG, HD, D).transpose(1, 0, 2, 3).reshape(NG, P, D),
        "bo": np.broadcast_to(a["L0_xattn_bo"], (P, D)),
        "gate": a["L0_ffn_gate_w"].T,
        "wall": np.concatenate([pieces(np.concatenate([wg, wu], axis=2)), pieces(wd)], axis=2),
        "wb": a["L1_ffn_Wb"].T,
        "aw": np.concatenate([a["L1_ffn_A"].reshape(LE * LR, D), a["L1_ffn_Wr"]]).T,
        "bm": a["L1_ffn_Bm"].transpose(0, 2, 1).reshape(LE * LR, D),
        "b1": np.broadcast_to(a["L1_ffn_bias"], (P, D)),
    }
    nc = bacc.Bacc("TRN2", target_bir_lowering=False, num_devices=1)
    arrays = {f"in_{k}": np.ascontiguousarray(v) for k, v in arrays.items()}
    io = [nc.dram_tensor(k, v.shape, mybir.dt.from_np(v.dtype), kind="ExternalInput").ap() for k, v in arrays.items()]
    io.append(nc.dram_tensor("out_0", (T, D), F32, kind="ExternalOutput").ap())
    block_program(nc, io)
    r = run_bass_kernel_spmd(nc, [arrays], core_ids=[0])
    return r.results[0]["out_0"].reshape(B, S, D)
```
